# Optimizing a Trainium2 kernel written in Bass

```python
import numpy as np
import jax
import jax.numpy as jnp

def _softmax(x, axis=-1):
    return jax.nn.softmax(x, axis=axis)

def _gelu(x):
    return jax.nn.gelu(x, approximate=True)

def _silu(x):
    return jax.nn.silu(x)

def _sigmoid(x):
    return jax.nn.sigmoid(x)

def _layernorm(x, axis=-1, eps=1e-05):
    m = jnp.mean(x, axis=axis, keepdims=True)
    v = jnp.var(x, axis=axis, keepdims=True)
    return (x - m) / jnp.sqrt(v + eps)

def _scatter_add(tgt, idx, src, axis=0):
    return tgt.at[idx].add(src)

def _segment_sum(src, seg, n):
    return jax.ops.segment_sum(src, seg, n)
kernel_name = 'mk_gnn_resnorm_d4_gnn_r32_621547'

def setup_inputs(seed: int=0):
    np.random.seed(seed)
    _w = jnp.asarray

    def _rec_inputs():
        import jax
        import jax.numpy as jnp
        _gk = jax.random.key(seed)
        x = -0.0003713 + 1 * jax.random.normal(jax.random.fold_in(_gk, 1), (3125, 128), jnp.float32)
        src = jax.random.randint(jax.random.fold_in(_gk, 2), (100000,), 0, 3125, jnp.int32)
        dst = jnp.minimum((3125 * jax.random.uniform(jax.random.fold_in(_gk, 3), (100000,)) ** 2.0).astype(jnp.int32), 99999)
        _o = jnp.argsort(dst, stable=True)
        src = src[_o]
        dst = dst[_o]
        edge_type_4 = jax.random.randint(jax.random.fold_in(_gk, 13), (100000,), 0, 4, jnp.int32)
        edge_weight = jax.random.uniform(jax.random.fold_in(_gk, 14), (100000,), jnp.float32, 0.0, 1)
        return (x, src, dst, edge_type_4, edge_weight)
    x, src, dst, edge_type_4, edge_weight = _rec_inputs()

    def _L0_gnn_setup():
        import jax, jax.numpy as jnp
        import numpy as np
        N = 3125
        D = 128
        E = 50000
        EPS = 1e-05

        def _linear_params(key, d_in, d_out):
            kw, kb = jax.random.split(key)
            s = 1.0 / np.sqrt(d_in)
            W = jax.random.uniform(kw, (d_out, d_in), dtype=jnp.float32, minval=-s, maxval=s)
            b = jax.random.uniform(kb, (d_out,), dtype=jnp.float32, minval=-s, maxval=s)
            return (W, b)

        def _bn(h, g, b):
            m = jnp.mean(h, axis=0)
            v = jnp.var(h, axis=0)
            return (h - m) * jax.lax.rsqrt(v + EPS) * g + b

        def _lin(h, W, b):
            return h @ W.T + b
        key = jax.random.key(seed)
        ks = jax.random.split(key, 16)
        inp = {'x': jax.random.normal(ks[0], (N, D), dtype=jnp.float32), 'edge_row': jax.random.randint(ks[1], (E,), 0, N), 'edge_col': jax.random.randint(ks[2], (E,), 0, N), 'edge_val': jax.random.uniform(ks[3], (E,), dtype=jnp.float32)}
        names = ['W1', 'U1', 'W2', 'U2', 'W3', 'U3']
        for i, n in enumerate(names):
            W, b = _linear_params(ks[4 + i], D, D)
            inp[n + 'w'], inp[n + 'b'] = (W, b)
        inp['bn_g'] = jnp.ones((D,), jnp.float32)
        inp['bn_b'] = jnp.zeros((D,), jnp.float32)
        inp['m_w0'], inp['m_b0'] = _linear_params(ks[10], D, D)
        inp['m_bng'] = jnp.ones((D,), jnp.float32)
        inp['m_bnb'] = jnp.zeros((D,), jnp.float32)
        inp['m_w1'], inp['m_b1'] = _linear_params(ks[11], D, D)
        return inp
    _L0_gnn_all = _L0_gnn_setup()
    _L0_gnn_in = {k: v for k, v in _L0_gnn_all.items() if k in ('W1w', 'W1b', 'U1w', 'U1b', 'W2w', 'W2b', 'U2w', 'U2b', 'W3w', 'W3b', 'U3w', 'U3b', 'bn_g', 'bn_b', 'm_w0', 'm_b0', 'm_bng', 'm_bnb', 'm_w1', 'm_b1')}
    del _L0_gnn_all

    def _L1_gnn_setup():
        import jax, jax.numpy as jnp
        import numpy as np
        N_NODES = 50000
        N_EDGES = 25000
        IN_DIM = 128
        OUT_DIM = 32
        N_HEADS = 4
        N_REL = 4
        NEG_SLOPE = 0.2
        LN_EPS = 1e-05
        key = jax.random.key(seed)
        ks = jax.random.split(key, 8)
        x = jax.random.normal(ks[0], (N_NODES, IN_DIM), dtype=jnp.float32)
        edge_index = jax.random.randint(ks[1], (2, N_EDGES), 0, N_NODES)
        edge_type = jax.random.randint(ks[2], (N_EDGES,), 0, N_REL)
        W = jax.random.normal(ks[3], (N_REL, IN_DIM, N_HEADS * OUT_DIM), dtype=jnp.float32) * 0.1
        attn_src = jax.random.normal(ks[4], (N_REL, N_HEADS, OUT_DIM), dtype=jnp.float32) * 0.1
        attn_dst = jax.random.normal(ks[5], (N_REL, N_HEADS, OUT_DIM), dtype=jnp.float32) * 0.1
        bias = jnp.zeros((N_HEADS * OUT_DIM,), dtype=jnp.float32)
        ln_gamma = jnp.ones((N_HEADS * OUT_DIM,), dtype=jnp.float32)
        ln_beta = jnp.zeros((N_HEADS * OUT_DIM,), dtype=jnp.float32)
        return {'x': x, 'edge_index': edge_index, 'edge_type': edge_type, 'W': W, 'attn_src': attn_src, 'attn_dst': attn_dst, 'bias': bias, 'ln_gamma': ln_gamma, 'ln_beta': ln_beta}
    _L1_gnn_all = _L1_gnn_setup()
    _L1_gnn_in = {k: v for k, v in _L1_gnn_all.items() if k in ('W', 'attn_src', 'attn_dst', 'bias', 'ln_gamma', 'ln_beta')}
    del _L1_gnn_all

    def _L2_gnn_setup():
        import jax, jax.numpy as jnp
        import numpy as np
        N, D, H, F = (50000, 128, 8, 512)
        HD = D // H
        EPS_BN = 1e-05

        def _batchnorm(x, gamma, beta):
            m = x.mean(axis=0)
            v = x.var(axis=0)
            return (x - m) * jax.lax.rsqrt(v + EPS_BN) * gamma + beta
        key = jax.random.key(seed)
        ks = jax.random.split(key, 12)
        s = 0.05
        return {'src': jax.random.normal(ks[0], (N, D), jnp.float32), 'edge_index': jax.random.randint(ks[1], (2, 25000), 0, N, jnp.int64), 'q_w': jax.random.normal(ks[2], (D, D), jnp.float32) * s, 'q_b': jnp.zeros((D,), jnp.float32), 'k_w': jax.random.normal(ks[3], (D, D), jnp.float32) * s, 'v_w': jax.random.normal(ks[4], (D, D), jnp.float32) * s, 'out_w': jax.random.normal(ks[5], (D, D), jnp.float32) * s, 'out_b': jnp.zeros((D,), jnp.float32), 'g1': jnp.ones((D,), jnp.float32), 'b1': jnp.zeros((D,), jnp.float32), 'lin1_w': jax.random.normal(ks[6], (F, D), jnp.float32) * s, 'lin1_b': jnp.zeros((F,), jnp.float32), 'lin2_w': jax.random.normal(ks[7], (D, F), jnp.float32) * s, 'lin2_b': jnp.zeros((D,), jnp.float32), 'g2': jnp.ones((D,), jnp.float32), 'b2': jnp.zeros((D,), jnp.float32)}
    _L2_gnn_all = _L2_gnn_setup()
    _L2_gnn_in = {k: v for k, v in _L2_gnn_all.items() if k in ('q_w', 'q_b', 'k_w', 'v_w', 'out_w', 'out_b', 'g1', 'b1', 'lin1_w', 'lin1_b', 'lin2_w', 'lin2_b', 'g2', 'b2')}
    del _L2_gnn_all

    def _L3_gnn_setup():
        import jax, jax.numpy as jnp
        import numpy as np
        N_NODES = 50000
        N_EDGES = 25000
        HID = 128
        key = jax.random.key(seed)
        ks = jax.random.split(key, 10)
        s_msg = 1.0 / np.sqrt(2 * HID + 1)
        s_u1 = 1.0 / np.sqrt(2 * HID)
        s_u2 = 1.0 / np.sqrt(HID)
        return {'z': jax.random.normal(ks[0], (N_NODES, HID), dtype=jnp.float32), 'edge_weight': jax.random.uniform(ks[1], (N_EDGES,), dtype=jnp.float32), 'edge_src': jax.random.randint(ks[2], (N_EDGES,), 0, N_NODES), 'edge_dst': jax.random.randint(ks[3], (N_EDGES,), 0, N_NODES), 'Wm': jax.random.normal(ks[4], (2 * HID + 1, HID), dtype=jnp.float32) * s_msg, 'bm': jax.random.normal(ks[5], (HID,), dtype=jnp.float32) * s_msg, 'W1': jax.random.normal(ks[6], (2 * HID, HID), dtype=jnp.float32) * s_u1, 'b1': jax.random.normal(ks[7], (HID,), dtype=jnp.float32) * s_u1, 'W2': jax.random.normal(ks[8], (HID, HID), dtype=jnp.float32) * s_u2, 'b2': jax.random.normal(ks[9], (HID,), dtype=jnp.float32) * s_u2}
    _L3_gnn_all = _L3_gnn_setup()
    _L3_gnn_in = {k: v for k, v in _L3_gnn_all.items() if k in ('Wm', 'bm', 'W1', 'b1', 'W2', 'b2')}
    del _L3_gnn_all
    return {'x': x, 'src': src, 'dst': dst, 'edge_type_4': edge_type_4, 'edge_weight': edge_weight, 'L0_gnn_W1w': _L0_gnn_in['W1w'], 'L0_gnn_W1b': _L0_gnn_in['W1b'], 'L0_gnn_U1w': _L0_gnn_in['U1w'], 'L0_gnn_U1b': _L0_gnn_in['U1b'], 'L0_gnn_W2w': _L0_gnn_in['W2w'], 'L0_gnn_W2b': _L0_gnn_in['W2b'], 'L0_gnn_U2w': _L0_gnn_in['U2w'], 'L0_gnn_U2b': _L0_gnn_in['U2b'], 'L0_gnn_W3w': _L0_gnn_in['W3w'], 'L0_gnn_W3b': _L0_gnn_in['W3b'], 'L0_gnn_U3w': _L0_gnn_in['U3w'], 'L0_gnn_U3b': _L0_gnn_in['U3b'], 'L0_gnn_bn_g': _L0_gnn_in['bn_g'], 'L0_gnn_bn_b': _L0_gnn_in['bn_b'], 'L0_gnn_m_w0': _L0_gnn_in['m_w0'], 'L0_gnn_m_b0': _L0_gnn_in['m_b0'], 'L0_gnn_m_bng': _L0_gnn_in['m_bng'], 'L0_gnn_m_bnb': _L0_gnn_in['m_bnb'], 'L0_gnn_m_w1': _L0_gnn_in['m_w1'], 'L0_gnn_m_b1': _L0_gnn_in['m_b1'], 'L1_gnn_W': _L1_gnn_in['W'], 'L1_gnn_attn_src': _L1_gnn_in['attn_src'], 'L1_gnn_attn_dst': _L1_gnn_in['attn_dst'], 'L1_gnn_bias': _L1_gnn_in['bias'], 'L1_gnn_ln_gamma': _L1_gnn_in['ln_gamma'], 'L1_gnn_ln_beta': _L1_gnn_in['ln_beta'], 'L2_gnn_q_w': _L2_gnn_in['q_w'], 'L2_gnn_q_b': _L2_gnn_in['q_b'], 'L2_gnn_k_w': _L2_gnn_in['k_w'], 'L2_gnn_v_w': _L2_gnn_in['v_w'], 'L2_gnn_out_w': _L2_gnn_in['out_w'], 'L2_gnn_out_b': _L2_gnn_in['out_b'], 'L2_gnn_g1': _L2_gnn_in['g1'], 'L2_gnn_b1': _L2_gnn_in['b1'], 'L2_gnn_lin1_w': _L2_gnn_in['lin1_w'], 'L2_gnn_lin1_b': _L2_gnn_in['lin1_b'], 'L2_gnn_lin2_w': _L2_gnn_in['lin2_w'], 'L2_gnn_lin2_b': _L2_gnn_in['lin2_b'], 'L2_gnn_g2': _L2_gnn_in['g2'], 'L2_gnn_b2': _L2_gnn_in['b2'], 'L3_gnn_Wm': _L3_gnn_in['Wm'], 'L3_gnn_bm': _L3_gnn_in['bm'], 'L3_gnn_W1': _L3_gnn_in['W1'], 'L3_gnn_b1': _L3_gnn_in['b1'], 'L3_gnn_W2': _L3_gnn_in['W2'], 'L3_gnn_b2': _L3_gnn_in['b2']}

def reference(x, src, dst, edge_type_4, edge_weight, L0_gnn_W1w, L0_gnn_W1b, L0_gnn_U1w, L0_gnn_U1b, L0_gnn_W2w, L0_gnn_W2b, L0_gnn_U2w, L0_gnn_U2b, L0_gnn_W3w, L0_gnn_W3b, L0_gnn_U3w, L0_gnn_U3b, L0_gnn_bn_g, L0_gnn_bn_b, L0_gnn_m_w0, L0_gnn_m_b0, L0_gnn_m_bng, L0_gnn_m_bnb, L0_gnn_m_w1, L0_gnn_m_b1, L1_gnn_W, L1_gnn_attn_src, L1_gnn_attn_dst, L1_gnn_bias, L1_gnn_ln_gamma, L1_gnn_ln_beta, L2_gnn_q_w, L2_gnn_q_b, L2_gnn_k_w, L2_gnn_v_w, L2_gnn_out_w, L2_gnn_out_b, L2_gnn_g1, L2_gnn_b1, L2_gnn_lin1_w, L2_gnn_lin1_b, L2_gnn_lin2_w, L2_gnn_lin2_b, L2_gnn_g2, L2_gnn_b2, L3_gnn_Wm, L3_gnn_bm, L3_gnn_W1, L3_gnn_b1, L3_gnn_W2, L3_gnn_b2):
    import jax
    import jax.numpy as jnp

    def _L0_gnn_ref(x, edge_row, edge_col, edge_val, W1w, W1b, U1w, U1b, W2w, W2b, U2w, U2b, W3w, W3b, U3w, U3b, bn_g, bn_b, m_w0, m_b0, m_bng, m_bnb, m_w1, m_b1):
        import jax, jax.numpy as jnp
        import numpy as np
        N = 3125
        D = 128
        E = 50000
        EPS = 1e-05

        def _linear_params(key, d_in, d_out):
            kw, kb = jax.random.split(key)
            s = 1.0 / np.sqrt(d_in)
            W = jax.random.uniform(kw, (d_out, d_in), dtype=jnp.float32, minval=-s, maxval=s)
            b = jax.random.uniform(kb, (d_out,), dtype=jnp.float32, minval=-s, maxval=s)
            return (W, b)

        def _bn(h, g, b):
            m = jnp.mean(h, axis=0)
            v = jnp.var(h, axis=0)
            return (h - m) * jax.lax.rsqrt(v + EPS) * g + b

        def _lin(h, W, b):
            return h @ W.T + b
        msgs = edge_val[:, None] * x[edge_col]
        agg = jax.ops.segment_sum(msgs, edge_row, num_segments=N)
        ul = jax.nn.relu(_lin(agg, W1w, W1b) + _lin(x, U1w, U1b))
        rl = jax.nn.relu(_lin(agg, W2w, W2b) + _lin(x, U2w, U2b))
        fl = jnp.tanh(_lin(agg, W3w, W3b) + _lin(rl * x, U3w, U3b))
        out = ul * fl + (1.0 - ul) * x
        out = jax.nn.relu(_bn(out, bn_g, bn_b))
        out = jax.nn.relu(_bn(_lin(out, m_w0, m_b0), m_bng, m_bnb))
        out = _lin(out, m_w1, m_b1)
        return out

    def _L1_gnn_ref(x, edge_index, edge_type, W, attn_src, attn_dst, bias, ln_gamma, ln_beta):
        import jax, jax.numpy as jnp
        import numpy as np
        N_NODES = 50000
        N_EDGES = 25000
        IN_DIM = 128
        OUT_DIM = 32
        N_HEADS = 4
        N_REL = 4
        NEG_SLOPE = 0.2
        LN_EPS = 1e-05
        N = x.shape[0]
        R, H, D = attn_src.shape
        src = edge_index[0]
        dst = edge_index[1]
        out = jnp.zeros((N, H * D), dtype=x.dtype)
        for r in range(R):
            mask = (edge_type == r)[:, None]
            h = (x @ W[r]).reshape(N, H, D)
            e_src = jnp.einsum('ehd,hd->eh', h[src], attn_src[r])
            e_dst = jnp.einsum('ehd,hd->eh', h[dst], attn_dst[r])
            e = jax.nn.leaky_relu(e_src + e_dst, negative_slope=NEG_SLOPE)
            e_for_max = jnp.where(mask, e, -1e+30)
            e_max = jnp.maximum(jax.ops.segment_max(e_for_max, dst, num_segments=N), 0.0)
            e_exp = jnp.where(mask, jnp.exp(e - e_max[dst]), 0.0)
            e_sum = jax.ops.segment_sum(e_exp, dst, num_segments=N)
            alpha = e_exp / (e_sum[dst] + 1e-08)
            msg = alpha[:, :, None] * h[src]
            out_rel = jax.ops.segment_sum(msg, dst, num_segments=N)
            out = out + out_rel.reshape(N, H * D)
        out = out + bias
        out = out + x
        mu = jnp.mean(out, axis=-1, keepdims=True)
        var = jnp.mean(jnp.square(out - mu), axis=-1, keepdims=True)
        out = (out - mu) * jax.lax.rsqrt(var + LN_EPS) * ln_gamma + ln_beta
        return out

    def _L2_gnn_ref(src, edge_index, q_w, q_b, k_w, v_w, out_w, out_b, g1, b1, lin1_w, lin1_b, lin2_w, lin2_b, g2, b2):
        import jax, jax.numpy as jnp
        import numpy as np
        N, D, H, F = (50000, 128, 8, 512)
        HD = D // H
        EPS_BN = 1e-05

        def _batchnorm(x, gamma, beta):
            m = x.mean(axis=0)
            v = x.var(axis=0)
            return (x - m) * jax.lax.rsqrt(v + EPS_BN) * gamma + beta
        n = src.shape[0]
        loops = jnp.arange(n, dtype=edge_index.dtype)
        ei = jnp.concatenate([edge_index, jnp.stack([loops, loops])], axis=1)
        e_src, e_dst = (ei[0], ei[1])
        scaling = float(HD) ** (-0.5)
        q = ((src @ q_w.T + q_b) * scaling).reshape(n, H, HD)
        k = (src @ k_w.T).reshape(n, H, HD)
        v = (src @ v_w.T).reshape(n, H, HD)
        w = jnp.einsum('ehd,ehd->eh', q[e_dst], k[e_src])
        mx = jax.ops.segment_max(w, e_dst, num_segments=n)
        ex = jnp.exp(w - mx[e_dst])
        den = jax.ops.segment_sum(ex, e_dst, num_segments=n)
        attn_w = ex / (den[e_dst] + 1e-16)
        msgs = attn_w[:, :, None] * v[e_src]
        agg = jax.ops.segment_sum(msgs, e_dst, num_segments=n)
        attn_out = agg.reshape(n, D) @ out_w.T + out_b
        x = _batchnorm(src + attn_out, g1, b1)
        ff = jax.nn.leaky_relu(x @ lin1_w.T + lin1_b, negative_slope=0.01)
        ff = ff @ lin2_w.T + lin2_b
        x = _batchnorm(x + ff, g2, b2)
        return x

    def _L3_gnn_ref(z, edge_weight, edge_src, edge_dst, Wm, bm, W1, b1, W2, b2):
        import jax, jax.numpy as jnp
        import numpy as np
        N_NODES = 50000
        N_EDGES = 25000
        HID = 128
        n, H = z.shape
        Wd, Ws, ww = (Wm[:H], Wm[H:2 * H], Wm[2 * H])
        msgs = z[edge_dst] @ Wd + z[edge_src] @ Ws + edge_weight[:, None] * ww[None, :] + bm
        agg = jax.ops.segment_max(msgs, edge_dst, num_segments=n)
        deg = jax.ops.segment_sum(jnp.ones_like(edge_weight), edge_dst, num_segments=n)
        agg = jnp.where(deg[:, None] > 0, agg, jnp.zeros((), dtype=z.dtype))
        W1a, W1b = (W1[:H], W1[H:])
        hidden = jax.nn.relu(z @ W1a + agg @ W1b + b1)
        return hidden @ W2 + b2
    edge_index = jnp.stack([src, dst])
    x = _layernorm(x + _L0_gnn_ref(x, src, dst, edge_weight, L0_gnn_W1w, L0_gnn_W1b, L0_gnn_U1w, L0_gnn_U1b, L0_gnn_W2w, L0_gnn_W2b, L0_gnn_U2w, L0_gnn_U2b, L0_gnn_W3w, L0_gnn_W3b, L0_gnn_U3w, L0_gnn_U3b, L0_gnn_bn_g, L0_gnn_bn_b, L0_gnn_m_w0, L0_gnn_m_b0, L0_gnn_m_bng, L0_gnn_m_bnb, L0_gnn_m_w1, L0_gnn_m_b1), axis=-1)
    x = _layernorm(x + _L1_gnn_ref(x, edge_index, edge_type_4, L1_gnn_W, L1_gnn_attn_src, L1_gnn_attn_dst, L1_gnn_bias, L1_gnn_ln_gamma, L1_gnn_ln_beta), axis=-1)
    x = _layernorm(x + _L2_gnn_ref(x, edge_index, L2_gnn_q_w, L2_gnn_q_b, L2_gnn_k_w, L2_gnn_v_w, L2_gnn_out_w, L2_gnn_out_b, L2_gnn_g1, L2_gnn_b1, L2_gnn_lin1_w, L2_gnn_lin1_b, L2_gnn_lin2_w, L2_gnn_lin2_b, L2_gnn_g2, L2_gnn_b2), axis=-1)
    x = _layernorm(x + _L3_gnn_ref(x, edge_weight, src, dst, L3_gnn_Wm, L3_gnn_bm, L3_gnn_W1, L3_gnn_b1, L3_gnn_W2, L3_gnn_b2), axis=-1)
    return x

_drawn_inputs = setup_inputs


def setup_inputs(seed=0):
    import zlib

    import numpy as np

    out = dict(_drawn_inputs(seed))
    spreads = {'L0_gnn_bn_g': (1.0, 0.2),
     'L0_gnn_bn_b': (0.0, 0.268),
     'L0_gnn_m_bng': (1.0, 0.2),
     'L0_gnn_m_bnb': (0.0, 0.1),
     'L1_gnn_bias': (0.0, 0.48),
     'L1_gnn_ln_gamma': (1.0, 0.2),
     'L1_gnn_ln_beta': (0.0, 0.347),
     'L2_gnn_q_b': (0.0, 0.8),
     'L2_gnn_out_b': (0.0, 0.8),
     'L2_gnn_g1': (1.0, 0.2),
     'L2_gnn_b1': (0.0, 0.606),
     'L2_gnn_lin1_b': (0.0, 0.318),
     'L2_gnn_lin2_b': (0.0, 0.8),
     'L2_gnn_g2': (1.0, 0.2),
     'L2_gnn_b2': (0.0, 0.1)}
    factors = {'L0_gnn_W1b': 5.36,
     'L0_gnn_U1b': 5.592,
     'L0_gnn_W2b': 8.0,
     'L0_gnn_U2b': 8.0,
     'L0_gnn_W3b': 7.312,
     'L0_gnn_U3b': 7.874,
     'L0_gnn_m_b0': 8.0,
     'L2_gnn_q_w': 4.948,
     'L2_gnn_k_w': 4.89}
    for name, (base, spread) in spreads.items():
        noise = np.random.default_rng([zlib.crc32(name.encode()), seed]).standard_normal(out[name].shape)
        drawn = base * np.exp(spread * noise) if base else spread * noise
        out[name] = jnp.asarray(drawn.astype(out[name].dtype))
    for name, factor in factors.items():
        out[name] = (out[name] * factor).astype(out[name].dtype)
    return out
```

```python
from contextlib import ExitStack, contextmanager

import concourse.bass as bass
from concourse import mybir

F32 = mybir.dt.float32
BF16 = mybir.dt.bfloat16
I32 = mybir.dt.int32
ALU = mybir.AluOpType
ACT = mybir.ActivationFunctionType
AX = mybir.AxisListType

P = 128
N, D, E = 3125, 128, 100000
NB = -(-N // P)
NP = NB * P
TAIL = N - (NB - 1) * P
HALF = 14
BODY = 2 * HALF
TURNS = 28
T = BODY * TURNS
EP = P * T
LAST = E - (P - 1) * T
assert EP >= E and 0 < LAST <= T
SEVEN = 7
TABS = 4
REL, H1, D1 = 4, 4, 32
RH = REL * H1
H2, D2 = 8, 16
FF = 4
R1 = REL * D + 2 * RH
R2 = D + 2 * H2
HS = D + H1
BIG = 1e30
EPS = 1e-5
CHUNKS = [(c, min(512, NP - c)) for c in range(0, NP, 512)]
REALCH = [(c, min(512, N - c)) for c in range(0, N, 512)]

TRANSPOSED = ["L0_gnn_W1w", "L0_gnn_U1w", "L0_gnn_W2w", "L0_gnn_U2w", "L0_gnn_W3w", "L0_gnn_U3w",
              "L0_gnn_m_w0", "L0_gnn_m_w1", "L2_gnn_q_w", "L2_gnn_k_w", "L2_gnn_v_w", "L2_gnn_out_w"]
LIN1 = len(TRANSPOSED)
LIN2 = LIN1 + FF
SLOTS = LIN2 + FF
COLUMNS = ["L0_gnn_W1b", "L0_gnn_U1b", "L0_gnn_W2b", "L0_gnn_U2b", "L0_gnn_W3b", "L0_gnn_U3b",
           "L0_gnn_bn_g", "L0_gnn_bn_b", "L0_gnn_m_b0", "L0_gnn_m_bng", "L0_gnn_m_bnb",
           "L2_gnn_out_b", "L2_gnn_g1", "L2_gnn_b1", "L2_gnn_lin2_b", "L2_gnn_g2", "L2_gnn_b2",
           "L3_gnn_b1"]
ROWS = ["L0_gnn_m_b1", "L1_gnn_bias", "L1_gnn_ln_gamma", "L1_gnn_ln_beta", "L2_gnn_q_b", "L3_gnn_bm", "L3_gnn_b2"]


class Memory:
    pass


def spread(ap, axis, shape):
    return ap.unsqueeze(axis).broadcast_to(shape)


def hold(eng, sem, value):
    eng.wait_ge(sem, value)
    eng.nop(nofuse=True)


@contextmanager
def phase(nc, of):
    sems = []

    def sem(name):
        sems.append(nc.alloc_semaphore(f"{of}_{name}"))
        return sems[-1]

    yield sem
    nc.clear_and_free_semaphores(sems)
    nc.all_engine_barrier()


def lanes(rows):
    return rows[0:EP, :].rearrange("(p t) f -> p t f", p=P)


def allocate(nc, ctx):
    m = Memory()

    def sb(name, shape, dt=F32):
        return ctx.enter_context(nc.sbuf_tensor(name, shape, dt))

    def dram(name, shape, dt=F32):
        return nc.dram_tensor(name, shape, dt, kind="Internal").ap()

    m.src = sb("src", [P, T + BODY], I32)
    m.src_rel = sb("src_rel", [P, T + BODY], I32)
    m.val = sb("val", [P, T])
    m.keep = sb("keep", [P, T])
    m.reset = sb("reset", [P, T])
    m.other_rel = sb("other_rel", [P, T, REL])
    m.lane_first = sb("lane_first", [P, 1], I32)
    m.first_end = sb("first_end", [P, 1], I32)
    m.first_fix = sb("first_fix", [P, 1], I32)
    m.whole_neg = sb("whole_neg", [P, P])
    m.start = sb("start", [P, NB], I32)
    m.end = sb("end", [P, NB], I32)
    m.has = sb("has", [P, NB])
    m.xN = sb("xN", [P, NB, D])
    m.xT = sb("xT", [P, NP])
    m.ident = sb("ident", [P, P])
    m.spare = sb("spare", [P, 1])
    m.lower = sb("lower", [P, P])
    m.tri = sb("tri", [P, P])
    m.ones = sb("ones", [P, P])
    m.eps = sb("eps", [P, 1])
    m.eps_zero = sb("eps_zero", [P, 1])
    m.wt = sb("wt", [P, SLOTS, P])
    m.cols = sb("cols", [P, len(COLUMNS)])
    m.lin1_b = sb("lin1_b", [P, FF])
    m.rows = sb("rows", [P, len(ROWS), D])
    m.w_rel = sb("w_rel", [P, REL, D])
    m.w3 = sb("w3", [P, 5, D])
    m.edge_w = sb("edge_w", [P, D])
    m.lane_end = sb("lane_end", [P, R1])
    m.arena = sb("arena", [P, 33500])
    m.psum = ctx.enter_context(nc.psum_tensor("psum", [P, 8, 512], F32))

    m.seg_rows = dram("seg_rows", [EP + NP, D])
    m.seg_dst = dram("seg_dst", [EP + NP, RH])
    m.tabs = [dram(f"tab{j}", [NP + P, D]) for j in range(TABS)]
    m.rows1 = dram("rows1", [EP + 1 + P, R1])
    m.rows2 = dram("rows2", [EP + 1 + P, R2])
    m.rows3 = dram("rows3", [EP + 1 + P, D])
    m.table1 = dram("table1", [NP * REL, HS])
    m.dst1 = dram("dst1", [NP, RH])
    m.query2 = dram("query2", [NP, D])
    m.table2 = dram("table2", [NP, 2 * D])
    m.table3 = dram("table3", [NP, D])
    return m


class Arena:

    def __init__(self, m):
        self.m, self.at = m, 0

    def __call__(self, *shape, dt=F32):
        n = 1
        for s in shape:
            n *= s
        words = n if dt != BF16 else -(-n // 2)
        ap = self.m.arena[:, self.at:self.at + words]
        self.at += words
        assert self.at <= 33500, self.at
        if dt != F32:
            ap = ap.bitcast(dt)
        if len(shape) == 2:
            ap = ap.rearrange("p (a b) -> p a b", b=shape[1])
        if len(shape) == 3:
            ap = ap.rearrange("p (a b c) -> p a b c", b=shape[1], c=shape[2])
        return ap


def setup_phase(nc, m, I):
    with phase(nc, "setup_phase") as sem:
        A = Arena(m)
        dst = A(T, dt=I32)
        typ = A(T, dt=I32)
        dstf = A(T)
        typf = A(T)
        lo_i = A(T, dt=I32)
        hi_i = A(T, dt=I32)
        lo = A(T, dt=BF16)
        hi = A(T, dt=BF16)
        same = A(T)
        prev_last = A(1, dt=I32)
        prev_lastf = A(1)
        iota = A(P, dt=BF16)
        iota_i = A(P, dt=I32)
        nul = A(P, dt=BF16)
        spare_start = A(NB)
        spare_row = A(1)
        lane_base = A(1)
        hot_lo = [A(HALF, P, dt=BF16) for _ in range(2)]
        hot_hi = [A(HALF, NB, dt=BF16) for _ in range(2)]
        deg, cum, tot, incl, end1, tmp, ones_nb = (A(NB) for _ in range(7))
        count, firstf, whole = A(1), A(1), A(1)
        zeros = A(BODY * D)
        neutral = A(R1 + D)
        w_nat = A(SLOTS, P)

        fixed = sem("fixed_parts_set")
        const = sem("constants_made")
        l_dst, l_edge, l_x, l_prev = sem("dst_loaded"), sem("edges_loaded"), sem("x_loaded"), sem("prev_loaded")
        l_w, l_small = sem("weights_loaded"), sem("small_loaded")
        zeroed = sem("scratch_zeroed")
        prep = sem("edge_parts")
        hot_free = [sem(f"hot_free{h}") for h in range(2)]
        hot_made = [sem(f"hot_made{h}") for h in range(2)]
        deg_done, cum_done, whole_done = sem("degrees_counted"), sem("degrees_summed"), sem("whole_spread")
        wt_done, wt_kept = sem("weights_turned"), sem("weights_kept")
        xt_done, xt_kept = sem("x_turned"), sem("x_kept")
        scattered = sem("x_scattered")
        ps = m.psum
        WGROUPS = SLOTS // 4

        (S_DSTF, S_LOI, S_HII, S_LO, S_HI, S_PREV) = range(1, 7)

        with nc.Block() as block:

            @block.gpsimd
            def _(eng):
                eng.memset(zeros, 0.0).then_inc(const, 1)
                eng.iota(iota_i, [[1, P]], base=0, channel_multiplier=0).then_inc(const, 1)
                eng.memset(nul, 0.0).then_inc(const, 1)
                eng.memset(m.ones[:, :], 1.0).then_inc(const, 1)
                eng.wait_ge(const, 4)
                eng.affine_select(out=m.ident[:, :], in_=m.ones[:, :], compare_op=ALU.is_equal, fill=0.0, base=0,
                                  pattern=[[-1, P]], channel_multiplier=1).then_inc(const, 1)
                eng.affine_select(out=m.lower[:, :], in_=m.ones[:, :], compare_op=ALU.is_gt, fill=0.0, base=0,
                                  pattern=[[-1, P]], channel_multiplier=1).then_inc(const, 1)
                eng.affine_select(out=m.tri[:, :], in_=m.ones[:, :], compare_op=ALU.is_ge, fill=0.0, base=0,
                                  pattern=[[1, P]], channel_multiplier=-1).then_inc(const, 1)
                eng.iota(spare_start, [[P, NB]], base=EP, channel_multiplier=1,
                         allow_small_or_imprecise_dtypes=True).then_inc(const, 1)
                eng.iota(m.spare[:, :], [[1, 1]], base=NP, channel_multiplier=1,
                         allow_small_or_imprecise_dtypes=True).then_inc(const, 1)
                eng.iota(spare_row, [[1, 1]], base=EP + 1, channel_multiplier=1,
                         allow_small_or_imprecise_dtypes=True).then_inc(const, 1)
                eng.iota(lane_base, [[1, 1]], base=-1, channel_multiplier=T,
                         allow_small_or_imprecise_dtypes=True).then_inc(const, 1)
                eng.memset(m.eps[:, :], EPS).then_inc(const, 1)
                eng.memset(ones_nb, 1.0).then_inc(const, 1)
                eng.memset(neutral[:, 0:R1], 0.0).then_inc(const, 1)
                eng.wait_ge(const, 14)
                eng.memset(neutral[:, R1 - RH:R1 + D], -BIG).then_inc(const, 1)
                eng.memset(m.eps_zero[:, :], 0.0).then_inc(const, 1)
                eng.wait_ge(l_x, 32)
                eng.wait_ge(zeroed, 16 * ZEROS)
                eng.wait_ge(prep, S_START)
                for b in range(NB):
                    eng.indirect_dma_start(out=m.seg_rows[:, :],
                                           out_offset=bass.IndirectOffsetOnAxis(ap=m.start[:, b:b + 1], axis=0),
                                           in_=m.xN[:, b, :], in_offset=None).then_inc(scattered, 16)
                eng.wait_ge(scattered, 16 * NB)

            @block.sync
            def _(eng):
                eng.wait_ge(fixed, 6)
                for tile, name, s in ((dst, "dst", l_dst), (m.src[:, 0:T], "src", l_edge),
                                      (typ, "edge_type_4", l_edge), (m.val[:, :], "edge_weight", l_edge)):
                    eng.dma_start(tile[0:112, :], I[name][0:112 * T].rearrange("(p t) -> p t", t=T)).then_inc(s, 16)
                    eng.dma_start(tile[112:127, :], I[name][112 * T:127 * T].rearrange("(p t) -> p t", t=T)).then_inc(s, 16)
                    eng.dma_start(tile[127:128, 0:LAST], I[name][127 * T:E].rearrange("(p t) -> p t", p=1)).then_inc(s, 16)
                eng.dma_start(prev_last[1:P, :], I["dst"][0:(P - 1) * T].rearrange("(p t) -> p t", t=T)[:, T - 1:T],
                              allow_slow_non_contiguous=True).then_inc(l_prev, 16)
                eng.dma_start(m.xN[:, 0:NB - 1, :], I["x"][0:(NB - 1) * P, :].rearrange("(b p) f -> p b f", p=P)).then_inc(l_x, 16)
                eng.dma_start(m.xN[0:TAIL, NB - 1, :], I["x"][(NB - 1) * P:N, :]).then_inc(l_x, 16)
                eng.wait_ge(const, 16)
                eng.dma_start(m.rows1[EP:EP + 1, :], neutral[0:1, 0:R1]).then_inc(zeroed, 16)
                eng.dma_start(m.rows2[EP:EP + 1, :], neutral[0:1, R1 - RH - D - H2:R1 - RH + H2]).then_inc(zeroed, 16)
                eng.dma_start(m.rows3[EP:EP + 1, :], neutral[0:1, R1:R1 + D]).then_inc(zeroed, 16)

                for rows, width in ((m.rows1, R1), (m.rows2, R2), (m.rows3, D)):
                    eng.dma_start(rows[EP + 1:EP + 1 + P, :], zeros[:, 0:width]).then_inc(zeroed, 16)

            @block.scalar
            def _(eng):
                for s, name in enumerate(TRANSPOSED):
                    eng.dma_start(w_nat[:, s, :], I[name]).then_inc(l_w, 16)
                eng.dma_start(w_nat[:, LIN1:LIN2, :], I["L2_gnn_lin1_w"].rearrange("(j o) i -> o j i", o=P)).then_inc(l_w, 16)
                eng.dma_start(w_nat[:, LIN2:SLOTS, :], I["L2_gnn_lin2_w"].rearrange("o (j i) -> o j i", i=P)).then_inc(l_w, 16)
                eng.wait_ge(const, 1)
                with eng.Fori(0, TURNS) as i:
                    eng.dma_start(lanes(m.seg_rows)[:, bass.ds(i * BODY, BODY), :].rearrange("p t f -> p (t f)"), zeros).then_inc(zeroed, 16)
                for k in range(2 * RH // 8):
                    eng.dma_start(m.seg_dst[0:EP, :].rearrange("(p t) f -> p (t f)", p=P)[:, k * T * 4:(k + 1) * T * 4],
                                  zeros[:, 0:T * 4]).then_inc(zeroed, 16)
                for c, name in enumerate(COLUMNS):
                    eng.dma_start(m.cols[:, c:c + 1], I[name].rearrange("(p a) -> p a", a=1), allow_slow_non_contiguous=True).then_inc(l_small, 16)
                eng.dma_start(m.lin1_b[:, :], I["L2_gnn_lin1_b"].rearrange("(j p) -> p j", p=P), allow_slow_non_contiguous=True).then_inc(l_small, 16)
                for r, name in enumerate(ROWS):
                    eng.dma_start(m.rows[:, r, :], I[name].partition_broadcast(P)).then_inc(l_small, 16)
                eng.dma_start(m.w_rel[:, :, :], I["L1_gnn_W"].rearrange("r i o -> i r o")).then_inc(l_small, 16)
                for k, (name, at) in enumerate((("L3_gnn_Wm", 0), ("L3_gnn_Wm", D), ("L3_gnn_W1", 0), ("L3_gnn_W1", D), ("L3_gnn_W2", 0))):
                    eng.dma_start(m.w3[:, k, :], I[name][at:at + D, :]).then_inc(l_small, 16)
                eng.dma_start(m.edge_w[:, :], I["L3_gnn_Wm"][2 * D, :].partition_broadcast(P)).then_inc(l_small, 16)
                for g in range(WGROUPS):
                    eng.wait_ge(wt_done, g + 1)
                    eng.activation(m.wt[:, 4 * g:4 * g + 4, :], ps[:, g, :].rearrange("p (a b) -> p a b", b=P), ACT.Copy).then_inc(wt_kept, 1)
                for k, (c, w) in enumerate(CHUNKS):
                    eng.wait_ge(xt_done, k + 1)
                    eng.activation(m.xT[:, c:c + w], ps[:, k % 2, 0:w], ACT.Copy).then_inc(xt_kept, 1)
                eng.wait_ge(l_small, 16 * SMALL)
                eng.wait_ge(zeroed, 16 * ZEROS)

            @block.tensor
            def _(eng):
                eng.wait_ge(const, 16)
                eng.wait_ge(l_w, 16 * (len(TRANSPOSED) + 2))
                for g in range(WGROUPS):
                    for k in range(4):
                        t = eng.transpose(ps[:, g, k * P:k * P + P], w_nat[:, 4 * g + k, :], m.ident[:, :])
                    t.then_inc(wt_done, 1)
                eng.wait_ge(l_x, 32)
                for k, (c, w) in enumerate(CHUNKS):
                    eng.wait_ge(wt_kept, 2)
                    if k >= 2:
                        eng.wait_ge(xt_kept, k - 1)
                    for b in range(w // P):
                        t = eng.transpose(ps[:, k % 2, b * P:b * P + P], m.xN[:, c // P + b, :], m.ident[:, :])
                    t.then_inc(xt_done, 1)
                eng.matmul(ps[:, 7, 0:NB], nul, nul[:, 0:NB], start=True, stop=False)
                for h in range(2):
                    eng.nop().then_inc(hot_free[h], 1)
                with eng.Fori(0, TURNS) as i:
                    for h in range(2):
                        eng.wait_ge(hot_made[h], 2 * i + 2)
                        for j in range(HALF):
                            t = eng.matmul(ps[:, 7, 0:NB], hot_lo[h][:, j, :], hot_hi[h][:, j, :], start=False, stop=False,
                                           skip_group_check=True)
                        t.then_inc(hot_free[h], 1)
                eng.matmul(ps[:, 7, 0:NB], nul, nul[:, 0:NB], start=False, stop=True).then_inc(deg_done, 1)
                eng.wait_ge(prep, S_DEG)
                eng.matmul(ps[:, 6, 0:NB], m.tri[:, :], deg, start=True, stop=True)
                eng.matmul(ps[:, 6, 64:64 + NB], m.ones[:, :], deg, start=True, stop=True).then_inc(cum_done, 1)
                eng.wait_ge(prep, S_WHOLE)
                eng.matmul(ps[:, 5, 0:P], whole.broadcast_to([P, P]), m.ident[:, :], start=True, stop=True).then_inc(whole_done, 1)

            @block.vector
            def _(eng):
                eng.memset(dst[96:P, LAST:T], NP - 1).then_inc(fixed, 1)
                eng.memset(m.src[:, LAST:T + BODY], 0).then_inc(fixed, 1)
                eng.memset(typ[96:P, LAST:T], 0).then_inc(fixed, 1)
                eng.memset(m.val[96:P, LAST:T], 0.0).then_inc(fixed, 1)
                eng.memset(prev_last, -1).then_inc(fixed, 1)
                eng.memset(m.xN[:, NB - 1, :], 0.0).then_inc(fixed, 1)
                eng.wait_ge(l_dst, 48)
                eng.tensor_copy(dstf, dst).then_inc(prep, 1)
                eng.tensor_scalar(lo_i, dst, P - 1, None, ALU.bitwise_and).then_inc(prep, 1)
                eng.tensor_scalar(hi_i, dst, 7, None, ALU.logical_shift_right).then_inc(prep, 1)
                eng.wait_ge(prep, S_LOI)
                eng.tensor_copy(lo, lo_i).then_inc(prep, 1)
                eng.wait_ge(prep, S_HII)
                eng.tensor_copy(hi, hi_i).then_inc(prep, 1)
                eng.wait_ge(const, 16)
                eng.tensor_copy(iota, iota_i).then_inc(prep, 1)
                eng.wait_ge(prep, S_PREV)
                with eng.Fori(0, TURNS) as i:
                    for h in range(2):
                        eng.wait_ge(hot_free[h], i + 1)
                        eng.tensor_tensor(hot_lo[h], spread(iota, 1, [P, HALF, P]),
                                          spread(lo[:, bass.ds(i * BODY + h * HALF, HALF)], 2, [P, HALF, P]), ALU.is_equal).then_inc(hot_made[h], 1)
                        eng.tensor_tensor(hot_hi[h], spread(iota[:, 0:NB], 1, [P, HALF, NB]),
                                          spread(hi[:, bass.ds(i * BODY + h * HALF, HALF)], 2, [P, HALF, NB]), ALU.is_equal).then_inc(hot_made[h], 1)
                n = S_PREV

                def step(ins):
                    nonlocal n
                    n += 1
                    ins.then_inc(prep, 1)
                    eng.wait_ge(prep, n)
                    return n

                eng.wait_ge(deg_done, 1)
                assert step(eng.tensor_copy(deg, ps[:, 7, 0:NB])) == S_DEG
                eng.wait_ge(cum_done, 1)
                step(eng.tensor_copy(tot, ps[:, 6, 64:64 + NB]))
                step(eng.tensor_tensor_scan(incl, ones_nb, tot, 0.0, ALU.mult, ALU.add))
                step(eng.tensor_tensor(incl, incl, tot, ALU.subtract))
                step(eng.tensor_tensor(end1, ps[:, 6, 0:NB], incl, ALU.add))
                step(eng.tensor_scalar(m.has[:, :], deg, 1.0, None, ALU.min))
                step(eng.tensor_tensor(tmp, end1, deg, ALU.subtract))
                step(eng.tensor_tensor(tmp, tmp, spare_start, ALU.subtract))
                step(eng.tensor_tensor(tmp, tmp, m.has[:, :], ALU.mult))
                assert step(eng.tensor_tensor(m.start[:, :], tmp, spare_start, ALU.add)) == S_START
                step(eng.scalar_tensor_tensor(out=tmp, in0=end1, scalar=float(-1 - EP), in1=m.has[:, :], op0=ALU.add, op1=ALU.mult))
                step(eng.tensor_scalar(m.end[:, :], tmp, float(EP), None, ALU.add))
                eng.wait_ge(l_prev, 16)
                step(eng.tensor_copy(prev_lastf, prev_last))
                assert step(eng.tensor_tensor(whole, dstf[:, T - 1:T], prev_lastf, ALU.is_equal)) == S_WHOLE
                step(eng.tensor_tensor(m.keep[:, 1:T], dstf[:, 1:T], dstf[:, 0:T - 1], ALU.is_equal))
                step(eng.tensor_tensor(m.keep[:, 0:1], dstf[:, 0:1], prev_lastf, ALU.is_equal))
                step(eng.tensor_scalar(m.reset[:, :], m.keep[:, :], -1.0, BIG, ALU.add, ALU.mult))
                step(eng.tensor_scalar(same, dstf, dstf[:, 0:1], None, ALU.is_equal))
                step(eng.tensor_reduce(count, same, AX.X, ALU.add))
                step(eng.tensor_tensor(firstf, count, lane_base, ALU.add))
                step(eng.tensor_copy(m.first_end[:, :], firstf))
                step(eng.tensor_tensor(firstf, firstf, spare_row, ALU.subtract))
                step(eng.tensor_tensor(firstf, firstf, m.keep[:, 0:1], ALU.mult))
                step(eng.tensor_tensor(m.first_fix[:, :], firstf, spare_row, ALU.add))
                step(eng.tensor_copy(m.lane_first[:, :], dst[:, 0:1]))
                eng.wait_ge(l_edge, 16 * 9)
                step(eng.tensor_copy(same, m.src[:, 0:T]))
                step(eng.tensor_copy(typf, typ))
                step(eng.scalar_tensor_tensor(out=m.src_rel[:, 0:T], in0=same, scalar=float(REL), in1=typf, op0=ALU.mult, op1=ALU.add))
                step(eng.memset(m.src_rel[:, T:T + BODY], 0))
                for r in range(REL):
                    step(eng.tensor_scalar(m.other_rel[:, :, r], typf, float(r), -BIG, ALU.not_equal, ALU.mult))
                eng.wait_ge(whole_done, 1)
                step(eng.tensor_scalar(m.whole_neg[:, :], ps[:, 5, 0:P], -1.0, BIG, ALU.add, ALU.mult))


S_DEG = 7
S_START = 16
S_WHOLE = 20
ZEROS = TURNS + 4 + 6
SMALL = len(COLUMNS) + 1 + len(ROWS) + 1 + 5 + 1


def layer0_edges(nc, m, I):
    with phase(nc, "layer0_edges") as sem:
        A = Arena(m)
        xr = [A(HALF, D) for _ in range(2)]
        xv = [A(SEVEN, D) for _ in range(2)]
        eq = [A(SEVEN, P) for _ in range(2)]
        before = A(SEVEN, P)
        rows = [A(SEVEN, D) for _ in range(4)]
        idx = [A(SEVEN, dt=I32) for _ in range(4)]
        srcs = A(BODY)
        vals = A(BODY)
        keeps = A(BODY)
        to_spare = A(BODY)
        rank = A(SEVEN)
        ranks = A(SEVEN)
        ps = m.psum

        def spread_bank(u):
            return ps[:, 2 * (u % 2):2 * (u % 2) + 2, :].rearrange("p a (b c) -> p (a b) c", c=P)[:, 0:SEVEN, :]

        def sum_bank(u):
            return ps[:, 4 + 2 * (u % 2):6 + 2 * (u % 2), :].rearrange("p a (b c) -> p (a b) c", c=P)[:, 0:SEVEN, :]

        first = sem("lane_first_row")
        landed = [sem(f"x_rows_landed{h}") for h in range(2)]
        carried = sem("x_carried")
        staged = sem("marks_staged")
        vals_staged = sem("weights_staged")
        weighed = sem("x_weighed")
        sources = sem("sources_spread")
        eq_made = sem("eq_made")
        ranked = sem("ranks")
        summed = sem("rows_summed")
        kept = sem("rows_kept")
        added = [sem(f"added{j}") for j in range(TABS)]
        UN = BODY // SEVEN
        RANK = 5

        zeros = A((NP + P) // P * D)
        cleared = sem("zeros_set")
        unit_added = sem("units_added")

        with nc.Block() as block:

            @block.sync
            def _(eng):
                def load(h, t):
                    eng.dma_start(xr[h], lanes(m.seg_rows)[:, t, :]).then_inc(landed[h], 16)

                load(0, bass.ds(0, HALF))
                with eng.Fori(0, TURNS - 1) as i:
                    hold(eng, carried, i * BODY + 2)
                    hold(eng, weighed, i * BODY + 1)
                    load(1, bass.ds(i * BODY + HALF, HALF))
                    hold(eng, carried, i * BODY + HALF + 2)
                    hold(eng, weighed, i * BODY + HALF + 1)
                    load(0, bass.ds(i * BODY + BODY, HALF))
                hold(eng, carried, (TURNS - 1) * BODY + 2)
                hold(eng, weighed, (TURNS - 1) * BODY + 1)
                load(1, bass.ds((TURNS - 1) * BODY + HALF, HALF))

            @block.gpsimd
            def _(eng):
                eng.indirect_dma_start(out=xr[1][:, HALF - 1, :], out_offset=None, in_=I["x"],
                                       in_offset=bass.IndirectOffsetOnAxis(ap=m.lane_first[:, 0:1], axis=0)).then_inc(first, 16)
                eng.wait_ge(cleared, 1)
                for j in range(TABS):
                    eng.dma_start(m.tabs[j].rearrange("(p r) f -> p (r f)", p=P), zeros).then_inc(added[j], 16)
                with eng.Fori(0, TURNS) as i:
                    for u in range(UN):
                        eng.wait_ge(kept, i * UN + u + 3)
                        eng.wait_ge(ranked, (i * UN + u + 1) * RANK + 1)
                        for k in range(SEVEN):
                            s = u * SEVEN + k
                            j = s % TABS
                            hold(eng, added[j], 16 * (i * (BODY // TABS) + s // TABS) + 16)
                            if k == TABS - 1:
                                eng.nop().then_inc(unit_added, 1)
                            eng.indirect_dma_start(out=m.tabs[j], out_offset=bass.IndirectOffsetOnAxis(ap=idx[u][:, k:k + 1], axis=0),
                                                   in_=rows[u][:, k, :], in_offset=None, compute_op=ALU.add).then_inc(added[j], 16)
                for j in range(TABS):
                    eng.wait_ge(added[j], 16 + 16 * (TURNS * BODY // TABS))

            @block.vector
            def _(eng):
                eng.memset(zeros, 0.0).then_inc(cleared, 1)
                eng.engine_nop().then_inc(unit_added, UN)
                eng.engine_nop().then_inc(carried, 1)
                eng.engine_nop().then_inc(ranked, 1)
                eng.engine_nop().then_inc(eq_made, 2)
                eng.wait_ge(first, 16)
                with eng.Fori(0, TURNS) as i:
                    eng.wait_ge(carried, i * BODY + 1)
                    hold(eng, ranked, i * UN * RANK + 1)
                    eng.tensor_copy(keeps, m.keep[:, bass.ds(i * BODY, BODY)]).then_inc(staged, 1)
                    eng.tensor_copy(srcs, m.src[:, bass.ds(i * BODY, BODY)]).then_inc(staged, 1)
                    eng.wait_ge(staged, 3 * i + 2)
                    eng.tensor_scalar(to_spare, srcs, -1.0, m.spare[:, 0:1], ALU.mult, ALU.add).then_inc(staged, 1)
                    eng.wait_ge(staged, 3 * i + 3)
                    for u in range(UN):
                        h = u // 2
                        if u % 2 == 0:
                            eng.wait_ge(landed[h], 16 * i + 16)
                        for k in range(SEVEN):
                            s = u * SEVEN + k
                            j = s % HALF
                            prev = xr[h][:, j - 1, :] if j else xr[1 - h][:, HALF - 1, :]
                            eng.wait_ge(carried, i * BODY + s + 1)
                            eng.scalar_tensor_tensor(out=xr[h][:, j, :], in0=prev, scalar=keeps[:, s:s + 1], in1=xr[h][:, j, :],
                                                     op0=ALU.mult, op1=ALU.add).then_inc(carried, 1)
                        eng.wait_ge(sources, i * UN + u + 1)
                        eng.wait_ge(summed, i * UN + u + 1)
                        eng.tensor_tensor(eq[u % 2], spread_bank(u), spread(srcs[:, u * SEVEN:(u + 1) * SEVEN], 2, [P, SEVEN, P]),
                                          ALU.is_equal).then_inc(eq_made, 1)
                        eng.wait_ge(eq_made, i * UN + u + 3)
                        eng.wait_ge(ranked, (i * UN + u) * RANK + 1)
                        at = (i * UN + u) * RANK
                        eng.tensor_tensor(before, eq[u % 2], spread(m.lower[:, :], 1, [P, SEVEN, P]), ALU.mult).then_inc(ranked, 1)
                        eng.wait_ge(ranked, at + 2)
                        eng.tensor_reduce(rank, before, AX.X, ALU.add).then_inc(ranked, 1)
                        eng.wait_ge(ranked, at + 3)
                        eng.tensor_scalar(ranks, rank, 1.0, None, ALU.min).then_inc(ranked, 1)
                        eng.wait_ge(ranked, at + 4)
                        eng.tensor_tensor(ranks, ranks, to_spare[:, u * SEVEN:(u + 1) * SEVEN], ALU.mult).then_inc(ranked, 1)
                        eng.wait_ge(ranked, at + 5)
                        eng.wait_ge(unit_added, i * UN + u + 2)
                        eng.tensor_tensor(idx[u], ranks, srcs[:, u * SEVEN:(u + 1) * SEVEN], ALU.add).then_inc(ranked, 1)

            @block.tensor
            def _(eng):
                eng.nop().then_inc(summed, 2)
                with eng.Fori(0, TURNS) as i:
                    eng.wait_ge(staged, 3 * i + 3)
                    for u in range(UN + 1):
                        if u < UN:
                            eng.wait_ge(eq_made, i * UN + u + 1)
                            for k in range(SEVEN):
                                s = u * SEVEN + k
                                t = eng.matmul(spread_bank(u)[:, k, :], srcs[:, s:s + 1].broadcast_to([P, P]), m.ident[:, :], start=True, stop=True)
                            t.then_inc(sources, 1)
                        if u > 0:
                            v = u - 1
                            eng.wait_ge(eq_made, i * UN + v + 3)
                            eng.wait_ge(weighed, i * BODY + (v + 1) * SEVEN + 1)
                            eng.wait_ge(kept, i * UN + v + 1)
                            for k in range(SEVEN):
                                t = eng.matmul(sum_bank(v)[:, k, :], eq[v % 2][:, k, :], xv[v % 2][:, k, :], start=True, stop=True)
                            t.then_inc(summed, 1)

            @block.scalar
            def _(eng):
                eng.nop().then_inc(weighed, 1)
                eng.nop().then_inc(kept, 2)
                with eng.Fori(0, TURNS) as i:
                    eng.activation(vals, m.val[:, bass.ds(i * BODY, BODY)], ACT.Copy).then_inc(vals_staged, 1)
                    eng.wait_ge(vals_staged, i + 1)
                    for u in range(UN + 1):
                        if u < UN:
                            eng.wait_ge(carried, i * BODY + (u + 1) * SEVEN + 1)
                            for k in range(SEVEN):
                                s = u * SEVEN + k
                                eng.activation(xv[u % 2][:, k, :], xr[s // HALF][:, s % HALF, :], ACT.Copy, scale=vals[:, s:s + 1]).then_inc(weighed, 1)
                        if u > 0:
                            v = u - 1
                            eng.wait_ge(summed, i * UN + v + 3)
                            eng.wait_ge(unit_added, i * UN + v + 2)
                            eng.activation(rows[v], sum_bank(v), ACT.Copy).then_inc(kept, 1)


class Steps:

    def __init__(self, eng, sem, start=0):
        self.eng, self.sem, self.n = eng, sem, start

    def put(self, ins):
        ins.then_inc(self.sem, 1)
        self.n += 1

    def wait(self):
        self.eng.wait_ge(self.sem, self.n)

    def then(self, ins):
        self.put(ins)
        self.wait()


def turn_out(eng, ps, nodes, turned, kept, ident, bank):
    for k, (c, w) in enumerate(CHUNKS):
        if k >= 2:
            eng.wait_ge(kept, k - 1)
        for b in range(w // P):
            t = eng.transpose(ps[:, bank + k % 2, b * P:b * P + P], nodes[:, c // P + b, :], ident)
        t.then_inc(turned, 1)


def turn_in(eng, ps, out, turned, kept, bank):
    for k, (c, w) in enumerate(CHUNKS):
        eng.wait_ge(turned, k + 1)
        eng.activation(out[:, c:c + w], ps[:, bank + k % 2, 0:w], ACT.Copy).then_inc(kept, 1)


def layer0_nodes(nc, m, I):
    with phase(nc, "layer0_nodes") as sem:
        A = Arena(m)
        big = A(8 * NP)
        agg = [big[:, j * NP:(j + 1) * NP].rearrange("p (b f) -> p b f", f=D) for j in range(TABS)]
        aggT, uT, rT, oT = (big[:, j * NP:(j + 1) * NP] for j in range(4, 8))
        fT, hT, gT, h2T = (big[:, j * NP:(j + 1) * NP] for j in (1, 2, 3, 1))
        y = agg[0]
        bias = A(3)
        st_b = A(len(REALCH), 6)
        mv_b = A(2)
        sd_b, scale, shift = A(1), A(1), A(1)
        st_n = A(NB, 6)
        mv_n = A(NB, 2)
        sd_n = A(NB)
        attn = A(2, REL * D)
        fold = A(REL * D)
        w_att = A(2 * RH)
        ed = A(NB, RH)
        tab = [A(REL, HS) for _ in range(2)]
        ps = m.psum
        wt, col = m.wt, m.cols

        def c(name):
            k = COLUMNS.index(name)
            return col[:, k:k + 1]

        def w(name):
            return wt[:, TRANSPOSED.index(name), :]

        tabs_in = [sem(f"table_landed{j}") for j in range(TABS)]
        attn_in = sem("attention_landed")
        vec = sem("vector_steps")
        agg_made = sem("agg_made")
        agg_t, agg_k = sem("agg_turned"), sem("agg_kept")
        u_sum, u_made = sem("u_summed"), sem("u_made")
        r_sum, r_made, rx_made = sem("r_summed"), sem("r_made"), sem("rx_made")
        f_sum, f_made, o_made = sem("f_summed"), sem("f_made"), sem("o_made")
        var1, root1, scale1 = sem("variance1"), sem("root1"), sem("scale1")
        h_made = sem("h_made")
        g_sum, g_made = sem("g_summed"), sem("g_made")
        var2, root2, scale2 = sem("variance2"), sem("root2"), sem("scale2")
        h2_made = sem("h2_made")
        y_sum, y_made = sem("y_summed"), sem("y_made")
        varn, rootn, x_made = sem("node_variance"), sem("node_root"), sem("x_made")
        x_t, x_k = sem("x_turned2"), sem("x_kept2")
        att_made = sem("attention_folded")
        tab_sum, tab_h, tab_e = sem("table_summed"), sem("table_features"), sem("table_scores")
        ed_made = sem("dst_scores")
        stored = [sem(f"table_stored{k}") for k in range(2)]
        ed_stored, scattered = sem("dst_scores_stored"), sem("dst_scores_scattered")
        NCH = len(CHUNKS)

        with nc.Block() as block:

            @block.sync
            def _(eng):
                for j in range(TABS):
                    eng.dma_start(agg[j], m.tabs[j][0:NP, :].rearrange("(b p) f -> p b f", p=P)).then_inc(tabs_in[j], 16)
                for k, name in enumerate(("L1_gnn_attn_src", "L1_gnn_attn_dst")):
                    eng.dma_start(attn[:, k, :], I[name].rearrange("r h d -> (r h d)").partition_broadcast(P)).then_inc(attn_in, 16)
                for b in range(NB):
                    eng.wait_ge(tab_h, b + 1)
                    eng.wait_ge(tab_e, b + 1)
                    eng.dma_start(m.table1.rearrange("(b p r) f -> b p r f", p=P, r=REL)[b], tab[b % 2]).then_inc(stored[b % 2], 16)
                eng.wait_ge(ed_made, NB)
                eng.dma_start(m.dst1.rearrange("(b p) f -> p b f", p=P), ed).then_inc(ed_stored, 16)
                eng.wait_ge(ed_stored, 16)
                for k in range(2):
                    eng.wait_ge(stored[k], 16 * len(range(k, NB, 2)))

            @block.gpsimd
            def _(eng):
                eng.wait_ge(ed_made, NB)
                for b in range(NB):
                    eng.indirect_dma_start(out=m.seg_dst, out_offset=bass.IndirectOffsetOnAxis(ap=m.start[:, b:b + 1], axis=0),
                                           in_=ed[:, b, :], in_offset=None).then_inc(scattered, 16)
                eng.wait_ge(scattered, 16 * NB)

            @block.tensor
            def _(eng):
                def pair(bank, cw, first, x1, second, x2):
                    k, (at, n) = cw
                    eng.matmul(ps[:, bank + k % 2, 0:n], first, x1[:, at:at + n], start=True, stop=False)
                    return eng.matmul(ps[:, bank + k % 2, 0:n], second, x2[:, at:at + n], start=False, stop=True)

                eng.wait_ge(agg_made, 1)
                turn_out(eng, ps, agg[0], agg_t, agg_k, m.ident[:, :], 0)
                for k, cw in enumerate(CHUNKS):
                    eng.wait_ge(agg_k, k + 1)
                    if k >= 2:
                        eng.wait_ge(u_made, k - 1)
                        eng.wait_ge(r_made, k - 1)
                    pair(2, (k, cw), w("L0_gnn_W1w"), aggT, w("L0_gnn_U1w"), m.xT).then_inc(u_sum, 1)
                    pair(4, (k, cw), w("L0_gnn_W2w"), aggT, w("L0_gnn_U2w"), m.xT).then_inc(r_sum, 1)
                for k, cw in enumerate(CHUNKS):
                    eng.wait_ge(rx_made, k + 1)
                    if k >= 2:
                        eng.wait_ge(f_made, k - 1)
                    pair(6, (k, cw), w("L0_gnn_W3w"), aggT, w("L0_gnn_U3w"), rT).then_inc(f_sum, 1)
                eng.wait_ge(agg_k, NCH)
                for k, (at, n) in enumerate(CHUNKS):
                    eng.wait_ge(h_made, k + 1)
                    if k >= 2:
                        eng.wait_ge(g_made, k - 1)
                    eng.matmul(ps[:, k % 2, 0:n], w("L0_gnn_m_w0"), hT[:, at:at + n], start=True, stop=True).then_inc(g_sum, 1)
                eng.wait_ge(u_made, NCH)
                for k, (at, n) in enumerate(CHUNKS):
                    eng.wait_ge(h2_made, k + 1)
                    if k >= 2:
                        eng.wait_ge(y_made, k - 1)
                    for b in range(n // P):
                        t = eng.matmul(ps[:, 2 + k % 2, b * P:b * P + P], h2T[:, at + b * P:at + b * P + P], w("L0_gnn_m_w1"), start=True, stop=True)
                    t.then_inc(y_sum, 1)
                eng.wait_ge(x_made, 1)
                eng.wait_ge(g_made, NCH)
                turn_out(eng, ps, m.xN, x_t, x_k, m.ident[:, :], 0)
                eng.wait_ge(att_made, 1)
                eng.wait_ge(r_made, NCH)
                eng.wait_ge(f_made, NCH)
                for b in range(NB):
                    eng.wait_ge(x_k, b // 4 + 1)
                    if b >= 2:
                        eng.wait_ge(tab_h, b - 1)
                        eng.wait_ge(ed_made, b - 1)
                    xb = m.xT[:, b * P:b * P + P]
                    eng.matmul(ps[:, 4 + b % 2, :], xb, m.w_rel[:, :, :].rearrange("p r f -> p (r f)"), start=True, stop=True)
                    eng.matmul(ps[:, 6 + b % 2, 0:2 * RH], xb, w_att, start=True, stop=True).then_inc(tab_sum, 1)

            @block.scalar
            def _(eng):
                turn_in(eng, ps, aggT, agg_t, agg_k, 0)
                eng.wait_ge(vec, 3)
                for k, (at, n) in enumerate(CHUNKS):
                    eng.wait_ge(u_sum, k + 1)
                    eng.activation(uT[:, at:at + n], ps[:, 2 + k % 2, 0:n], ACT.Relu, bias=bias[:, 0:1]).then_inc(u_made, 1)
                    eng.wait_ge(r_sum, k + 1)
                    eng.activation(rT[:, at:at + n], ps[:, 4 + k % 2, 0:n], ACT.Relu, bias=bias[:, 1:2]).then_inc(r_made, 1)
                for k, (at, n) in enumerate(CHUNKS):
                    eng.wait_ge(f_sum, k + 1)
                    eng.activation(fT[:, at:at + n], ps[:, 6 + k % 2, 0:n], ACT.Tanh, bias=bias[:, 2:3]).then_inc(f_made, 1)
                eng.wait_ge(var1, 1)
                eng.activation(sd_b, mv_b[:, 1:2], ACT.Sqrt, bias=m.eps[:, 0:1]).then_inc(root1, 1)
                eng.wait_ge(scale1, 1)
                for k, (at, n) in enumerate(CHUNKS):
                    eng.activation(hT[:, at:at + n], oT[:, at:at + n], ACT.Relu, bias=shift, scale=scale).then_inc(h_made, 1)
                for k, (at, n) in enumerate(CHUNKS):
                    eng.wait_ge(g_sum, k + 1)
                    eng.activation(gT[:, at:at + n], ps[:, k % 2, 0:n], ACT.Identity, bias=c("L0_gnn_m_b0")).then_inc(g_made, 1)
                eng.wait_ge(var2, 1)
                eng.activation(sd_b, mv_b[:, 1:2], ACT.Sqrt, bias=m.eps[:, 0:1]).then_inc(root2, 1)
                eng.wait_ge(scale2, 1)
                for k, (at, n) in enumerate(CHUNKS):
                    eng.activation(h2T[:, at:at + n], gT[:, at:at + n], ACT.Relu, bias=shift, scale=scale).then_inc(h2_made, 1)
                eng.wait_ge(varn, 1)
                eng.activation(sd_n, mv_n[:, :, 1], ACT.Sqrt, bias=m.eps[:, 0:1]).then_inc(rootn, 1)
                turn_in(eng, ps, m.xT, x_t, x_k, 0)
                for b in range(NB):
                    eng.wait_ge(tab_sum, b + 1)
                    if b >= 2:
                        eng.wait_ge(stored[b % 2], 16 * (b // 2))
                    eng.activation(tab[b % 2][:, :, 0:D], ps[:, 4 + b % 2, :].rearrange("p (r f) -> p r f", f=D), ACT.Copy).then_inc(tab_h, 1)

            @block.vector
            def _(eng):
                v = Steps(eng, vec)
                for k, (a, b) in enumerate((("W1b", "U1b"), ("W2b", "U2b"), ("W3b", "U3b"))):
                    v.put(eng.tensor_tensor(bias[:, k:k + 1], c("L0_gnn_" + a), c("L0_gnn_" + b), ALU.add))
                eng.wait_ge(attn_in, 32)
                for k in range(2):
                    v.then(eng.tensor_tensor(fold, m.w_rel[:, :, :].rearrange("p r f -> p (r f)"), attn[:, k, :], ALU.mult))
                    v.then(eng.tensor_reduce(w_att[:, k * RH:(k + 1) * RH], fold.rearrange("p (a d) -> p a d", d=D1), AX.X, ALU.add))
                eng.engine_nop().then_inc(att_made, 1)
                for j in range(TABS):
                    eng.wait_ge(tabs_in[j], 16)
                    if j:
                        v.then(eng.tensor_tensor(agg[0], agg[0], agg[j], ALU.add))
                eng.engine_nop().then_inc(agg_made, 1)
                for k, (at, n) in enumerate(CHUNKS):
                    eng.wait_ge(r_made, k + 1)
                    eng.tensor_tensor(rT[:, at:at + n], rT[:, at:at + n], m.xT[:, at:at + n], ALU.mult).then_inc(rx_made, 1)
                for k, (at, n) in enumerate(CHUNKS):
                    f, o, x, u = (t[:, at:at + n] for t in (fT, oT, m.xT, uT))
                    eng.wait_ge(f_made, k + 1)
                    v.then(eng.tensor_tensor(f, f, x, ALU.subtract))
                    v.then(eng.tensor_tensor(f, f, u, ALU.mult))
                    eng.tensor_tensor(o, f, x, ALU.add).then_inc(o_made, 1)
                v.then(eng.tensor_tensor(m.xN[:, :, :], m.xN[:, :, :], spread(m.rows[:, ROWS.index("L0_gnn_m_b1"), :], 1, [P, NB, D]), ALU.add))
                for made, var, root, scaled, x, g, b in ((o_made, var1, root1, scale1, oT, "L0_gnn_bn_g", "L0_gnn_bn_b"),
                                                         (g_made, var2, root2, scale2, gT, "L0_gnn_m_bng", "L0_gnn_m_bnb")):
                    for k, (at, n) in enumerate(REALCH):
                        eng.wait_ge(made, k + 1)
                        v.put(eng.bn_stats(st_b[:, k, :], x[:, at:at + n]))
                    v.wait()
                    eng.bn_aggr(mv_b, st_b).then_inc(var, 1)
                    eng.wait_ge(root, 1)
                    v.then(eng.reciprocal(sd_b, sd_b))
                    v.then(eng.tensor_tensor(scale, sd_b, c(g), ALU.mult))
                    v.then(eng.tensor_tensor(sd_b, mv_b[:, 0:1], scale, ALU.mult))
                    eng.tensor_tensor(shift, c(b), sd_b, ALU.subtract).then_inc(scaled, 1)
                    eng.wait_ge(scaled, 1)
                for k, (at, n) in enumerate(CHUNKS):
                    eng.wait_ge(y_sum, k + 1)
                    b0, b1 = at // P, (at + n) // P
                    eng.tensor_tensor(y[:, b0:b1, :], ps[:, 2 + k % 2, 0:n].rearrange("p (b f) -> p b f", f=D), m.xN[:, b0:b1, :], ALU.add).then_inc(y_made, 1)
                eng.wait_ge(y_made, NCH)
                for b in range(NB):
                    v.put(eng.bn_stats(st_n[:, b, :], y[:, b, :]))
                v.wait()
                for b in range(NB):
                    v.put(eng.bn_aggr(mv_n[:, b, :], st_n[:, b, :]))
                v.wait()
                eng.engine_nop().then_inc(varn, 1)
                eng.wait_ge(rootn, 1)
                v.then(eng.reciprocal(sd_n, sd_n))
                for b in range(NB):
                    v.put(eng.tensor_scalar(m.xN[:, b, :], y[:, b, :], mv_n[:, b, 0:1], sd_n[:, b:b + 1], ALU.subtract, ALU.mult))
                v.wait()
                eng.engine_nop().then_inc(x_made, 1)
                for b in range(NB):
                    eng.wait_ge(tab_sum, b + 1)
                    if b >= 2:
                        eng.wait_ge(stored[b % 2], 16 * (b // 2))
                    sc = ps[:, 6 + b % 2, 0:2 * RH]
                    eng.tensor_copy(tab[b % 2][:, :, D:HS], sc[:, 0:RH].rearrange("p (r h) -> p r h", h=H1)).then_inc(tab_e, 1)
                    eng.tensor_copy(ed[:, b, :], sc[:, RH:2 * RH]).then_inc(ed_made, 1)


class TurnSteps(Steps):

    def __init__(self, eng, sem, i, per_turn, start=0):
        Steps.__init__(self, eng, sem, start)
        self.i, self.per_turn = i, per_turn

    def wait(self):
        self.eng.wait_ge(self.sem, self.i * self.per_turn + self.n)


SCORE1 = 3 + HALF + (HALF - 1) + 2
TAKEN1 = SCORE1 + REL
STEPS1 = TAKEN1 + 3 + (HALF - 1)
PER_TURN1 = 2 * STEPS1 + 2


def layer1_edges(nc, m, I):
    with phase(nc, "layer1_edges") as sem:
        A = Arena(m)
        ed = A(T, RH)
        feat = [A(HALF, HS) for _ in range(2)]
        rows = [A(HALF, R1) for _ in range(2)]
        e = A(HALF, RH)
        gap, fade = A(RH), A(RH)
        old = A(REL * D + RH)
        keeps, resets = A(BODY), A(BODY)
        idx = [A(HALF, dt=I32) for _ in range(2)]
        ed_first = A(RH)
        SUM, MAX = REL * D, REL * D + RH

        ed_in, ed_first_in = sem("dst_scores_landed"), sem("first_scores_landed")
        filled = sem("dst_scores_filled")
        steps = sem("edge_steps")
        exped = sem("exponentials")
        staged = [sem(f"indices_staged{h}") for h in range(2)]
        landed = [sem(f"features_landed{h}") for h in range(2)]
        free = [sem(f"features_used{h}") for h in range(2)]
        stored = [sem(f"states_stored{h}") for h in range(2)]
        rows_free = [sem(f"states_free{h}") for h in range(2)]

        with nc.Block() as block:

            @block.sync
            def _(eng):
                eng.dma_start(ed.rearrange("p t f -> p (t f)"), lanes(m.seg_dst).rearrange("p t f -> p (t f)")).then_inc(ed_in, 16)
                with eng.Fori(0, TURNS) as i:
                    for h in range(2):
                        hold(eng, steps, i * PER_TURN1 + 3 + (h + 1) * STEPS1)
                        eng.dma_start(lanes(m.rows1)[:, bass.ds(i * BODY + h * HALF, HALF), :], rows[h]).then_inc(stored[h], 16)
                        hold(eng, stored[h], 16 * i + 16)
                        eng.nop().then_inc(rows_free[h], 1)

            @block.gpsimd
            def _(eng):
                eng.indirect_dma_start(out=ed_first, out_offset=None, in_=m.dst1,
                                       in_offset=bass.IndirectOffsetOnAxis(ap=m.lane_first[:, 0:1], axis=0)).then_inc(ed_first_in, 16)
                with eng.Fori(0, TURNS) as i:
                    for h in range(2):
                        hold(eng, staged[h], i + 1)
                        hold(eng, free[h], i + 1)
                        for j in range(HALF):
                            eng.indirect_dma_start(out=feat[h][:, j, :], out_offset=None, in_=m.table1,
                                                   in_offset=bass.IndirectOffsetOnAxis(ap=idx[h][:, j:j + 1], axis=0)).then_inc(landed[h], 16)

            @block.scalar
            def _(eng):
                for h in range(2):
                    eng.activation(idx[h], m.src_rel[:, h * HALF:(h + 1) * HALF], ACT.Copy).then_inc(staged[h], 1)
                with eng.Fori(0, TURNS) as i:
                    for h in range(2):
                        hold(eng, landed[h], 16 * HALF * (i + 1))
                        eng.activation(idx[h], m.src_rel[:, bass.ds(i * BODY + BODY + h * HALF, HALF)], ACT.Copy).then_inc(staged[h], 1)
                        eng.wait_ge(steps, i * PER_TURN1 + 3 + h * STEPS1 + SCORE1)
                        eng.activation(rows[h][:, :, SUM:MAX], e, ACT.Exp).then_inc(exped, 1)
                        eng.activation(fade, gap, ACT.Exp).then_inc(exped, 1)

            @block.vector
            def _(eng):
                for h in range(2):
                    eng.engine_nop().then_inc(free[h], 1)
                    eng.engine_nop().then_inc(rows_free[h], 1)
                f = Steps(eng, filled)
                f.put(eng.memset(rows[1][:, HALF - 1, 0:MAX], 0.0))
                f.put(eng.memset(rows[1][:, HALF - 1, MAX:R1], -BIG))
                eng.wait_ge(ed_in, 16)
                eng.wait_ge(ed_first_in, 16)
                for k in range(RH):
                    f.put(eng.tensor_tensor_scan(ed[:, :, k], m.keep[:, :], ed[:, :, k], ed_first[:, k:k + 1], ALU.mult, ALU.add))
                f.wait()
                eng.engine_nop().then_inc(steps, 1)
                with eng.Fori(0, TURNS) as i:
                    v = TurnSteps(eng, steps, i, PER_TURN1, start=1)
                    eng.wait_ge(steps, i * PER_TURN1 + 1)
                    eng.nop(nofuse=True)
                    v.put(eng.tensor_copy(keeps, m.keep[:, bass.ds(i * BODY, BODY)]))
                    v.put(eng.tensor_copy(resets, m.reset[:, bass.ds(i * BODY, BODY)]))
                    for h in range(2):
                        here = bass.ds(i * BODY + h * HALF, HALF)
                        row, before = rows[h], rows[1 - h][:, HALF - 1, :]
                        top = row[:, :, MAX:R1]
                        e4 = e.rearrange("p t (r a) -> p t r a", a=H1)
                        eng.wait_ge(landed[h], 16 * HALF * (i + 1))
                        v.then(eng.tensor_tensor(e4, spread(feat[h][:, :, D:HS], 2, [P, HALF, REL, H1]),
                                                 ed[:, here, :].rearrange("p t (r a) -> p t r a", a=H1), ALU.add))
                        v.then(eng.scalar_tensor_tensor(out=e, in0=e, scalar=0.2, in1=e, op0=ALU.mult, op1=ALU.max))
                        v.then(eng.tensor_tensor(e4, e4, spread(m.other_rel[:, here, :], 3, [P, HALF, REL, H1]), ALU.add))
                        eng.wait_ge(rows_free[h], i + 1)
                        for j in range(HALF):
                            s = h * HALF + j
                            v.then(eng.scalar_tensor_tensor(out=top[:, j, :], in0=top[:, j - 1, :] if j else before[:, MAX:R1],
                                                            scalar=resets[:, s:s + 1], in1=e[:, j, :], op0=ALU.add, op1=ALU.max))
                        for j in range(HALF - 2, -1, -1):
                            s = h * HALF + j + 1
                            v.then(eng.scalar_tensor_tensor(out=top[:, j, :], in0=top[:, j + 1, :], scalar=resets[:, s:s + 1],
                                                            in1=top[:, j, :], op0=ALU.add, op1=ALU.max))
                        v.put(eng.tensor_tensor(e, e, top, ALU.subtract))
                        v.put(eng.scalar_tensor_tensor(out=gap, in0=before[:, MAX:R1], scalar=resets[:, h * HALF:h * HALF + 1],
                                                       in1=top[:, 0, :], op0=ALU.add, op1=ALU.subtract))
                        assert v.n == 3 + h * STEPS1 + SCORE1
                        eng.wait_ge(exped, 4 * i + 2 * h + 2)
                        for r in range(REL):
                            v.put(eng.tensor_tensor(row[:, :, r * D:(r + 1) * D].rearrange("p t (a d) -> p t a d", d=D1),
                                                    feat[h][:, :, 0:D].rearrange("p t (a d) -> p t a d", d=D1),
                                                    spread(row[:, :, SUM + r * H1:SUM + (r + 1) * H1], 3, [P, HALF, H1, D1]), ALU.mult))
                        v.put(eng.tensor_tensor(old[:, 0:SUM].rearrange("p (a d) -> p a d", d=D1), before[:, 0:SUM].rearrange("p (a d) -> p a d", d=D1),
                                                spread(fade, 2, [P, RH, D1]), ALU.mult))
                        v.then(eng.tensor_tensor(old[:, SUM:MAX], before[:, SUM:MAX], fade, ALU.mult))
                        eng.nop(nofuse=True).then_inc(free[h], 1)
                        v.then(eng.tensor_tensor(row[:, 0, 0:MAX], row[:, 0, 0:MAX], old, ALU.add))
                        for j in range(1, HALF):
                            s = h * HALF + j
                            v.then(eng.scalar_tensor_tensor(out=row[:, j, 0:MAX], in0=row[:, j - 1, 0:MAX], scalar=keeps[:, s:s + 1],
                                                            in1=row[:, j, 0:MAX], op0=ALU.mult, op1=ALU.add))
                        assert v.n == 3 + (h + 1) * STEPS1
                eng.wait_ge(steps, TURNS * PER_TURN1 + 1)
                f.then(eng.tensor_copy(m.lane_end[:, 0:R1], rows[1][:, HALF - 1, :]))


def carry_sums(nc, m, states, chunks, heads):
    with phase(nc, f"carry_sums_{heads}") as sem:
        A = Arena(m)
        W, C, H, DH = chunks * P, chunks, heads, P // heads
        R = W + 2 * C * H
        wide = [A(3, P) for _ in range(C)]
        run = [A(3, P + 1) for _ in range(C)]
        ex = [A(2, P) for _ in range(C)]
        add = [A(2, P) for _ in range(C)]
        row = A(R)
        new_max = A(C * H)
        dm = A(2, C * H)
        part = A(W + C * H)
        ps = m.psum

        row_in, fixed = sem("first_rows_landed"), sem("first_rows_fixed")
        vec = sem("vector_steps")
        wide_made, turned = sem("states_spread"), sem("states_turned")
        exps_of, exped = sem("exponents"), sem("exponentials")
        run_made, back = sem("lanes_summed"), sem("lane_sums_turned")
        merge_of, merge_exp = sem("merge_exponents"), sem("merge_exponentials")
        merged = sem("rows_merged")

        def head(k, t):
            return t.rearrange("p (a d) -> p a d", d=DH)[:, :, 0]

        with nc.Block() as block:

            @block.gpsimd
            def _(eng):
                eng.indirect_dma_start(out=row, out_offset=None, in_=states,
                                       in_offset=bass.IndirectOffsetOnAxis(ap=m.first_end[:, 0:1], axis=0)).then_inc(row_in, 16)
                eng.wait_ge(merged, 1)
                eng.indirect_dma_start(out=states, out_offset=bass.IndirectOffsetOnAxis(ap=m.first_fix[:, 0:1], axis=0),
                                       in_=row, in_offset=None).then_inc(fixed, 16)
                eng.wait_ge(fixed, 16)

            @block.tensor
            def _(eng):
                for c in range(C):
                    eng.wait_ge(wide_made, c + 1)
                    for k in range(3):
                        t = eng.transpose(ps[:, c, k * P:(k + 1) * P], wide[c][:, k, :], m.ident[:, :])
                    t.then_inc(turned, 1)
                for c in range(C):
                    eng.wait_ge(run_made, c + 1)
                    for k in range(3):
                        t = eng.transpose(ps[:, 4 + c, k * P:(k + 1) * P], run[c][:, k, 0:P], m.ident[:, :])
                    t.then_inc(back, 1)

            @block.scalar
            def _(eng):
                for c in range(C):
                    eng.wait_ge(exps_of, c + 1)
                    eng.activation(ex[c], ex[c], ACT.Exp).then_inc(exped, 1)
                eng.wait_ge(merge_of, 1)
                eng.activation(dm, dm, ACT.Exp).then_inc(merge_exp, 1)

            @block.vector
            def _(eng):
                v = Steps(eng, vec)
                end = m.lane_end
                for c in range(C):
                    v.put(eng.tensor_copy(wide[c][:, 0, :], end[:, c * P:(c + 1) * P]))
                    for k in range(2):
                        at = W + k * C * H + c * H
                        v.put(eng.tensor_copy(wide[c][:, 1 + k, :].rearrange("p (a d) -> p a d", d=DH), spread(end[:, at:at + H], 2, [P, H, DH])))
                    v.put(eng.memset(run[c][:, 0:2, 0:1], 0.0))
                    v.put(eng.memset(run[c][:, 2, 0:1], -BIG))
                    v.wait()
                    eng.engine_nop().then_inc(wide_made, 1)
                for c in range(C):
                    eng.wait_ge(turned, c + 1)
                    v.then(eng.tensor_tensor_scan(run[c][:, 2, 1:P + 1], m.whole_neg[:, :], ps[:, c, 2 * P:3 * P], -BIG, ALU.add, ALU.max))
                    v.put(eng.tensor_tensor(ex[c][:, 1, :], ps[:, c, 2 * P:3 * P], run[c][:, 2, 1:P + 1], ALU.subtract))
                    v.then(eng.tensor_tensor(ex[c][:, 0, :], run[c][:, 2, 0:P], m.whole_neg[:, :], ALU.add))
                    v.then(eng.tensor_tensor(ex[c][:, 0, :], ex[c][:, 0, :], run[c][:, 2, 1:P + 1], ALU.subtract))
                    eng.engine_nop().then_inc(exps_of, 1)
                for c in range(C):
                    eng.wait_ge(exped, c + 1)
                    for k in range(2):
                        v.put(eng.tensor_tensor(add[c][:, k, :], ps[:, c, k * P:(k + 1) * P], ex[c][:, 1, :], ALU.mult))
                    v.wait()
                    for k in range(2):
                        v.put(eng.tensor_tensor_scan(run[c][:, k, 1:P + 1], ex[c][:, 0, :], add[c][:, k, :], 0.0, ALU.mult, ALU.add))
                    v.wait()
                    eng.engine_nop().then_inc(run_made, 1)
                eng.wait_ge(row_in, 16)
                for c in range(C):
                    eng.wait_ge(back, c + 1)
                    v.put(eng.tensor_tensor(new_max[:, c * H:(c + 1) * H], row[:, W + C * H + c * H:W + C * H + (c + 1) * H],
                                            head(c, ps[:, 4 + c, 2 * P:3 * P]), ALU.max))
                v.wait()
                v.put(eng.tensor_tensor(dm[:, 0, :], row[:, W + C * H:R], new_max, ALU.subtract))
                for c in range(C):
                    v.put(eng.tensor_tensor(dm[:, 1, c * H:(c + 1) * H], head(c, ps[:, 4 + c, 2 * P:3 * P]), new_max[:, c * H:(c + 1) * H], ALU.subtract))
                v.wait()
                eng.engine_nop().then_inc(merge_of, 1)
                eng.wait_ge(merge_exp, 1)
                v.put(eng.tensor_tensor(row[:, 0:W].rearrange("p (a d) -> p a d", d=DH), row[:, 0:W].rearrange("p (a d) -> p a d", d=DH),
                                        spread(dm[:, 0, :], 2, [P, C * H, DH]), ALU.mult))
                v.put(eng.tensor_tensor(row[:, W:W + C * H], row[:, W:W + C * H], dm[:, 0, :], ALU.mult))
                for c in range(C):
                    v.put(eng.tensor_tensor(part[:, c * P:(c + 1) * P].rearrange("p (a d) -> p a d", d=DH),
                                            ps[:, 4 + c, 0:P].rearrange("p (a d) -> p a d", d=DH),
                                            spread(dm[:, 1, c * H:(c + 1) * H], 2, [P, H, DH]), ALU.mult))
                    v.put(eng.tensor_tensor(part[:, W + c * H:W + (c + 1) * H], head(c, ps[:, 4 + c, P:2 * P]), dm[:, 1, c * H:(c + 1) * H], ALU.mult))
                v.wait()
                v.put(eng.tensor_tensor(row[:, 0:W + C * H], row[:, 0:W + C * H], part, ALU.add))
                v.put(eng.tensor_copy(row[:, W + C * H:R], new_max))
                v.wait()
                eng.engine_nop().then_inc(merged, 1)


def layer1_nodes(nc, m, I):
    with phase(nc, "layer1_nodes") as sem:
        A = Arena(m)
        SUM, MAX = REL * D, REL * D + RH
        st = A(NB, R1)
        fac = A(NB, RH)
        den = A(NB, RH)
        y = A(NB, D)
        st_n = A(NB, 6)
        mv_n = A(NB, 2)
        sd_n = A(NB)
        q2 = A(NB, D)
        kv = [A(2, D) for _ in range(2)]
        ps = m.psum

        def r(name):
            return m.rows[:, ROWS.index(name), :]

        def w(name):
            return m.wt[:, TRANSPOSED.index(name), :]

        state_in = sem("states_landed")
        vec = sem("vector_steps")
        expo, exped = sem("exponents"), sem("exponentials")
        varn, rootn = sem("node_variance"), sem("node_root")
        x_made = sem("x_made")
        x_t, x_k = sem("x_turned"), sem("x_kept")
        qkv_sum, q_made, kv_made = sem("qkv_summed"), sem("queries_made"), sem("keys_values_made")
        stored = [sem(f"keys_values_stored{k}") for k in range(2)]
        q_stored, scattered = sem("queries_stored"), sem("queries_scattered")

        with nc.Block() as block:

            @block.gpsimd
            def _(eng):
                for b in range(NB):
                    eng.indirect_dma_start(out=st[:, b, :], out_offset=None, in_=m.rows1,
                                           in_offset=bass.IndirectOffsetOnAxis(ap=m.end[:, b:b + 1], axis=0)).then_inc(state_in, 16)
                eng.wait_ge(q_made, NB)
                for b in range(NB):
                    eng.indirect_dma_start(out=m.seg_rows, out_offset=bass.IndirectOffsetOnAxis(ap=m.start[:, b:b + 1], axis=0),
                                           in_=q2[:, b, :], in_offset=None).then_inc(scattered, 16)
                eng.wait_ge(scattered, 16 * NB)

            @block.sync
            def _(eng):
                for b in range(NB):
                    eng.wait_ge(kv_made, b + 1)
                    eng.dma_start(m.table2.rearrange("(b p) f -> b p f", p=P)[b], kv[b % 2].rearrange("p a f -> p (a f)")).then_inc(stored[b % 2], 16)
                eng.wait_ge(q_made, NB)
                eng.dma_start(m.query2.rearrange("(b p) f -> p b f", p=P), q2[:, :, :]).then_inc(q_stored, 16)
                eng.wait_ge(q_stored, 16)
                for k in range(2):
                    eng.wait_ge(stored[k], 16 * len(range(k, NB, 2)))

            @block.tensor
            def _(eng):
                eng.wait_ge(x_made, 1)
                turn_out(eng, ps, m.xN, x_t, x_k, m.ident[:, :], 0)
                for b in range(NB):
                    eng.wait_ge(x_k, b // 4 + 1)
                    if b >= 2:
                        eng.wait_ge(q_made, b - 1)
                        eng.wait_ge(kv_made, b - 1)
                    xb = m.xT[:, b * P:b * P + P]
                    for k, name in enumerate(("L2_gnn_q_w", "L2_gnn_k_w", "L2_gnn_v_w")):
                        bank = 2 + b % 2 + 2 * (k > 0)
                        t = eng.matmul(ps[:, bank, k * P:(k + 1) * P], xb, w(name), start=True, stop=True)
                    t.then_inc(qkv_sum, 1)

            @block.scalar
            def _(eng):
                eng.wait_ge(expo, 1)
                eng.activation(fac, fac, ACT.Exp).then_inc(exped, 1)
                for n in range(2):
                    eng.wait_ge(varn, n + 1)
                    eng.activation(sd_n, mv_n[:, :, 1], ACT.Sqrt, bias=m.eps[:, 0:1]).then_inc(rootn, 1)
                turn_in(eng, ps, m.xT, x_t, x_k, 0)
                for b in range(NB):
                    eng.wait_ge(qkv_sum, b + 1)
                    if b >= 2:
                        eng.wait_ge(stored[b % 2], 16 * (b // 2))
                    eng.activation(kv[b % 2].rearrange("p a f -> p (a f)"), ps[:, 4 + b % 2, P:3 * P], ACT.Copy).then_inc(kv_made, 1)

            @block.vector
            def _(eng):
                v = Steps(eng, vec)
                eng.wait_ge(state_in, 16 * NB)
                v.then(eng.tensor_scalar(fac, st[:, :, MAX:R1], 0.0, None, ALU.min))
                eng.engine_nop().then_inc(expo, 1)
                eng.wait_ge(exped, 1)
                v.then(eng.tensor_tensor(den, st[:, :, SUM:MAX], fac, ALU.mult))
                v.then(eng.tensor_scalar(den, den, 1e-8, None, ALU.add))
                v.then(eng.reciprocal(den, den))
                v.then(eng.tensor_tensor(fac, fac, den, ALU.mult))
                acc = st[:, :, 0:SUM]
                v.then(eng.tensor_tensor(acc.rearrange("p b (a d) -> p b a d", d=D1), acc.rearrange("p b (a d) -> p b a d", d=D1),
                                         spread(fac, 3, [P, NB, RH, D1]), ALU.mult))
                v.then(eng.tensor_tensor(y, st[:, :, 0:D], st[:, :, D:2 * D], ALU.add))
                for k in range(2, REL):
                    v.then(eng.tensor_tensor(y, y, st[:, :, k * D:(k + 1) * D], ALU.add))
                v.then(eng.tensor_tensor(y, y, spread(r("L1_gnn_bias"), 1, [P, NB, D]), ALU.add))
                v.then(eng.tensor_tensor(y, y, m.xN[:, :, :], ALU.add))
                for n in range(2):
                    for b in range(NB):
                        v.put(eng.bn_stats(st_n[:, b, :], y[:, b, :]))
                    v.wait()
                    for b in range(NB):
                        v.put(eng.bn_aggr(mv_n[:, b, :], st_n[:, b, :]))
                    v.wait()
                    eng.engine_nop().then_inc(varn, 1)
                    eng.wait_ge(rootn, n + 1)
                    v.then(eng.reciprocal(sd_n, sd_n))
                    to = y if n == 0 else m.xN
                    for b in range(NB):
                        v.put(eng.tensor_scalar(to[:, b, :], y[:, b, :], mv_n[:, b, 0:1], sd_n[:, b:b + 1], ALU.subtract, ALU.mult))
                    v.wait()
                    if n == 0:
                        v.then(eng.tensor_tensor(y, y, spread(r("L1_gnn_ln_gamma"), 1, [P, NB, D]), ALU.mult))
                        v.then(eng.tensor_tensor(y, y, spread(r("L1_gnn_ln_beta"), 1, [P, NB, D]), ALU.add))
                        v.then(eng.tensor_tensor(y, y, m.xN[:, :, :], ALU.add))
                eng.engine_nop().then_inc(x_made, 1)
                for b in range(NB):
                    eng.wait_ge(qkv_sum, b + 1)
                    v.then(eng.tensor_tensor(q2[:, b, :], ps[:, 2 + b % 2, 0:P], r("L2_gnn_q_b"), ALU.add))
                    v.then(eng.tensor_scalar(q2[:, b, :], q2[:, b, :], float(D2) ** -0.5, None, ALU.mult))
                    eng.engine_nop().then_inc(q_made, 1)


SCORE2 = HALF + 2 + HALF + (HALF - 1) + 2
STEPS2 = SCORE2 + 1 + 3 + (HALF - 1)
PER_TURN2 = 2 * STEPS2 + 2


def layer2_edges(nc, m, I):
    with phase(nc, "layer2_edges") as sem:
        A = Arena(m)
        kv = [A(HALF, 2 * D) for _ in range(2)]
        q = [A(HALF, D) for _ in range(2)]
        rows = [A(HALF, R2) for _ in range(2)]
        prod = A(HALF, D)
        e = A(HALF, H2)
        gap, fade = A(H2), A(H2)
        old = A(D + H2)
        keeps, resets = A(BODY), A(BODY)
        idx = [A(HALF, dt=I32) for _ in range(2)]
        SUM, MAX = D, D + H2

        q_first = sem("first_queries_landed")
        q_in = [sem(f"queries_landed{h}") for h in range(2)]
        begun = sem("states_begun")
        steps = sem("edge_steps")
        exped = sem("exponentials")
        staged = [sem(f"indices_staged{h}") for h in range(2)]
        landed = [sem(f"keys_values_landed{h}") for h in range(2)]
        free = [sem(f"keys_values_used{h}") for h in range(2)]
        stored = [sem(f"states_stored{h}") for h in range(2)]
        rows_free = [sem(f"states_free{h}") for h in range(2)]

        def at(i, h, n):
            return i * PER_TURN2 + 3 + h * STEPS2 + n

        with nc.Block() as block:

            @block.sync
            def _(eng):
                def load(h, t):
                    eng.dma_start(q[h], lanes(m.seg_rows)[:, t, :]).then_inc(q_in[h], 16)

                def store(i, h):
                    hold(eng, steps, at(i, h, STEPS2))
                    eng.dma_start(lanes(m.rows2)[:, bass.ds(i * BODY + h * HALF, HALF), :], rows[h]).then_inc(stored[h], 16)

                def ended(i, h):
                    hold(eng, stored[h], 16 * i + 16)
                    eng.nop().then_inc(rows_free[h], 1)

                load(0, bass.ds(0, HALF))
                with eng.Fori(0, TURNS - 1) as i:
                    hold(eng, steps, at(i, 0, 1))
                    load(1, bass.ds(i * BODY + HALF, HALF))
                    store(i, 0)
                    ended(i, 0)
                    hold(eng, steps, at(i, 1, 1))
                    load(0, bass.ds(i * BODY + BODY, HALF))
                    store(i, 1)
                    ended(i, 1)
                i = TURNS - 1
                eng.wait_ge(steps, at(i, 0, 1))
                load(1, bass.ds(i * BODY + HALF, HALF))
                for h in range(2):
                    eng.wait_ge(steps, at(i, h, STEPS2))
                    eng.dma_start(lanes(m.rows2)[:, i * BODY + h * HALF:i * BODY + (h + 1) * HALF, :], rows[h]).then_inc(stored[h], 16)
                for h in range(2):
                    eng.wait_ge(stored[h], 16 * TURNS)
                    eng.nop().then_inc(rows_free[h], 1)

            @block.gpsimd
            def _(eng):
                eng.indirect_dma_start(out=q[1][:, HALF - 1, :], out_offset=None, in_=m.query2,
                                       in_offset=bass.IndirectOffsetOnAxis(ap=m.lane_first[:, 0:1], axis=0)).then_inc(q_first, 16)
                with eng.Fori(0, TURNS) as i:
                    for h in range(2):
                        hold(eng, staged[h], i + 1)
                        hold(eng, free[h], i + 1)
                        for j in range(HALF):
                            eng.indirect_dma_start(out=kv[h][:, j, :], out_offset=None, in_=m.table2,
                                                   in_offset=bass.IndirectOffsetOnAxis(ap=idx[h][:, j:j + 1], axis=0)).then_inc(landed[h], 16)

            @block.scalar
            def _(eng):
                for h in range(2):
                    eng.activation(idx[h], m.src[:, h * HALF:(h + 1) * HALF], ACT.Copy).then_inc(staged[h], 1)
                with eng.Fori(0, TURNS) as i:
                    for h in range(2):
                        hold(eng, landed[h], 16 * HALF * (i + 1))
                        eng.activation(idx[h], m.src[:, bass.ds(i * BODY + BODY + h * HALF, HALF)], ACT.Copy).then_inc(staged[h], 1)
                        eng.wait_ge(steps, at(i, h, SCORE2))
                        eng.activation(rows[h][:, :, SUM:MAX], e, ACT.Exp).then_inc(exped, 1)
                        eng.activation(fade, gap, ACT.Exp).then_inc(exped, 1)

            @block.vector
            def _(eng):
                for h in range(2):
                    eng.engine_nop().then_inc(free[h], 1)
                    eng.engine_nop().then_inc(rows_free[h], 1)
                f = Steps(eng, begun)
                f.put(eng.memset(rows[1][:, HALF - 1, 0:MAX], 0.0))
                f.then(eng.memset(rows[1][:, HALF - 1, MAX:R2], -BIG))
                eng.wait_ge(q_first, 16)
                eng.engine_nop().then_inc(steps, 1)
                with eng.Fori(0, TURNS) as i:
                    v = TurnSteps(eng, steps, i, PER_TURN2, start=1)
                    v.wait()
                    eng.nop(nofuse=True)
                    v.put(eng.tensor_copy(keeps, m.keep[:, bass.ds(i * BODY, BODY)]))
                    v.put(eng.tensor_copy(resets, m.reset[:, bass.ds(i * BODY, BODY)]))
                    for h in range(2):
                        row, before = rows[h], rows[1 - h][:, HALF - 1, :]
                        top = row[:, :, MAX:R2]
                        eng.wait_ge(q_in[h], 16 * i + 16)
                        v.wait()
                        for j in range(HALF):
                            s = h * HALF + j
                            v.then(eng.scalar_tensor_tensor(out=q[h][:, j, :], in0=q[h][:, j - 1, :] if j else q[1 - h][:, HALF - 1, :],
                                                            scalar=keeps[:, s:s + 1], in1=q[h][:, j, :], op0=ALU.mult, op1=ALU.add))
                        eng.wait_ge(landed[h], 16 * HALF * (i + 1))
                        v.then(eng.tensor_tensor(prod, q[h], kv[h][:, :, 0:D], ALU.mult))
                        v.then(eng.tensor_reduce(e, prod.rearrange("p t (a d) -> p t a d", d=D2), AX.X, ALU.add))
                        eng.wait_ge(rows_free[h], i + 1)
                        for j in range(HALF):
                            s = h * HALF + j
                            v.then(eng.scalar_tensor_tensor(out=top[:, j, :], in0=top[:, j - 1, :] if j else before[:, MAX:R2],
                                                            scalar=resets[:, s:s + 1], in1=e[:, j, :], op0=ALU.add, op1=ALU.max))
                        for j in range(HALF - 2, -1, -1):
                            s = h * HALF + j + 1
                            v.then(eng.scalar_tensor_tensor(out=top[:, j, :], in0=top[:, j + 1, :], scalar=resets[:, s:s + 1],
                                                            in1=top[:, j, :], op0=ALU.add, op1=ALU.max))
                        v.put(eng.tensor_tensor(e, e, top, ALU.subtract))
                        v.put(eng.scalar_tensor_tensor(out=gap, in0=before[:, MAX:R2], scalar=resets[:, h * HALF:h * HALF + 1],
                                                       in1=top[:, 0, :], op0=ALU.add, op1=ALU.subtract))
                        assert v.n == 3 + h * STEPS2 + SCORE2
                        eng.wait_ge(exped, 4 * i + 2 * h + 2)
                        v.put(eng.tensor_tensor(row[:, :, 0:D].rearrange("p t (a d) -> p t a d", d=D2),
                                                kv[h][:, :, D:2 * D].rearrange("p t (a d) -> p t a d", d=D2),
                                                spread(row[:, :, SUM:MAX], 3, [P, HALF, H2, D2]), ALU.mult))
                        v.put(eng.tensor_tensor(old[:, 0:SUM].rearrange("p (a d) -> p a d", d=D2), before[:, 0:SUM].rearrange("p (a d) -> p a d", d=D2),
                                                spread(fade, 2, [P, H2, D2]), ALU.mult))
                        v.then(eng.tensor_tensor(old[:, SUM:MAX], before[:, SUM:MAX], fade, ALU.mult))
                        eng.nop(nofuse=True).then_inc(free[h], 1)
                        v.then(eng.tensor_tensor(row[:, 0, 0:MAX], row[:, 0, 0:MAX], old, ALU.add))
                        for j in range(1, HALF):
                            s = h * HALF + j
                            v.then(eng.scalar_tensor_tensor(out=row[:, j, 0:MAX], in0=row[:, j - 1, 0:MAX], scalar=keeps[:, s:s + 1],
                                                            in1=row[:, j, 0:MAX], op0=ALU.mult, op1=ALU.add))
                        assert v.n == 3 + (h + 1) * STEPS2
                eng.wait_ge(steps, TURNS * PER_TURN2 + 1)
                f.then(eng.tensor_copy(m.lane_end[:, 0:R2], rows[1][:, HALF - 1, :]))


def layer2_nodes(nc, m, I):
    with phase(nc, "layer2_nodes") as sem:
        A = Arena(m)
        st = A(NB, R2)
        big = A(4 * NP)
        q, y = (big[:, j * NP:(j + 1) * NP].rearrange("p (b f) -> p b f", f=D) for j in range(2))
        aT, sT = (big[:, j * NP:(j + 1) * NP] for j in range(2, 4))
        kvn = A(NB, 2 * D)
        hid = [kvn[:, 8 * k:8 * k + 8, :].rearrange("p b f -> p (b f)").rearrange("p (j n) -> p j n", j=FF) for k in range(2)]
        out = kvn[:, 16:20, :].rearrange("p b f -> p (b f)").rearrange("p (a b f) -> p a b f", a=2, f=D)
        own = A(NB, H2)
        top = A(NB, H2)
        ex = A(2, NB * H2)
        den = A(NB, H2)
        st_b = A(len(REALCH), 6)
        mv_b = A(2)
        sd_b, scale, shift = A(1), A(1), A(1)
        st_n = A(NB, 6)
        mv_n = A(NB, 2)
        sd_n = A(NB)
        ps = m.psum
        SUM, MAX = D, D + H2
        aN = st[:, :, 0:D]
        bT = aT

        def c(name):
            k = COLUMNS.index(name)
            return m.cols[:, k:k + 1]

        state_in, own_in = sem("states_landed"), sem("own_rows_landed")
        vec = sem("vector_steps")
        expo, exped = sem("exponents"), sem("exponentials")
        a_made, a_t, a_k = sem("values_made"), sem("values_turned"), sem("values_kept")
        o_sum, s_made = sem("output_summed"), sem("sum_made")
        var1, root1, scale1, b_made = sem("variance1"), sem("root1"), sem("scale1"), sem("normed1")
        l1_sum, hid_made, leaky, l2_sum, s2_made = sem("hidden_summed"), sem("hidden_made"), sem("hidden_leaky"), sem("second_summed"), sem("sum2_made")
        var2, root2, scale2, b2_made = sem("variance2"), sem("root2"), sem("scale2"), sem("normed2")
        n_t, y_made = sem("normed_turned"), sem("y_made")
        varn, rootn, x_made = sem("node_variance"), sem("node_root"), sem("x_made")
        x_t, x_k = sem("x_turned"), sem("x_kept")
        t_sum, t_made = sem("table_summed"), sem("table_made")
        stored = [sem(f"table_stored{k}") for k in range(2)]
        NCH = len(CHUNKS)

        with nc.Block() as block:

            @block.gpsimd
            def _(eng):
                for b in range(NB):
                    eng.indirect_dma_start(out=st[:, b, :], out_offset=None, in_=m.rows2,
                                           in_offset=bass.IndirectOffsetOnAxis(ap=m.end[:, b:b + 1], axis=0)).then_inc(state_in, 16)

            @block.sync
            def _(eng):
                eng.dma_start(q, m.query2.rearrange("(b p) f -> p b f", p=P)).then_inc(own_in, 16)
                eng.dma_start(kvn, m.table2.rearrange("(b p) f -> p b f", p=P)).then_inc(own_in, 16)
                for k, (at, n) in enumerate(CHUNKS):
                    eng.wait_ge(t_made, k + 1)
                    eng.dma_start(m.table3.rearrange("(b p) f -> p b f", p=P)[:, at // P:(at + n) // P, :], out2(out, k, n)).then_inc(stored[k % 2], 16)
                for k in range(2):
                    eng.wait_ge(stored[k], 16 * len(range(k, NCH, 2)))

            @block.tensor
            def _(eng):
                eng.wait_ge(a_made, 1)
                turn_out(eng, ps, aN, a_t, a_k, m.ident[:, :], 0)
                for k, (at, n) in enumerate(CHUNKS):
                    eng.wait_ge(a_k, k + 1)
                    if k >= 2:
                        eng.wait_ge(s_made, k - 1)
                    eng.matmul(ps[:, 2 + k % 2, 0:n], m.wt[:, TRANSPOSED.index("L2_gnn_out_w"), :], aT[:, at:at + n], start=True, stop=True).then_inc(o_sum, 1)
                eng.wait_ge(a_k, NCH)
                eng.wait_ge(s_made, NCH)
                for k, (at, n) in enumerate(CHUNKS):
                    eng.wait_ge(b_made, k + 1)
                    for j in range(FF):
                        if k:
                            eng.wait_ge(hid_made, FF * (k - 1) + j + 1)
                        eng.matmul(ps[:, j, 0:n], m.wt[:, LIN1 + j, :], bT[:, at:at + n], start=True, stop=True).then_inc(l1_sum, 1)
                    eng.wait_ge(leaky, k + 1)
                    if k >= 2:
                        eng.wait_ge(s2_made, k - 1)
                    for j in range(FF):
                        t = eng.matmul(ps[:, 4 + k % 2, 0:n], m.wt[:, LIN2 + j, :], hid[k % 2][:, j, 0:n], start=(j == 0), stop=(j == FF - 1))
                    t.then_inc(l2_sum, 1)
                for k, (at, n) in enumerate(CHUNKS):
                    eng.wait_ge(b2_made, k + 1)
                    if k >= 2:
                        eng.wait_ge(y_made, k - 1)
                    for b in range(n // P):
                        t = eng.transpose(ps[:, 6 + k % 2, b * P:(b + 1) * P], sT[:, at + b * P:at + (b + 1) * P], m.ident[:, :])
                    t.then_inc(n_t, 1)
                eng.wait_ge(x_made, 1)
                eng.wait_ge(hid_made, FF * NCH)
                turn_out(eng, ps, m.xN, x_t, x_k, m.ident[:, :], 0)
                for k, (at, n) in enumerate(CHUNKS):
                    eng.wait_ge(x_k, k + 1)
                    if k >= 2:
                        eng.wait_ge(t_made, k - 1)
                    for b in range(n // P):
                        t = eng.matmul(ps[:, 2 + k % 2, b * P:(b + 1) * P], m.xT[:, at + b * P:at + (b + 1) * P], m.w3[:, 1, :], start=True, stop=True)
                    t.then_inc(t_sum, 1)

            @block.scalar
            def _(eng):
                eng.wait_ge(expo, 1)
                eng.activation(ex, ex, ACT.Exp).then_inc(exped, 1)
                turn_in(eng, ps, aT, a_t, a_k, 0)
                eng.wait_ge(var1, 1)
                eng.activation(sd_b, mv_b[:, 1:2], ACT.Sqrt, bias=m.eps[:, 0:1]).then_inc(root1, 1)
                eng.wait_ge(scale1, 1)
                for k, (at, n) in enumerate(CHUNKS):
                    eng.activation(bT[:, at:at + n], sT[:, at:at + n], ACT.Identity, bias=shift, scale=scale).then_inc(b_made, 1)
                for k, (at, n) in enumerate(CHUNKS):
                    if k >= 2:
                        eng.wait_ge(l2_sum, k - 1)
                    for j in range(FF):
                        eng.wait_ge(l1_sum, FF * k + j + 1)
                        eng.activation(hid[k % 2][:, j, 0:n], ps[:, j, 0:n], ACT.Identity, bias=m.lin1_b[:, j:j + 1]).then_inc(hid_made, 1)
                eng.wait_ge(var2, 1)
                eng.activation(sd_b, mv_b[:, 1:2], ACT.Sqrt, bias=m.eps[:, 0:1]).then_inc(root2, 1)
                eng.wait_ge(scale2, 1)
                for k, (at, n) in enumerate(CHUNKS):
                    eng.activation(sT[:, at:at + n], sT[:, at:at + n], ACT.Identity, bias=shift, scale=scale).then_inc(b2_made, 1)
                eng.wait_ge(varn, 1)
                eng.activation(sd_n, mv_n[:, :, 1], ACT.Sqrt, bias=m.eps[:, 0:1]).then_inc(rootn, 1)
                turn_in(eng, ps, m.xT, x_t, x_k, 0)
                for k, (at, n) in enumerate(CHUNKS):
                    eng.wait_ge(t_sum, k + 1)
                    if k >= 2:
                        eng.wait_ge(stored[k % 2], 16 * (k // 2))
                    eng.activation(out2(out, k, n), ps[:, 2 + k % 2, 0:n].rearrange("p (b f) -> p b f", f=D), ACT.Copy).then_inc(t_made, 1)

            @block.vector
            def _(eng):
                v = Steps(eng, vec)
                eng.wait_ge(own_in, 32)
                v.then(eng.tensor_tensor(q, q, kvn[:, :, 0:D], ALU.mult))
                v.then(eng.tensor_reduce(own, q.rearrange("p b (a d) -> p b a d", d=D2), AX.X, ALU.add))
                eng.wait_ge(state_in, 16 * NB)
                v.then(eng.tensor_tensor(top, own, st[:, :, MAX:R2], ALU.max))
                ex4 = ex.rearrange("p k (b a) -> p k b a", a=H2)
                v.put(eng.tensor_tensor(ex4[:, 0, :, :], st[:, :, MAX:R2], top, ALU.subtract))
                v.then(eng.tensor_tensor(ex4[:, 1, :, :], own, top, ALU.subtract))
                eng.engine_nop().then_inc(expo, 1)
                eng.wait_ge(exped, 1)
                v.then(eng.tensor_tensor(den, st[:, :, SUM:MAX], ex4[:, 0, :, :], ALU.mult))
                v.then(eng.tensor_tensor(den, den, ex4[:, 1, :, :], ALU.add))
                v.then(eng.tensor_scalar(den, den, 1e-16, None, ALU.add))
                v.then(eng.reciprocal(den, den))
                for k in range(2):
                    v.put(eng.tensor_tensor(ex4[:, k, :, :], ex4[:, k, :, :], den, ALU.mult))
                v.wait()
                for k, x in ((0, aN), (1, kvn[:, :, D:2 * D])):
                    x4 = x.rearrange("p b (a d) -> p b a d", d=D2)
                    v.put(eng.tensor_tensor(x4, x4, spread(ex4[:, k, :, :], 3, [P, NB, H2, D2]), ALU.mult))
                v.wait()
                v.then(eng.tensor_tensor(aN, aN, kvn[:, :, D:2 * D], ALU.add))
                eng.engine_nop().then_inc(a_made, 1)
                for k, (at, n) in enumerate(CHUNKS):
                    eng.wait_ge(o_sum, k + 1)
                    eng.scalar_tensor_tensor(out=sT[:, at:at + n], in0=ps[:, 2 + k % 2, 0:n], scalar=c("L2_gnn_out_b"), in1=m.xT[:, at:at + n],
                                             op0=ALU.add, op1=ALU.add).then_inc(s_made, 1)

                def norm(made, var, root, scaled, gamma, beta):
                    for k, (at, n) in enumerate(REALCH):
                        eng.wait_ge(made, k + 1)
                        v.put(eng.bn_stats(st_b[:, k, :], sT[:, at:at + n]))
                    v.wait()
                    eng.bn_aggr(mv_b, st_b).then_inc(var, 1)
                    eng.wait_ge(root, 1)
                    v.then(eng.reciprocal(sd_b, sd_b))
                    v.then(eng.tensor_tensor(scale, sd_b, c(gamma), ALU.mult))
                    v.then(eng.tensor_tensor(sd_b, mv_b[:, 0:1], scale, ALU.mult))
                    eng.tensor_tensor(shift, c(beta), sd_b, ALU.subtract).then_inc(scaled, 1)
                    eng.wait_ge(scaled, 1)

                norm(s_made, var1, root1, scale1, "L2_gnn_g1", "L2_gnn_b1")
                for k in range(NCH + 1):
                    if k < NCH:
                        hk = hid[k % 2][:, :, 0:CHUNKS[k][1]]
                        eng.wait_ge(hid_made, FF * (k + 1))
                        eng.scalar_tensor_tensor(out=hk, in0=hk, scalar=0.01, in1=hk, op0=ALU.mult, op1=ALU.max).then_inc(leaky, 1)
                    if k == 0:
                        continue
                    at, n = CHUNKS[k - 1]
                    eng.wait_ge(l2_sum, k)
                    eng.scalar_tensor_tensor(out=sT[:, at:at + n], in0=ps[:, 4 + (k - 1) % 2, 0:n], scalar=c("L2_gnn_lin2_b"), in1=bT[:, at:at + n],
                                             op0=ALU.add, op1=ALU.add).then_inc(s2_made, 1)
                norm(s2_made, var2, root2, scale2, "L2_gnn_g2", "L2_gnn_b2")
                for k, (at, n) in enumerate(CHUNKS):
                    eng.wait_ge(n_t, k + 1)
                    b0, b1 = at // P, (at + n) // P
                    eng.tensor_tensor(y[:, b0:b1, :], ps[:, 6 + k % 2, 0:n].rearrange("p (b f) -> p b f", f=D), m.xN[:, b0:b1, :], ALU.add).then_inc(y_made, 1)
                eng.wait_ge(y_made, NCH)
                for b in range(NB):
                    v.put(eng.bn_stats(st_n[:, b, :], y[:, b, :]))
                v.wait()
                for b in range(NB):
                    v.put(eng.bn_aggr(mv_n[:, b, :], st_n[:, b, :]))
                v.wait()
                eng.engine_nop().then_inc(varn, 1)
                eng.wait_ge(rootn, 1)
                v.then(eng.reciprocal(sd_n, sd_n))
                for b in range(NB):
                    v.put(eng.tensor_scalar(m.xN[:, b, :], y[:, b, :], mv_n[:, b, 0:1], sd_n[:, b:b + 1], ALU.subtract, ALU.mult))
                v.wait()
                eng.engine_nop().then_inc(x_made, 1)


def out2(out, k, n):
    return out[:, k % 2, 0:n // P, :]


PER_TURN3 = 2 * 2 * HALF + 3


def layer3_edges(nc, m, I):
    with phase(nc, "layer3_edges") as sem:
        A = Arena(m)
        feat = [A(HALF, D) for _ in range(2)]
        rows = [A(HALF, D) for _ in range(2)]
        resets, vals = A(BODY), A(BODY)
        idx = [A(HALF, dt=I32) for _ in range(2)]
        begun = sem("states_begun")
        steps = sem("edge_steps")
        staged = [sem(f"indices_staged{h}") for h in range(2)]
        landed = [sem(f"rows_landed{h}") for h in range(2)]
        free = [sem(f"rows_used{h}") for h in range(2)]
        stored = [sem(f"states_stored{h}") for h in range(2)]
        rows_free = [sem(f"states_free{h}") for h in range(2)]

        with nc.Block() as block:

            @block.sync
            def _(eng):
                with eng.Fori(0, TURNS) as i:
                    for h in range(2):
                        hold(eng, steps, i * PER_TURN3 + 3 + (h + 1) * 2 * HALF)
                        eng.dma_start(lanes(m.rows3)[:, bass.ds(i * BODY + h * HALF, HALF), :], rows[h]).then_inc(stored[h], 16)
                        hold(eng, stored[h], 16 * i + 16)
                        eng.nop().then_inc(rows_free[h], 1)

            @block.gpsimd
            def _(eng):
                with eng.Fori(0, TURNS) as i:
                    for h in range(2):
                        hold(eng, staged[h], i + 1)
                        hold(eng, free[h], i + 1)
                        for j in range(HALF):
                            eng.indirect_dma_start(out=feat[h][:, j, :], out_offset=None, in_=m.table3,
                                                   in_offset=bass.IndirectOffsetOnAxis(ap=idx[h][:, j:j + 1], axis=0)).then_inc(landed[h], 16)

            @block.scalar
            def _(eng):
                for h in range(2):
                    eng.activation(idx[h], m.src[:, h * HALF:(h + 1) * HALF], ACT.Copy).then_inc(staged[h], 1)
                with eng.Fori(0, TURNS) as i:
                    for h in range(2):
                        hold(eng, landed[h], 16 * HALF * (i + 1))
                        eng.activation(idx[h], m.src[:, bass.ds(i * BODY + BODY + h * HALF, HALF)], ACT.Copy).then_inc(staged[h], 1)

            @block.vector
            def _(eng):
                for h in range(2):
                    eng.engine_nop().then_inc(free[h], 1)
                    eng.engine_nop().then_inc(rows_free[h], 1)
                f = Steps(eng, begun)
                f.then(eng.memset(rows[1][:, HALF - 1, :], -BIG))
                eng.engine_nop().then_inc(steps, 1)
                with eng.Fori(0, TURNS) as i:
                    v = TurnSteps(eng, steps, i, PER_TURN3, start=1)
                    v.wait()
                    eng.nop(nofuse=True)
                    v.put(eng.tensor_copy(resets, m.reset[:, bass.ds(i * BODY, BODY)]))
                    v.put(eng.tensor_copy(vals, m.val[:, bass.ds(i * BODY, BODY)]))
                    v.wait()
                    for h in range(2):
                        eng.wait_ge(landed[h], 16 * HALF * (i + 1))
                        for j in range(HALF):
                            s = h * HALF + j
                            v.put(eng.scalar_tensor_tensor(out=feat[h][:, j, :], in0=m.edge_w[:, :], scalar=vals[:, s:s + 1],
                                                           in1=feat[h][:, j, :], op0=ALU.mult, op1=ALU.add))
                        v.wait()
                        eng.wait_ge(rows_free[h], i + 1)
                        for j in range(HALF):
                            s = h * HALF + j
                            v.then(eng.scalar_tensor_tensor(out=rows[h][:, j, :], in0=rows[h][:, j - 1, :] if j else rows[1 - h][:, HALF - 1, :],
                                                            scalar=resets[:, s:s + 1], in1=feat[h][:, j, :], op0=ALU.add, op1=ALU.max))
                        assert v.n == 3 + (h + 1) * 2 * HALF
                        eng.nop(nofuse=True).then_inc(free[h], 1)
                    v.put(eng.engine_nop())
                eng.wait_ge(steps, TURNS * PER_TURN3 + 1)
                f.then(eng.tensor_copy(m.lane_end[:, 0:D], rows[1][:, HALF - 1, :]))


def layer3_nodes(nc, m, I, result):
    with phase(nc, "layer3_nodes") as sem:
        A = Arena(m)
        lane_max = A(P + 1)
        row = A(D)
        agg = A(NB, D)
        aT, hT = A(NP), A(NP)
        y = A(NB, D)
        st_n = A(NB, 6)
        mv_n = A(NB, 2)
        sd_n = A(NB)
        ps = m.psum

        def r(name):
            return m.rows[:, ROWS.index(name), :]

        row_in, fixed, agg_in = sem("first_rows_landed"), sem("first_rows_fixed"), sem("maxima_landed")
        vec = sem("vector_steps")
        l_t, l_made, l_back, merged = sem("lanes_turned"), sem("lane_maxima"), sem("lane_maxima_turned"), sem("rows_merged")
        d_sum, a_made, a_t, a_k = sem("target_part_summed"), sem("agg_made"), sem("agg_turned"), sem("agg_kept")
        h_sum, h_made, y_sum, y_made = sem("hidden_summed"), sem("hidden_made"), sem("y_summed"), sem("y_made")
        varn, rootn, x_made, out_done = sem("node_variance"), sem("node_root"), sem("x_made"), sem("result_stored")
        NCH = len(CHUNKS)

        with nc.Block() as block:

            @block.gpsimd
            def _(eng):
                eng.indirect_dma_start(out=row, out_offset=None, in_=m.rows3,
                                       in_offset=bass.IndirectOffsetOnAxis(ap=m.first_end[:, 0:1], axis=0)).then_inc(row_in, 16)
                eng.wait_ge(merged, 1)
                eng.indirect_dma_start(out=m.rows3, out_offset=bass.IndirectOffsetOnAxis(ap=m.first_fix[:, 0:1], axis=0),
                                       in_=row, in_offset=None).then_inc(fixed, 16)
                eng.wait_ge(fixed, 16)
                for b in range(NB):
                    eng.indirect_dma_start(out=agg[:, b, :], out_offset=None, in_=m.rows3,
                                           in_offset=bass.IndirectOffsetOnAxis(ap=m.end[:, b:b + 1], axis=0)).then_inc(agg_in, 16)

            @block.sync
            def _(eng):
                eng.wait_ge(x_made, 1)
                eng.dma_start(result[0:(NB - 1) * P, :].rearrange("(b p) f -> p b f", p=P), m.xN[:, 0:NB - 1, :]).then_inc(out_done, 16)
                eng.dma_start(result[(NB - 1) * P:N, :], m.xN[0:TAIL, NB - 1, :]).then_inc(out_done, 16)
                eng.wait_ge(out_done, 32)

            @block.tensor
            def _(eng):
                eng.transpose(ps[:, 6, 0:P], m.lane_end[:, 0:D], m.ident[:, :]).then_inc(l_t, 1)
                eng.wait_ge(l_made, 1)
                eng.transpose(ps[:, 7, 0:P], lane_max[:, 0:P], m.ident[:, :]).then_inc(l_back, 1)
                for k, (at, n) in enumerate(CHUNKS):
                    if k >= 2:
                        eng.wait_ge(a_made, k - 1)
                    for b in range(n // P):
                        t = eng.matmul(ps[:, 2 + k % 2, b * P:(b + 1) * P], m.xT[:, at + b * P:at + (b + 1) * P], m.w3[:, 0, :], start=True, stop=True)
                    t.then_inc(d_sum, 1)
                eng.wait_ge(a_made, NCH)
                turn_out(eng, ps, agg, a_t, a_k, m.ident[:, :], 0)
                for k, (at, n) in enumerate(CHUNKS):
                    eng.wait_ge(a_k, k + 1)
                    if k >= 2:
                        eng.wait_ge(h_made, k - 1)
                    eng.matmul(ps[:, 4 + k % 2, 0:n], m.w3[:, 2, :], m.xT[:, at:at + n], start=True, stop=False)
                    eng.matmul(ps[:, 4 + k % 2, 0:n], m.w3[:, 3, :], aT[:, at:at + n], start=False, stop=True).then_inc(h_sum, 1)
                for k, (at, n) in enumerate(CHUNKS):
                    eng.wait_ge(h_made, k + 1)
                    if k >= 2:
                        eng.wait_ge(y_made, k - 1)
                    for b in range(n // P):
                        t = eng.matmul(ps[:, 2 + k % 2, b * P:(b + 1) * P], hT[:, at + b * P:at + (b + 1) * P], m.w3[:, 4, :], start=True, stop=True)
                    t.then_inc(y_sum, 1)

            @block.scalar
            def _(eng):
                turn_in(eng, ps, aT, a_t, a_k, 0)
                k3 = COLUMNS.index("L3_gnn_b1")
                for k, (at, n) in enumerate(CHUNKS):
                    eng.wait_ge(h_sum, k + 1)
                    eng.activation(hT[:, at:at + n], ps[:, 4 + k % 2, 0:n], ACT.Relu, bias=m.cols[:, k3:k3 + 1]).then_inc(h_made, 1)
                eng.wait_ge(varn, 1)
                eng.activation(sd_n, mv_n[:, :, 1], ACT.Sqrt, bias=m.eps[:, 0:1]).then_inc(rootn, 1)

            @block.vector
            def _(eng):
                v = Steps(eng, vec)
                v.put(eng.memset(lane_max[:, 0:1], -BIG))
                eng.wait_ge(l_t, 1)
                v.then(eng.tensor_tensor_scan(lane_max[:, 1:P + 1], m.whole_neg[:, :], ps[:, 6, 0:P], -BIG, ALU.add, ALU.max))
                eng.engine_nop().then_inc(l_made, 1)
                eng.wait_ge(row_in, 16)
                eng.wait_ge(l_back, 1)
                eng.tensor_tensor(row, row, ps[:, 7, 0:P], ALU.max).then_inc(merged, 1)
                eng.wait_ge(agg_in, 16 * NB)
                for k, (at, n) in enumerate(CHUNKS):
                    b0, b1 = at // P, (at + n) // P
                    a = agg[:, b0:b1, :]
                    eng.wait_ge(d_sum, k + 1)
                    v.then(eng.tensor_tensor(a, a, ps[:, 2 + k % 2, 0:n].rearrange("p (b f) -> p b f", f=D), ALU.add))
                    v.then(eng.tensor_tensor(a, a, spread(r("L3_gnn_bm"), 1, [P, b1 - b0, D]), ALU.add))
                    eng.tensor_tensor(a, a, spread(m.has[:, b0:b1], 2, [P, b1 - b0, D]), ALU.mult).then_inc(a_made, 1)
                v.then(eng.tensor_tensor(m.xN[:, :, :], m.xN[:, :, :], spread(r("L3_gnn_b2"), 1, [P, NB, D]), ALU.add))
                for k, (at, n) in enumerate(CHUNKS):
                    eng.wait_ge(y_sum, k + 1)
                    b0, b1 = at // P, (at + n) // P
                    eng.tensor_tensor(y[:, b0:b1, :], ps[:, 2 + k % 2, 0:n].rearrange("p (b f) -> p b f", f=D), m.xN[:, b0:b1, :], ALU.add).then_inc(y_made, 1)
                eng.wait_ge(y_made, NCH)
                for b in range(NB):
                    v.put(eng.bn_stats(st_n[:, b, :], y[:, b, :]))
                v.wait()
                for b in range(NB):
                    v.put(eng.bn_aggr(mv_n[:, b, :], st_n[:, b, :]))
                v.wait()
                eng.engine_nop().then_inc(varn, 1)
                eng.wait_ge(rootn, 1)
                v.then(eng.reciprocal(sd_n, sd_n))
                for b in range(NB):
                    v.put(eng.tensor_scalar(m.xN[:, b, :], y[:, b, :], mv_n[:, b, 0:1], sd_n[:, b:b + 1], ALU.subtract, ALU.mult))
                v.wait()
                eng.engine_nop().then_inc(x_made, 1)


def gnn_resnorm_stack(nc, I, out):
    with ExitStack() as ctx:
        m = allocate(nc, ctx)
        setup_phase(nc, m, I)
        layer0_edges(nc, m, I)
        layer0_nodes(nc, m, I)
        layer1_edges(nc, m, I)
        carry_sums(nc, m, m.rows1, REL, H1)
        layer1_nodes(nc, m, I)
        layer2_edges(nc, m, I)
        carry_sums(nc, m, m.rows2, 1, H2)
        layer2_nodes(nc, m, I)
        layer3_edges(nc, m, I)
        layer3_nodes(nc, m, I, out)


_INS = ['x', 'src', 'dst', 'edge_type_4', 'edge_weight'] + [
    'L0_gnn_' + n for n in ('W1w', 'W1b', 'U1w', 'U1b', 'W2w', 'W2b', 'U2w', 'U2b', 'W3w', 'W3b', 'U3w', 'U3b', 'bn_g',
                            'bn_b', 'm_w0', 'm_b0', 'm_bng', 'm_bnb', 'm_w1', 'm_b1')] + [
    'L1_gnn_' + n for n in ('W', 'attn_src', 'attn_dst', 'bias', 'ln_gamma', 'ln_beta')] + [
    'L2_gnn_' + n for n in ('q_w', 'q_b', 'k_w', 'v_w', 'out_w', 'out_b', 'g1', 'b1', 'lin1_w', 'lin1_b', 'lin2_w',
                            'lin2_b', 'g2', 'b2')] + [
    'L3_gnn_' + n for n in ('Wm', 'bm', 'W1', 'b1', 'W2', 'b2')]
_OUTS = [((3125, 128), 'float32')]


def kernel(**inputs):
    import numpy as _np
    import concourse.bacc as _bacc
    from concourse import mybir as _mybir
    from concourse.bass_utils import run_bass_kernel_spmd as _run

    nc = _bacc.Bacc("TRN2", target_bir_lowering=False, num_devices=1)
    arrays, I, outs = {}, {}, []
    for name in _INS:
        a = _np.ascontiguousarray(inputs[name])
        arrays[f"in_{name}_dram"] = a
        I[name] = nc.dram_tensor(f"in_{name}_dram", a.shape, _mybir.dt.from_np(a.dtype), kind="ExternalInput").ap()
    for i, (shape, dtype) in enumerate(_OUTS):
        dt = _mybir.dt.from_np(_np.dtype(dtype))
        outs.append(nc.dram_tensor(f"out_{i}_dram", shape, dt, kind="ExternalOutput").ap())
    gnn_resnorm_stack(nc, I, outs[0])
    r = _run(nc, [arrays], core_ids=[0])
    got = tuple(r.results[0][f"out_{i}_dram"] for i in range(len(_OUTS)))
    return got[0]
```

```python
from contextlib import ExitStack, contextmanager

import concourse.bass as bass
from concourse import mybir

F32 = mybir.dt.float32
BF16 = mybir.dt.bfloat16
I32 = mybir.dt.int32
ALU = mybir.AluOpType
ACT = mybir.ActivationFunctionType
AX = mybir.AxisListType

P = 128
N, D, E = 3125, 128, 100000
NB = -(-N // P)
NP = NB * P
TAIL = N - (NB - 1) * P
HALF = 14
BODY = 2 * HALF
TURNS = 28
T = BODY * TURNS
EP = P * T
LAST = E - (P - 1) * T
assert EP >= E and 0 < LAST <= T
RING = 4
LOOPS = T // (RING * HALF)
AHEAD = RING * HALF
assert T == LOOPS * RING * HALF
SEVEN = 7
TABS = 4
REL, H1, D1 = 4, 4, 32
RH = REL * H1
H2, D2 = 8, 16
FF = 4
R1 = REL * D + 2 * RH
R2 = D + 2 * H2
HS = D + H1
BIG = 1e30
EPS = 1e-5
CHUNKS = [(c, min(512, NP - c)) for c in range(0, NP, 512)]
REALCH = [(c, min(512, N - c)) for c in range(0, N, 512)]

TRANSPOSED = ["L0_gnn_W1w", "L0_gnn_U1w", "L0_gnn_W2w", "L0_gnn_U2w", "L0_gnn_W3w", "L0_gnn_U3w",
              "L0_gnn_m_w0", "L0_gnn_m_w1", "L2_gnn_q_w", "L2_gnn_k_w", "L2_gnn_v_w", "L2_gnn_out_w"]
LIN1 = len(TRANSPOSED)
LIN2 = LIN1 + FF
SLOTS = LIN2 + FF
COLUMNS = ["L0_gnn_W1b", "L0_gnn_U1b", "L0_gnn_W2b", "L0_gnn_U2b", "L0_gnn_W3b", "L0_gnn_U3b",
           "L0_gnn_bn_g", "L0_gnn_bn_b", "L0_gnn_m_b0", "L0_gnn_m_bng", "L0_gnn_m_bnb",
           "L2_gnn_out_b", "L2_gnn_g1", "L2_gnn_b1", "L2_gnn_lin2_b", "L2_gnn_g2", "L2_gnn_b2",
           "L3_gnn_b1"]
ROWS = ["L0_gnn_m_b1", "L1_gnn_bias", "L1_gnn_ln_gamma", "L1_gnn_ln_beta", "L2_gnn_q_b", "L3_gnn_bm", "L3_gnn_b2"]


class Memory:
    pass


def spread(ap, axis, shape):
    return ap.unsqueeze(axis).broadcast_to(shape)


def hold(eng, sem, value):
    eng.wait_ge(sem, value)
    eng.nop(nofuse=True)


@contextmanager
def phase(nc, of):
    sems = []

    def sem(name):
        sems.append(nc.alloc_semaphore(f"{of}_{name}"))
        return sems[-1]

    yield sem
    nc.clear_and_free_semaphores(sems)
    nc.all_engine_barrier()


def lanes(rows):
    return rows[0:EP, :].rearrange("(p t) f -> p t f", p=P)


def allocate(nc, ctx):
    m = Memory()

    def sb(name, shape, dt=F32):
        return ctx.enter_context(nc.sbuf_tensor(name, shape, dt))

    def dram(name, shape, dt=F32):
        return nc.dram_tensor(name, shape, dt, kind="Internal").ap()

    m.src = sb("src", [P, T + AHEAD], I32)
    m.src_rel = sb("src_rel", [P, T + AHEAD], I32)
    m.val = sb("val", [P, T])
    m.keep = sb("keep", [P, T + BODY])
    m.reset = sb("reset", [P, T + BODY])
    m.other_rel = sb("other_rel", [P, T, REL], BF16)
    m.lane_first = sb("lane_first", [P, 1], I32)
    m.first_end = sb("first_end", [P, 1], I32)
    m.first_fix = sb("first_fix", [P, 1], I32)
    m.whole_neg = sb("whole_neg", [P, P])
    m.start = sb("start", [P, NB], I32)
    m.end = sb("end", [P, NB], I32)
    m.has = sb("has", [P, NB])
    m.xN = sb("xN", [P, NB, D])
    m.xT = sb("xT", [P, NP])
    m.ident = sb("ident", [P, P])
    m.spare = sb("spare", [P, 1])
    m.lower = sb("lower", [P, P])
    m.tri = sb("tri", [P, P])
    m.ones = sb("ones", [P, P])
    m.eps = sb("eps", [P, 1])
    m.wt = sb("wt", [P, SLOTS, P])
    m.cols = sb("cols", [P, len(COLUMNS)])
    m.lin1_b = sb("lin1_b", [P, FF])
    m.rows = sb("rows", [P, len(ROWS), D])
    m.w_rel = sb("w_rel", [P, REL, D])
    m.w3 = sb("w3", [P, 5, D])
    m.edge_w = sb("edge_w", [P, D])
    m.lane_end = sb("lane_end", [P, R1])
    m.arena = sb("arena", [P, 35040])
    m.psum = ctx.enter_context(nc.psum_tensor("psum", [P, 8, 512], F32))

    m.seg_rows = dram("seg_rows", [EP + NP, D])
    m.seg_dst = dram("seg_dst", [EP + NP, RH])
    m.tabs = [dram(f"tab{j}", [NP + P, D]) for j in range(TABS)]
    m.rows1 = dram("rows1", [EP + 1 + P, R1])
    m.rows2 = dram("rows2", [EP + 1 + P, R2])
    m.rows3 = dram("rows3", [EP + 1 + P, D])
    m.table1 = dram("table1", [NP * REL, HS])
    m.dst1 = dram("dst1", [NP, RH])
    m.query2 = dram("query2", [NP, D])
    m.table2 = dram("table2", [NP, 2 * D])
    m.table3 = dram("table3", [NP, D])
    return m


class Arena:

    def __init__(self, m):
        self.m, self.at = m, 0

    def __call__(self, *shape, dt=F32):
        n = 1
        for s in shape:
            n *= s
        words = n if dt != BF16 else -(-n // 2)
        ap = self.m.arena[:, self.at:self.at + words]
        self.at += words
        assert self.at <= 35040, self.at
        if dt != F32:
            ap = ap.bitcast(dt)
        if len(shape) == 2:
            ap = ap.rearrange("p (a b) -> p a b", b=shape[1])
        if len(shape) == 3:
            ap = ap.rearrange("p (a b c) -> p a b c", b=shape[1], c=shape[2])
        return ap


def setup_phase(nc, m, I):
    with phase(nc, "setup_phase") as sem:
        A = Arena(m)
        dst = A(T, dt=I32)
        typ = A(T, dt=I32)
        dstf = A(T)
        typf = A(T)
        lo_i = A(T, dt=I32)
        hi_i = A(T, dt=I32)
        lo = A(T, dt=BF16)
        hi = A(T, dt=BF16)
        same = A(T)
        prev_last = A(1, dt=I32)
        prev_lastf = A(1)
        iota = A(P, dt=BF16)
        iota_i = A(P, dt=I32)
        nul = A(P, dt=BF16)
        spare_start = A(NB)
        spare_row = A(1)
        lane_base = A(1)
        hot_lo = [A(HALF, P, dt=BF16) for _ in range(2)]
        hot_hi = [A(HALF, NB, dt=BF16) for _ in range(2)]
        deg, cum, tot, incl, end1, tmp, ones_nb = (A(NB) for _ in range(7))
        count, firstf, whole = A(1), A(1), A(1)
        zeros = A(BODY * D)
        neutral = A(R1 + D)
        w_nat = A(SLOTS, P)

        fixed = sem("fixed_parts_set")
        const = sem("constants_made")
        l_dst, l_edge, l_x, l_prev = sem("dst_loaded"), sem("edges_loaded"), sem("x_loaded"), sem("prev_loaded")
        l_w, l_small = sem("weights_loaded"), sem("small_loaded")
        zeroed = sem("scratch_zeroed")
        prep = sem("edge_parts")
        hot_free = [sem(f"hot_free{h}") for h in range(2)]
        hot_made = [sem(f"hot_made{h}") for h in range(2)]
        deg_done, cum_done, whole_done = sem("degrees_counted"), sem("degrees_summed"), sem("whole_spread")
        wt_done, wt_kept = sem("weights_turned"), sem("weights_kept")
        xt_done, xt_kept = sem("x_turned"), sem("x_kept")
        scattered = sem("x_scattered")
        ps = m.psum
        WGROUPS = SLOTS // 4

        (S_DSTF, S_LOI, S_HII, S_LO, S_HI, S_PREV) = range(1, 7)

        with nc.Block() as block:

            @block.gpsimd
            def _(eng):
                eng.memset(zeros, 0.0).then_inc(const, 1)
                eng.iota(iota_i, [[1, P]], base=0, channel_multiplier=0).then_inc(const, 1)
                eng.memset(nul, 0.0).then_inc(const, 1)
                eng.memset(m.ones[:, :], 1.0).then_inc(const, 1)
                eng.wait_ge(const, 4)
                eng.affine_select(out=m.ident[:, :], in_=m.ones[:, :], compare_op=ALU.is_equal, fill=0.0, base=0,
                                  pattern=[[-1, P]], channel_multiplier=1).then_inc(const, 1)
                eng.affine_select(out=m.lower[:, :], in_=m.ones[:, :], compare_op=ALU.is_gt, fill=0.0, base=0,
                                  pattern=[[-1, P]], channel_multiplier=1).then_inc(const, 1)
                eng.affine_select(out=m.tri[:, :], in_=m.ones[:, :], compare_op=ALU.is_ge, fill=0.0, base=0,
                                  pattern=[[1, P]], channel_multiplier=-1).then_inc(const, 1)
                eng.iota(spare_start, [[P, NB]], base=EP, channel_multiplier=1,
                         allow_small_or_imprecise_dtypes=True).then_inc(const, 1)
                eng.iota(m.spare[:, :], [[1, 1]], base=NP, channel_multiplier=1,
                         allow_small_or_imprecise_dtypes=True).then_inc(const, 1)
                eng.iota(spare_row, [[1, 1]], base=EP + 1, channel_multiplier=1,
                         allow_small_or_imprecise_dtypes=True).then_inc(const, 1)
                eng.iota(lane_base, [[1, 1]], base=-1, channel_multiplier=T,
                         allow_small_or_imprecise_dtypes=True).then_inc(const, 1)
                eng.memset(m.eps[:, :], EPS).then_inc(const, 1)
                eng.memset(ones_nb, 1.0).then_inc(const, 1)
                eng.memset(neutral[:, 0:R1], 0.0).then_inc(const, 1)
                eng.wait_ge(const, 14)
                eng.memset(neutral[:, R1 - RH:R1 + D], -BIG).then_inc(const, 1)
                eng.wait_ge(l_x, 32)
                eng.wait_ge(zeroed, 16 * ZEROS)
                eng.wait_ge(prep, S_START)
                for b in range(NB):
                    eng.indirect_dma_start(out=m.seg_rows[:, :],
                                           out_offset=bass.IndirectOffsetOnAxis(ap=m.start[:, b:b + 1], axis=0),
                                           in_=m.xN[:, b, :], in_offset=None).then_inc(scattered, 16)
                eng.wait_ge(scattered, 16 * NB)

            @block.sync
            def _(eng):
                eng.wait_ge(fixed, 6)
                for tile, name, s in ((dst, "dst", l_dst), (m.src[:, 0:T], "src", l_edge),
                                      (typ, "edge_type_4", l_edge), (m.val[:, :], "edge_weight", l_edge)):
                    eng.dma_start(tile[0:112, :], I[name][0:112 * T].rearrange("(p t) -> p t", t=T)).then_inc(s, 16)
                    eng.dma_start(tile[112:127, :], I[name][112 * T:127 * T].rearrange("(p t) -> p t", t=T)).then_inc(s, 16)
                    eng.dma_start(tile[127:128, 0:LAST], I[name][127 * T:E].rearrange("(p t) -> p t", p=1)).then_inc(s, 16)
                eng.dma_start(prev_last[1:P, :], I["dst"][0:(P - 1) * T].rearrange("(p t) -> p t", t=T)[:, T - 1:T],
                              allow_slow_non_contiguous=True).then_inc(l_prev, 16)
                eng.dma_start(m.xN[:, 0:NB - 1, :], I["x"][0:(NB - 1) * P, :].rearrange("(b p) f -> p b f", p=P)).then_inc(l_x, 16)
                eng.dma_start(m.xN[0:TAIL, NB - 1, :], I["x"][(NB - 1) * P:N, :]).then_inc(l_x, 16)
                eng.wait_ge(const, 15)
                eng.dma_start(m.rows1[EP:EP + 1, :], neutral[0:1, 0:R1]).then_inc(zeroed, 16)
                eng.dma_start(m.rows2[EP:EP + 1, :], neutral[0:1, R1 - RH - D - H2:R1 - RH + H2]).then_inc(zeroed, 16)
                eng.dma_start(m.rows3[EP:EP + 1, :], neutral[0:1, R1:R1 + D]).then_inc(zeroed, 16)

                for rows, width in ((m.rows1, R1), (m.rows2, R2), (m.rows3, D)):
                    eng.dma_start(rows[EP + 1:EP + 1 + P, :], zeros[:, 0:width]).then_inc(zeroed, 16)

            @block.scalar
            def _(eng):
                for s, name in enumerate(TRANSPOSED):
                    eng.dma_start(w_nat[:, s, :], I[name]).then_inc(l_w, 16)
                eng.dma_start(w_nat[:, LIN1:LIN2, :], I["L2_gnn_lin1_w"].rearrange("(j o) i -> o j i", o=P)).then_inc(l_w, 16)
                eng.dma_start(w_nat[:, LIN2:SLOTS, :], I["L2_gnn_lin2_w"].rearrange("o (j i) -> o j i", i=P)).then_inc(l_w, 16)
                eng.wait_ge(const, 1)
                eng.wait_ge(l_dst, 48)
                with eng.Fori(0, TURNS) as i:
                    eng.dma_start(lanes(m.seg_rows)[:, bass.ds(i * BODY, BODY), :].rearrange("p t f -> p (t f)"), zeros).then_inc(zeroed, 16)
                for c, name in enumerate(COLUMNS):
                    eng.dma_start(m.cols[:, c:c + 1], I[name].rearrange("(p a) -> p a", a=1), allow_slow_non_contiguous=True).then_inc(l_small, 16)
                eng.dma_start(m.lin1_b[:, :], I["L2_gnn_lin1_b"].rearrange("(j p) -> p j", p=P), allow_slow_non_contiguous=True).then_inc(l_small, 16)
                for r, name in enumerate(ROWS):
                    eng.dma_start(m.rows[:, r, :], I[name].partition_broadcast(P)).then_inc(l_small, 16)
                eng.dma_start(m.w_rel[:, :, :], I["L1_gnn_W"].rearrange("r i o -> i r o")).then_inc(l_small, 16)
                for k, (name, at) in enumerate((("L3_gnn_Wm", 0), ("L3_gnn_Wm", D), ("L3_gnn_W1", 0), ("L3_gnn_W1", D), ("L3_gnn_W2", 0))):
                    eng.dma_start(m.w3[:, k, :], I[name][at:at + D, :]).then_inc(l_small, 16)
                eng.dma_start(m.edge_w[:, :], I["L3_gnn_Wm"][2 * D, :].partition_broadcast(P)).then_inc(l_small, 16)
                for g in range(WGROUPS):
                    eng.wait_ge(wt_done, g + 1)
                    eng.activation(m.wt[:, 4 * g:4 * g + 4, :], ps[:, g, :].rearrange("p (a b) -> p a b", b=P), ACT.Copy).then_inc(wt_kept, 1)
                for k, (c, w) in enumerate(CHUNKS):
                    eng.wait_ge(xt_done, k + 1)
                    eng.activation(m.xT[:, c:c + w], ps[:, k % 2, 0:w], ACT.Copy).then_inc(xt_kept, 1)
                eng.wait_ge(l_small, 16 * SMALL)
                eng.wait_ge(zeroed, 16 * ZEROS)

            @block.tensor
            def _(eng):
                eng.wait_ge(const, 15)
                eng.matmul(ps[:, 7, 0:NB], nul, nul[:, 0:NB], start=True, stop=False)
                for h in range(2):
                    eng.nop().then_inc(hot_free[h], 1)
                with eng.Fori(0, TURNS) as i:
                    for h in range(2):
                        eng.wait_ge(hot_made[h], 2 * i + 2)
                        for j in range(HALF):
                            t = eng.matmul(ps[:, 7, 0:NB], hot_lo[h][:, j, :], hot_hi[h][:, j, :], start=False, stop=False,
                                           skip_group_check=True)
                        t.then_inc(hot_free[h], 1)
                eng.matmul(ps[:, 7, 0:NB], nul, nul[:, 0:NB], start=False, stop=True).then_inc(deg_done, 1)
                eng.wait_ge(prep, S_DEG)
                eng.matmul(ps[:, 6, 0:NB], m.tri[:, :], deg, start=True, stop=True)
                eng.matmul(ps[:, 6, 64:64 + NB], m.ones[:, :], deg, start=True, stop=True).then_inc(cum_done, 1)
                eng.wait_ge(prep, S_WHOLE)
                eng.matmul(ps[:, 5, 0:P], whole.broadcast_to([P, P]), m.ident[:, :], start=True, stop=True).then_inc(whole_done, 1)
                eng.wait_ge(l_w, 16 * (len(TRANSPOSED) + 2))
                for g in range(WGROUPS):
                    for k in range(4):
                        t = eng.transpose(ps[:, g, k * P:k * P + P], w_nat[:, 4 * g + k, :], m.ident[:, :])
                    t.then_inc(wt_done, 1)
                eng.wait_ge(l_x, 32)
                for k, (c, w) in enumerate(CHUNKS):
                    eng.wait_ge(wt_kept, 2)
                    if k >= 2:
                        eng.wait_ge(xt_kept, k - 1)
                    for b in range(w // P):
                        t = eng.transpose(ps[:, k % 2, b * P:b * P + P], m.xN[:, c // P + b, :], m.ident[:, :])
                    t.then_inc(xt_done, 1)

            @block.vector
            def _(eng):
                eng.memset(dst[96:P, LAST:T], NP - 1).then_inc(fixed, 1)
                eng.memset(m.src[:, LAST:T + AHEAD], 0).then_inc(fixed, 1)
                eng.memset(typ[96:P, LAST:T], 0).then_inc(fixed, 1)
                eng.memset(m.val[96:P, LAST:T], 0.0).then_inc(fixed, 1)
                eng.memset(prev_last, -1).then_inc(fixed, 1)
                eng.memset(m.xN[:, NB - 1, :], 0.0).then_inc(fixed, 1)
                eng.wait_ge(l_dst, 48)
                eng.tensor_copy(dstf, dst).then_inc(prep, 1)
                eng.tensor_scalar(lo_i, dst, P - 1, None, ALU.bitwise_and).then_inc(prep, 1)
                eng.tensor_scalar(hi_i, dst, 7, None, ALU.logical_shift_right).then_inc(prep, 1)
                eng.wait_ge(prep, S_LOI)
                eng.tensor_copy(lo, lo_i).then_inc(prep, 1)
                eng.wait_ge(prep, S_HII)
                eng.tensor_copy(hi, hi_i).then_inc(prep, 1)
                eng.wait_ge(const, 15)
                eng.tensor_copy(iota, iota_i).then_inc(prep, 1)
                eng.wait_ge(prep, S_PREV)
                with eng.Fori(0, TURNS) as i:
                    for h in range(2):
                        eng.wait_ge(hot_free[h], i + 1)
                        eng.tensor_tensor(hot_lo[h], spread(iota, 1, [P, HALF, P]),
                                          spread(lo[:, bass.ds(i * BODY + h * HALF, HALF)], 2, [P, HALF, P]), ALU.is_equal).then_inc(hot_made[h], 1)
                        eng.tensor_tensor(hot_hi[h], spread(iota[:, 0:NB], 1, [P, HALF, NB]),
                                          spread(hi[:, bass.ds(i * BODY + h * HALF, HALF)], 2, [P, HALF, NB]), ALU.is_equal).then_inc(hot_made[h], 1)
                n = S_PREV

                def step(ins):
                    nonlocal n
                    n += 1
                    ins.then_inc(prep, 1)
                    eng.wait_ge(prep, n)
                    return n

                eng.wait_ge(deg_done, 1)
                assert step(eng.tensor_copy(deg, ps[:, 7, 0:NB])) == S_DEG
                eng.wait_ge(cum_done, 1)
                step(eng.tensor_copy(tot, ps[:, 6, 64:64 + NB]))
                step(eng.tensor_tensor_scan(incl, ones_nb, tot, 0.0, ALU.mult, ALU.add))
                step(eng.tensor_tensor(incl, incl, tot, ALU.subtract))
                step(eng.tensor_tensor(end1, ps[:, 6, 0:NB], incl, ALU.add))
                step(eng.tensor_scalar(m.has[:, :], deg, 1.0, None, ALU.min))
                step(eng.tensor_tensor(tmp, end1, deg, ALU.subtract))
                step(eng.tensor_tensor(tmp, tmp, spare_start, ALU.subtract))
                step(eng.tensor_tensor(tmp, tmp, m.has[:, :], ALU.mult))
                assert step(eng.tensor_tensor(m.start[:, :], tmp, spare_start, ALU.add)) == S_START
                step(eng.scalar_tensor_tensor(out=tmp, in0=end1, scalar=float(-1 - EP), in1=m.has[:, :], op0=ALU.add, op1=ALU.mult))
                step(eng.tensor_scalar(m.end[:, :], tmp, float(EP), None, ALU.add))
                eng.wait_ge(l_prev, 16)
                step(eng.tensor_copy(prev_lastf, prev_last))
                assert step(eng.tensor_tensor(whole, dstf[:, T - 1:T], prev_lastf, ALU.is_equal)) == S_WHOLE
                step(eng.tensor_tensor(m.keep[:, 1:T], dstf[:, 1:T], dstf[:, 0:T - 1], ALU.is_equal))
                step(eng.tensor_tensor(m.keep[:, 0:1], dstf[:, 0:1], prev_lastf, ALU.is_equal))
                step(eng.memset(m.keep[:, T:T + BODY], 0.0))
                step(eng.tensor_scalar(m.reset[:, :], m.keep[:, :], -1.0, BIG, ALU.add, ALU.mult))
                step(eng.tensor_scalar(same, dstf, dstf[:, 0:1], None, ALU.is_equal))
                step(eng.tensor_reduce(count, same, AX.X, ALU.add))
                step(eng.tensor_tensor(firstf, count, lane_base, ALU.add))
                step(eng.tensor_copy(m.first_end[:, :], firstf))
                step(eng.tensor_tensor(firstf, firstf, spare_row, ALU.subtract))
                step(eng.tensor_tensor(firstf, firstf, m.keep[:, 0:1], ALU.mult))
                step(eng.tensor_tensor(m.first_fix[:, :], firstf, spare_row, ALU.add))
                step(eng.tensor_copy(m.lane_first[:, :], dst[:, 0:1]))
                eng.wait_ge(l_edge, 16 * 9)
                step(eng.tensor_copy(same, m.src[:, 0:T]))
                step(eng.tensor_copy(typf, typ))
                step(eng.scalar_tensor_tensor(out=m.src_rel[:, 0:T], in0=same, scalar=float(REL), in1=typf, op0=ALU.mult, op1=ALU.add))
                step(eng.memset(m.src_rel[:, T:T + AHEAD], 0))
                for r in range(REL):
                    step(eng.tensor_scalar(m.other_rel[:, :, r], typf, float(r), -BIG, ALU.not_equal, ALU.mult))
                eng.wait_ge(whole_done, 1)
                step(eng.tensor_scalar(m.whole_neg[:, :], ps[:, 5, 0:P], -1.0, BIG, ALU.add, ALU.mult))


S_DEG = 7
S_START = 16
S_WHOLE = 20
ZEROS = TURNS + 6
SMALL = len(COLUMNS) + 1 + len(ROWS) + 1 + 5 + 1


def layer0_edges(nc, m, I):
    with phase(nc, "layer0_edges") as sem:
        A = Arena(m)
        xr = [A(HALF, D) for _ in range(2)]
        xv = [A(SEVEN, D) for _ in range(2)]
        eq = [A(SEVEN, P) for _ in range(2)]
        before = A(SEVEN, P)
        rows = [A(SEVEN, D) for _ in range(4)]
        idx = [A(SEVEN, dt=I32) for _ in range(4)]
        srcs = A(BODY)
        vals = A(BODY)
        keeps = A(BODY)
        to_spare = A(BODY)
        rank = A(SEVEN)
        ranks = A(SEVEN)
        ps = m.psum

        def spread_bank(u):
            return ps[:, 2 * (u % 2):2 * (u % 2) + 2, :].rearrange("p a (b c) -> p (a b) c", c=P)[:, 0:SEVEN, :]

        def sum_bank(u):
            return ps[:, 4 + 2 * (u % 2):6 + 2 * (u % 2), :].rearrange("p a (b c) -> p (a b) c", c=P)[:, 0:SEVEN, :]

        first = sem("lane_first_row")
        landed = [sem(f"x_rows_landed{h}") for h in range(2)]
        carried = sem("x_carried")
        staged = sem("marks_staged")
        vals_staged = sem("weights_staged")
        weighed = sem("x_weighed")
        sources = sem("sources_spread")
        eq_made = sem("eq_made")
        ranked = sem("ranks")
        summed = sem("rows_summed")
        kept = sem("rows_kept")
        added = [sem(f"added{j}") for j in range(TABS)]
        UN = BODY // SEVEN
        RANK = 5

        zeros = A((NP + P) // P * D)
        cleared = sem("zeros_set")
        dst_cleared = sem("dst_scores_cleared")
        unit_added = sem("units_added")

        with nc.Block() as block:

            @block.sync
            def _(eng):
                def load(h, t):
                    eng.dma_start(xr[h], lanes(m.seg_rows)[:, t, :]).then_inc(landed[h], 16)

                load(0, bass.ds(0, HALF))
                with eng.Fori(0, TURNS - 1) as i:
                    hold(eng, carried, i * BODY + 2)
                    hold(eng, weighed, i * BODY + 1)
                    load(1, bass.ds(i * BODY + HALF, HALF))
                    hold(eng, carried, i * BODY + HALF + 2)
                    hold(eng, weighed, i * BODY + HALF + 1)
                    load(0, bass.ds(i * BODY + BODY, HALF))
                hold(eng, carried, (TURNS - 1) * BODY + 2)
                hold(eng, weighed, (TURNS - 1) * BODY + 1)
                load(1, bass.ds((TURNS - 1) * BODY + HALF, HALF))
                eng.wait_ge(cleared, 1)
                for k in range(RH // 4):
                    eng.dma_start(m.seg_dst[0:EP, :].rearrange("(p t) f -> p (t f)", p=P)[:, k * T * 4:(k + 1) * T * 4],
                                  zeros[:, 0:T * 4]).then_inc(dst_cleared, 16)
                eng.wait_ge(dst_cleared, 16 * (RH // 4))

            @block.gpsimd
            def _(eng):
                eng.indirect_dma_start(out=xr[1][:, HALF - 1, :], out_offset=None, in_=I["x"],
                                       in_offset=bass.IndirectOffsetOnAxis(ap=m.lane_first[:, 0:1], axis=0)).then_inc(first, 16)
                eng.wait_ge(cleared, 1)
                for j in range(TABS):
                    eng.dma_start(m.tabs[j].rearrange("(p r) f -> p (r f)", p=P), zeros).then_inc(added[j], 16)
                with eng.Fori(0, TURNS) as i:
                    for u in range(UN):
                        eng.wait_ge(kept, i * UN + u + 3)
                        eng.wait_ge(ranked, (i * UN + u + 1) * RANK + 1)
                        for k in range(SEVEN):
                            s = u * SEVEN + k
                            j = s % TABS
                            hold(eng, added[j], 16 * (i * (BODY // TABS) + s // TABS) + 16)
                            if k == TABS - 1:
                                eng.nop().then_inc(unit_added, 1)
                            eng.indirect_dma_start(out=m.tabs[j], out_offset=bass.IndirectOffsetOnAxis(ap=idx[u][:, k:k + 1], axis=0),
                                                   in_=rows[u][:, k, :], in_offset=None, compute_op=ALU.add).then_inc(added[j], 16)
                for j in range(TABS):
                    eng.wait_ge(added[j], 16 + 16 * (TURNS * BODY // TABS))

            @block.vector
            def _(eng):
                eng.memset(zeros, 0.0).then_inc(cleared, 1)
                eng.engine_nop().then_inc(unit_added, UN)
                eng.engine_nop().then_inc(carried, 1)
                eng.engine_nop().then_inc(ranked, 1)
                eng.engine_nop().then_inc(eq_made, 2)
                eng.wait_ge(first, 16)
                with eng.Fori(0, TURNS) as i:
                    eng.wait_ge(carried, i * BODY + 1)
                    hold(eng, ranked, i * UN * RANK + 1)
                    eng.tensor_copy(keeps, m.keep[:, bass.ds(i * BODY, BODY)]).then_inc(staged, 1)
                    eng.tensor_copy(srcs, m.src[:, bass.ds(i * BODY, BODY)]).then_inc(staged, 1)
                    eng.wait_ge(staged, 3 * i + 2)
                    eng.tensor_scalar(to_spare, srcs, -1.0, m.spare[:, 0:1], ALU.mult, ALU.add).then_inc(staged, 1)
                    eng.wait_ge(staged, 3 * i + 3)
                    for u in range(UN):
                        h = u // 2
                        if u % 2 == 0:
                            eng.wait_ge(landed[h], 16 * i + 16)
                        for k in range(SEVEN):
                            s = u * SEVEN + k
                            j = s % HALF
                            prev = xr[h][:, j - 1, :] if j else xr[1 - h][:, HALF - 1, :]
                            eng.wait_ge(carried, i * BODY + s + 1)
                            eng.scalar_tensor_tensor(out=xr[h][:, j, :], in0=prev, scalar=keeps[:, s:s + 1], in1=xr[h][:, j, :],
                                                     op0=ALU.mult, op1=ALU.add).then_inc(carried, 1)
                        eng.wait_ge(sources, i * UN + u + 1)
                        eng.wait_ge(summed, i * UN + u + 1)
                        eng.tensor_tensor(eq[u % 2], spread_bank(u), spread(srcs[:, u * SEVEN:(u + 1) * SEVEN], 2, [P, SEVEN, P]),
                                          ALU.is_equal).then_inc(eq_made, 1)
                        eng.wait_ge(eq_made, i * UN + u + 3)
                        eng.wait_ge(ranked, (i * UN + u) * RANK + 1)
                        at = (i * UN + u) * RANK
                        eng.tensor_tensor(before, eq[u % 2], spread(m.lower[:, :], 1, [P, SEVEN, P]), ALU.mult).then_inc(ranked, 1)
                        eng.wait_ge(ranked, at + 2)
                        eng.tensor_reduce(rank, before, AX.X, ALU.add).then_inc(ranked, 1)
                        eng.wait_ge(ranked, at + 3)
                        eng.tensor_scalar(ranks, rank, 1.0, None, ALU.min).then_inc(ranked, 1)
                        eng.wait_ge(ranked, at + 4)
                        eng.tensor_tensor(ranks, ranks, to_spare[:, u * SEVEN:(u + 1) * SEVEN], ALU.mult).then_inc(ranked, 1)
                        eng.wait_ge(ranked, at + 5)
                        eng.wait_ge(unit_added, i * UN + u + 2)
                        eng.tensor_tensor(idx[u], ranks, srcs[:, u * SEVEN:(u + 1) * SEVEN], ALU.add).then_inc(ranked, 1)

            @block.tensor
            def _(eng):
                eng.nop().then_inc(summed, 2)
                with eng.Fori(0, TURNS) as i:
                    eng.wait_ge(staged, 3 * i + 3)
                    for u in range(UN + 1):
                        if u < UN:
                            eng.wait_ge(eq_made, i * UN + u + 1)
                            for k in range(SEVEN):
                                s = u * SEVEN + k
                                t = eng.matmul(spread_bank(u)[:, k, :], srcs[:, s:s + 1].broadcast_to([P, P]), m.ident[:, :], start=True, stop=True)
                            t.then_inc(sources, 1)
                        if u > 0:
                            v = u - 1
                            eng.wait_ge(eq_made, i * UN + v + 3)
                            eng.wait_ge(weighed, i * BODY + (v + 1) * SEVEN + 1)
                            eng.wait_ge(kept, i * UN + v + 1)
                            for k in range(SEVEN):
                                t = eng.matmul(sum_bank(v)[:, k, :], eq[v % 2][:, k, :], xv[v % 2][:, k, :], start=True, stop=True)
                            t.then_inc(summed, 1)

            @block.scalar
            def _(eng):
                eng.nop().then_inc(weighed, 1)
                eng.nop().then_inc(kept, 2)
                with eng.Fori(0, TURNS) as i:
                    eng.activation(vals, m.val[:, bass.ds(i * BODY, BODY)], ACT.Copy).then_inc(vals_staged, 1)
                    eng.wait_ge(vals_staged, i + 1)
                    for u in range(UN + 1):
                        if u < UN:
                            eng.wait_ge(carried, i * BODY + (u + 1) * SEVEN + 1)
                            for k in range(SEVEN):
                                s = u * SEVEN + k
                                eng.activation(xv[u % 2][:, k, :], xr[s // HALF][:, s % HALF, :], ACT.Copy, scale=vals[:, s:s + 1]).then_inc(weighed, 1)
                        if u > 0:
                            v = u - 1
                            eng.wait_ge(summed, i * UN + v + 3)
                            eng.wait_ge(unit_added, i * UN + v + 2)
                            eng.activation(rows[v], sum_bank(v), ACT.Copy).then_inc(kept, 1)


class Steps:

    def __init__(self, eng, sem, start=0):
        self.eng, self.sem, self.n = eng, sem, start

    def put(self, ins):
        ins.then_inc(self.sem, 1)
        self.n += 1

    def wait(self):
        self.eng.wait_ge(self.sem, self.n)

    def then(self, ins):
        self.put(ins)
        self.wait()


def turn_out(eng, ps, nodes, turned, kept, ident, bank):
    for k, (c, w) in enumerate(CHUNKS):
        if k >= 2:
            eng.wait_ge(kept, k - 1)
        for b in range(w // P):
            t = eng.transpose(ps[:, bank + k % 2, b * P:b * P + P], nodes[:, c // P + b, :], ident)
        t.then_inc(turned, 1)


def turn_in(eng, ps, out, turned, kept, bank):
    for k, (c, w) in enumerate(CHUNKS):
        eng.wait_ge(turned, k + 1)
        eng.activation(out[:, c:c + w], ps[:, bank + k % 2, 0:w], ACT.Copy).then_inc(kept, 1)


def layer0_nodes(nc, m, I):
    with phase(nc, "layer0_nodes") as sem:
        A = Arena(m)
        big = A(8 * NP)
        agg = [big[:, j * NP:(j + 1) * NP].rearrange("p (b f) -> p b f", f=D) for j in range(TABS)]
        aggT, uT, rT, oT = (big[:, j * NP:(j + 1) * NP] for j in range(4, 8))
        fT, hT, gT, h2T = (big[:, j * NP:(j + 1) * NP] for j in (1, 2, 3, 1))
        y = agg[0]
        bias = A(3)
        st_b = A(len(REALCH), 6)
        mv_b = A(2)
        sd_b, scale, shift = A(1), A(1), A(1)
        st_n = A(NB, 6)
        mv_n = A(NB, 2)
        sd_n = A(NB)
        attn = A(2, REL * D)
        fold = A(REL * D)
        w_att = A(2 * RH)
        ed = A(NB, RH)
        tab = [A(REL, HS) for _ in range(2)]
        ps = m.psum
        wt, col = m.wt, m.cols

        def c(name):
            k = COLUMNS.index(name)
            return col[:, k:k + 1]

        def w(name):
            return wt[:, TRANSPOSED.index(name), :]

        tabs_in = [sem(f"table_landed{j}") for j in range(TABS)]
        attn_in = sem("attention_landed")
        vec = sem("vector_steps")
        agg_made = sem("agg_made")
        agg_t, agg_k = sem("agg_turned"), sem("agg_kept")
        u_sum, u_made = sem("u_summed"), sem("u_made")
        r_sum, r_made, rx_made = sem("r_summed"), sem("r_made"), sem("rx_made")
        f_sum, f_made, o_made = sem("f_summed"), sem("f_made"), sem("o_made")
        var1, root1, scale1 = sem("variance1"), sem("root1"), sem("scale1")
        h_made = sem("h_made")
        g_sum, g_made = sem("g_summed"), sem("g_made")
        var2, root2, scale2 = sem("variance2"), sem("root2"), sem("scale2")
        h2_made = sem("h2_made")
        y_sum, y_made = sem("y_summed"), sem("y_made")
        varn, rootn, x_made = sem("node_variance"), sem("node_root"), sem("x_made")
        x_t, x_k = sem("x_turned2"), sem("x_kept2")
        att_made = sem("attention_folded")
        tab_sum, tab_h, tab_e = sem("table_summed"), sem("table_features"), sem("table_scores")
        ed_made = sem("dst_scores")
        stored = [sem(f"table_stored{k}") for k in range(2)]
        ed_stored, scattered = sem("dst_scores_stored"), sem("dst_scores_scattered")
        NCH = len(CHUNKS)

        with nc.Block() as block:

            @block.sync
            def _(eng):
                for j in range(TABS):
                    eng.dma_start(agg[j], m.tabs[j][0:NP, :].rearrange("(b p) f -> p b f", p=P)).then_inc(tabs_in[j], 16)
                for k, name in enumerate(("L1_gnn_attn_src", "L1_gnn_attn_dst")):
                    eng.dma_start(attn[:, k, :], I[name].rearrange("r h d -> (r h d)").partition_broadcast(P)).then_inc(attn_in, 16)
                for b in range(NB):
                    eng.wait_ge(tab_h, b + 1)
                    eng.wait_ge(tab_e, b + 1)
                    eng.dma_start(m.table1.rearrange("(b p r) f -> b p r f", p=P, r=REL)[b], tab[b % 2]).then_inc(stored[b % 2], 16)
                eng.wait_ge(ed_made, NB)
                eng.dma_start(m.dst1.rearrange("(b p) f -> p b f", p=P), ed).then_inc(ed_stored, 16)
                eng.wait_ge(ed_stored, 16)
                for k in range(2):
                    eng.wait_ge(stored[k], 16 * len(range(k, NB, 2)))

            @block.gpsimd
            def _(eng):
                eng.wait_ge(ed_made, NB)
                for b in range(NB):
                    eng.indirect_dma_start(out=m.seg_dst, out_offset=bass.IndirectOffsetOnAxis(ap=m.start[:, b:b + 1], axis=0),
                                           in_=ed[:, b, :], in_offset=None).then_inc(scattered, 16)
                eng.wait_ge(scattered, 16 * NB)

            @block.tensor
            def _(eng):
                def pair(bank, cw, first, x1, second, x2):
                    k, (at, n) = cw
                    eng.matmul(ps[:, bank + k % 2, 0:n], first, x1[:, at:at + n], start=True, stop=False)
                    return eng.matmul(ps[:, bank + k % 2, 0:n], second, x2[:, at:at + n], start=False, stop=True)

                eng.wait_ge(agg_made, 1)
                turn_out(eng, ps, agg[0], agg_t, agg_k, m.ident[:, :], 0)
                for k, cw in enumerate(CHUNKS):
                    eng.wait_ge(agg_k, k + 1)
                    if k >= 2:
                        eng.wait_ge(u_made, k - 1)
                        eng.wait_ge(r_made, k - 1)
                    pair(2, (k, cw), w("L0_gnn_W1w"), aggT, w("L0_gnn_U1w"), m.xT).then_inc(u_sum, 1)
                    pair(4, (k, cw), w("L0_gnn_W2w"), aggT, w("L0_gnn_U2w"), m.xT).then_inc(r_sum, 1)
                for k, cw in enumerate(CHUNKS):
                    eng.wait_ge(rx_made, k + 1)
                    if k >= 2:
                        eng.wait_ge(f_made, k - 1)
                    pair(6, (k, cw), w("L0_gnn_W3w"), aggT, w("L0_gnn_U3w"), rT).then_inc(f_sum, 1)
                eng.wait_ge(agg_k, NCH)
                for k, (at, n) in enumerate(CHUNKS):
                    eng.wait_ge(h_made, k + 1)
                    if k >= 2:
                        eng.wait_ge(g_made, k - 1)
                    eng.matmul(ps[:, k % 2, 0:n], w("L0_gnn_m_w0"), hT[:, at:at + n], start=True, stop=True).then_inc(g_sum, 1)
                eng.wait_ge(u_made, NCH)
                for k, (at, n) in enumerate(CHUNKS):
                    eng.wait_ge(h2_made, k + 1)
                    if k >= 2:
                        eng.wait_ge(y_made, k - 1)
                    for b in range(n // P):
                        t = eng.matmul(ps[:, 2 + k % 2, b * P:b * P + P], h2T[:, at + b * P:at + b * P + P], w("L0_gnn_m_w1"), start=True, stop=True)
                    t.then_inc(y_sum, 1)
                eng.wait_ge(x_made, 1)
                eng.wait_ge(g_made, NCH)
                turn_out(eng, ps, m.xN, x_t, x_k, m.ident[:, :], 0)
                eng.wait_ge(att_made, 1)
                eng.wait_ge(r_made, NCH)
                eng.wait_ge(f_made, NCH)
                for b in range(NB):
                    eng.wait_ge(x_k, b // 4 + 1)
                    if b >= 2:
                        eng.wait_ge(tab_h, b - 1)
                        eng.wait_ge(ed_made, b - 1)
                    xb = m.xT[:, b * P:b * P + P]
                    eng.matmul(ps[:, 4 + b % 2, :], xb, m.w_rel[:, :, :].rearrange("p r f -> p (r f)"), start=True, stop=True)
                    eng.matmul(ps[:, 6 + b % 2, 0:2 * RH], xb, w_att, start=True, stop=True).then_inc(tab_sum, 1)

            @block.scalar
            def _(eng):
                turn_in(eng, ps, aggT, agg_t, agg_k, 0)
                eng.wait_ge(vec, 3)
                for k, (at, n) in enumerate(CHUNKS):
                    eng.wait_ge(u_sum, k + 1)
                    eng.activation(uT[:, at:at + n], ps[:, 2 + k % 2, 0:n], ACT.Relu, bias=bias[:, 0:1]).then_inc(u_made, 1)
                    eng.wait_ge(r_sum, k + 1)
                    eng.activation(rT[:, at:at + n], ps[:, 4 + k % 2, 0:n], ACT.Relu, bias=bias[:, 1:2]).then_inc(r_made, 1)
                for k, (at, n) in enumerate(CHUNKS):
                    eng.wait_ge(f_sum, k + 1)
                    eng.activation(fT[:, at:at + n], ps[:, 6 + k % 2, 0:n], ACT.Tanh, bias=bias[:, 2:3]).then_inc(f_made, 1)
                eng.wait_ge(var1, 1)
                eng.activation(sd_b, mv_b[:, 1:2], ACT.Sqrt, bias=m.eps[:, 0:1]).then_inc(root1, 1)
                eng.wait_ge(scale1, 1)
                for k, (at, n) in enumerate(CHUNKS):
                    eng.activation(hT[:, at:at + n], oT[:, at:at + n], ACT.Relu, bias=shift, scale=scale).then_inc(h_made, 1)
                for k, (at, n) in enumerate(CHUNKS):
                    eng.wait_ge(g_sum, k + 1)
                    eng.activation(gT[:, at:at + n], ps[:, k % 2, 0:n], ACT.Identity, bias=c("L0_gnn_m_b0")).then_inc(g_made, 1)
                eng.wait_ge(var2, 1)
                eng.activation(sd_b, mv_b[:, 1:2], ACT.Sqrt, bias=m.eps[:, 0:1]).then_inc(root2, 1)
                eng.wait_ge(scale2, 1)
                for k, (at, n) in enumerate(CHUNKS):
                    eng.activation(h2T[:, at:at + n], gT[:, at:at + n], ACT.Relu, bias=shift, scale=scale).then_inc(h2_made, 1)
                eng.wait_ge(varn, 1)
                eng.activation(sd_n, mv_n[:, :, 1], ACT.Sqrt, bias=m.eps[:, 0:1]).then_inc(rootn, 1)
                turn_in(eng, ps, m.xT, x_t, x_k, 0)
                for b in range(NB):
                    eng.wait_ge(tab_sum, b + 1)
                    if b >= 2:
                        eng.wait_ge(stored[b % 2], 16 * (b // 2))
                    eng.activation(tab[b % 2][:, :, 0:D], ps[:, 4 + b % 2, :].rearrange("p (r f) -> p r f", f=D), ACT.Copy).then_inc(tab_h, 1)

            @block.vector
            def _(eng):
                v = Steps(eng, vec)
                for k, (a, b) in enumerate((("W1b", "U1b"), ("W2b", "U2b"), ("W3b", "U3b"))):
                    v.put(eng.tensor_tensor(bias[:, k:k + 1], c("L0_gnn_" + a), c("L0_gnn_" + b), ALU.add))
                eng.wait_ge(attn_in, 32)
                for k in range(2):
                    v.then(eng.tensor_tensor(fold, m.w_rel[:, :, :].rearrange("p r f -> p (r f)"), attn[:, k, :], ALU.mult))
                    v.then(eng.tensor_reduce(w_att[:, k * RH:(k + 1) * RH], fold.rearrange("p (a d) -> p a d", d=D1), AX.X, ALU.add))
                eng.engine_nop().then_inc(att_made, 1)
                for j in range(TABS):
                    eng.wait_ge(tabs_in[j], 16)
                    if j:
                        v.then(eng.tensor_tensor(agg[0], agg[0], agg[j], ALU.add))
                eng.engine_nop().then_inc(agg_made, 1)
                for k, (at, n) in enumerate(CHUNKS):
                    eng.wait_ge(r_made, k + 1)
                    eng.tensor_tensor(rT[:, at:at + n], rT[:, at:at + n], m.xT[:, at:at + n], ALU.mult).then_inc(rx_made, 1)
                for k, (at, n) in enumerate(CHUNKS):
                    f, o, x, u = (t[:, at:at + n] for t in (fT, oT, m.xT, uT))
                    eng.wait_ge(f_made, k + 1)
                    v.then(eng.tensor_tensor(f, f, x, ALU.subtract))
                    v.then(eng.tensor_tensor(f, f, u, ALU.mult))
                    eng.tensor_tensor(o, f, x, ALU.add).then_inc(o_made, 1)
                v.then(eng.tensor_tensor(m.xN[:, :, :], m.xN[:, :, :], spread(m.rows[:, ROWS.index("L0_gnn_m_b1"), :], 1, [P, NB, D]), ALU.add))
                for made, var, root, scaled, x, g, b in ((o_made, var1, root1, scale1, oT, "L0_gnn_bn_g", "L0_gnn_bn_b"),
                                                         (g_made, var2, root2, scale2, gT, "L0_gnn_m_bng", "L0_gnn_m_bnb")):
                    for k, (at, n) in enumerate(REALCH):
                        eng.wait_ge(made, k + 1)
                        v.put(eng.bn_stats(st_b[:, k, :], x[:, at:at + n]))
                    v.wait()
                    eng.bn_aggr(mv_b, st_b).then_inc(var, 1)
                    eng.wait_ge(root, 1)
                    v.then(eng.reciprocal(sd_b, sd_b))
                    v.then(eng.tensor_tensor(scale, sd_b, c(g), ALU.mult))
                    v.then(eng.tensor_tensor(sd_b, mv_b[:, 0:1], scale, ALU.mult))
                    eng.tensor_tensor(shift, c(b), sd_b, ALU.subtract).then_inc(scaled, 1)
                    eng.wait_ge(scaled, 1)
                for k, (at, n) in enumerate(CHUNKS):
                    eng.wait_ge(y_sum, k + 1)
                    b0, b1 = at // P, (at + n) // P
                    eng.tensor_tensor(y[:, b0:b1, :], ps[:, 2 + k % 2, 0:n].rearrange("p (b f) -> p b f", f=D), m.xN[:, b0:b1, :], ALU.add).then_inc(y_made, 1)
                eng.wait_ge(y_made, NCH)
                for b in range(NB):
                    v.put(eng.bn_stats(st_n[:, b, :], y[:, b, :]))
                v.wait()
                for b in range(NB):
                    v.put(eng.bn_aggr(mv_n[:, b, :], st_n[:, b, :]))
                v.wait()
                eng.engine_nop().then_inc(varn, 1)
                eng.wait_ge(rootn, 1)
                v.then(eng.reciprocal(sd_n, sd_n))
                for b in range(NB):
                    v.put(eng.tensor_scalar(m.xN[:, b, :], y[:, b, :], mv_n[:, b, 0:1], sd_n[:, b:b + 1], ALU.subtract, ALU.mult))
                v.wait()
                eng.engine_nop().then_inc(x_made, 1)
                for b in range(NB):
                    eng.wait_ge(tab_sum, b + 1)
                    if b >= 2:
                        eng.wait_ge(stored[b % 2], 16 * (b // 2))
                    sc = ps[:, 6 + b % 2, 0:2 * RH]
                    eng.tensor_copy(tab[b % 2][:, :, D:HS], sc[:, 0:RH].rearrange("p (r h) -> p r h", h=H1)).then_inc(tab_e, 1)
                    eng.tensor_copy(ed[:, b, :], sc[:, RH:2 * RH]).then_inc(ed_made, 1)


class LoopSteps(Steps):

    def __init__(self, eng, sem, before):
        Steps.__init__(self, eng, sem)
        self.before = before

    def wait(self):
        self.eng.wait_ge(self.sem, self.before + self.n)


FLOOR = -1e28
COLS = HALF + 1


def maxima_step(eng, step, resets, e, fwd, top, gap):
    n = fwd.shape[1] * COLS

    def flat(t):
        return t.rearrange("p a t -> p (a t)")

    if step == 0:
        return eng.tensor_copy(e[:, :, 0:1], fwd[:, :, HALF:COLS])
    if step == 1:
        return eng.tensor_tensor_scan(flat(fwd), resets[:, 0:n], flat(e), -BIG, ALU.add, ALU.max)
    if step == 2:
        return eng.tensor_tensor_scan(flat(top)[:, ::-1], resets[:, 1:n + 1][:, ::-1], flat(fwd)[:, ::-1], -BIG, ALU.add, ALU.max)
    return eng.scalar_tensor_tensor(out=gap, in0=top, scalar=FLOOR, in1=e, op0=ALU.max, op1=ALU.subtract)


SCORES1 = 3 + 4
OLD1 = 3
SUMS1 = OLD1 + HALF
BY_DVE = 10
MASKED1 = REL * HALF - BY_DVE
WEIGHED1 = 3


def layer1_edges(nc, m, I):
    with phase(nc, "layer1_edges") as sem:
        A = Arena(m)
        states = A(2 * HALF * R1)
        rows = [states[:, h * HALF * R1:(h + 1) * HALF * R1].rearrange("p (t f) -> p t f", f=R1) for h in range(2)]
        ed_all = states[:, 0:T * RH].rearrange("p (t f) -> p t f", f=RH)
        ed = A(T, H1)
        apart = A(HALF, REL * D)
        feat = [A(HALF, HS) for _ in range(RING - 1)]
        W = HALF * HS
        feat.append(m.xT[:, 0:W].rearrange("p (t f) -> p t f", f=HS))
        e, fwd, *top = ([m.xT[:, W + k * RH * COLS:W + (k + 1) * RH * COLS].rearrange("p (a t) -> p a t", t=COLS) for k in range(5)]
                        + [A(RH, COLS)])
        gap = [A(RH, COLS) for _ in range(2)]
        ex = [A(RH, COLS) for _ in range(2)]
        sums = [A(RH, COLS) for _ in range(2)]
        weight = A(HALF, H1)
        score4 = A(HALF, H1)
        old = m.lane_end[:, 0:REL * D]
        keeps = [A(HALF) for _ in range(2)]
        all_keeps = [A(RH * COLS) for _ in range(2)]
        resets = [A(RH * COLS + 1) for _ in range(2)]
        hot = [A(HALF, REL) for _ in range(2)]
        idx = [A(HALF, dt=I32) for _ in range(RING)]
        ed_first = A(RH)
        SUM, MAX = REL * D, REL * D + RH

        ed_in, ed_first_in = sem("dst_scores_landed"), sem("first_scores_landed")
        begun, ed_steps = sem("buffers_begun"), sem("dst_scores_steps")
        scored, weighed, summed = sem("score_steps"), sem("weight_steps"), sem("sum_steps")
        exped, hot_made, masked, filled = sem("exponentials"), sem("relations_staged"), sem("features_apart"), sem("state_columns_filled")
        marks, kept = sem("resets_staged"), sem("keeps_staged")
        staged = [sem(f"indices_staged{k}") for k in range(RING)]
        landed = [sem(f"features_landed{k}") for k in range(RING)]
        stored, rows_free = sem("states_stored"), sem("states_free")

        def nth(i, k):
            return i * RING + k

        def half(i, k):
            return (i + k // RING, k % RING)

        def sums_before(i, k):
            return i * (RING * SUMS1) + (k + 1) * SUMS1

        def weighed_before(i, k):
            return i * (RING * WEIGHED1) + (RING + k) * WEIGHED1

        def masked_before(i, k):
            return i * (RING * MASKED1) + (RING + k) * MASKED1

        def edges(i, k):
            return bass.ds(i * (RING * HALF) + k * HALF, HALF)

        def inner(t):
            return t[:, :, 1:COLS].rearrange("p a t -> p t a")

        with nc.Block() as block:

            @block.sync
            def _(eng):
                eng.dma_start(ed_all.rearrange("p t f -> p (t f)"), lanes(m.seg_dst).rearrange("p t f -> p (t f)")).then_inc(ed_in, 16)
                with eng.Fori(0, LOOPS) as i:
                    for k in range(RING):
                        hold(eng, summed, sums_before(i, k) + SUMS1)
                        hold(eng, filled, 2 * nth(i, k) + 4)
                        eng.dma_start(lanes(m.rows1)[:, edges(i, k), :], rows[k % 2]).then_inc(stored, 16)
                        hold(eng, stored, 16 * RING * i + 16 * k + 16)
                        eng.nop().then_inc(rows_free, 1)

            @block.gpsimd
            def _(eng):
                eng.indirect_dma_start(out=ed_first, out_offset=None, in_=m.dst1,
                                       in_offset=bass.IndirectOffsetOnAxis(ap=m.lane_first[:, 0:1], axis=0)).then_inc(ed_first_in, 16)
                with eng.Fori(0, LOOPS) as i:
                    for k in range(RING):
                        hold(eng, staged[k], i + 1)
                        hold(eng, masked, masked_before(i, k) - (RING - 1) * MASKED1)
                        hold(eng, weighed, weighed_before(i, k) - (RING - 1) * WEIGHED1)
                        for j in range(HALF):
                            eng.indirect_dma_start(out=feat[k][:, j, :], out_offset=None, in_=m.table1,
                                                   in_offset=bass.IndirectOffsetOnAxis(ap=idx[k][:, j:j + 1], axis=0)).then_inc(landed[k], 16)

            @block.scalar
            def _(eng):
                def over_heads(t):
                    return t[:, 0:RH * COLS].rearrange("p (a t) -> p a t", t=COLS)[:, :, 1:COLS]

                def stage_resets(i, k):
                    eng.activation(over_heads(resets[k % 2]), spread(m.reset[:, edges(i, k)], 1, [P, RH, HALF]), ACT.Copy).then_inc(marks, 1)

                def stage_keeps(i, k):
                    eng.activation(over_heads(all_keeps[k % 2]), spread(m.keep[:, edges(i, k)], 1, [P, RH, HALF]), ACT.Copy).then_inc(kept, 1)
                    eng.activation(keeps[k % 2], m.keep[:, edges(i, k)], ACT.Copy).then_inc(kept, 1)

                def fill(k):
                    eng.activation(rows[k % 2][:, :, SUM:MAX], inner(sums[k % 2]), ACT.Copy).then_inc(filled, 1)
                    eng.activation(rows[k % 2][:, :, MAX:R1], inner(top[k]), ACT.Copy).then_inc(filled, 1)

                for k in range(RING):
                    eng.activation(idx[k], m.src_rel[:, k * HALF:(k + 1) * HALF], ACT.Copy).then_inc(staged[k], 1)
                eng.nop().then_inc(masked, RING * MASKED1)
                eng.wait_ge(begun, 8)
                for k in range(2):
                    stage_resets(0, k)
                stage_keeps(0, 0)

                def exponentials(i, k):
                    hold(eng, landed[k], 16 * HALF * (i + 1))
                    eng.activation(idx[k], m.src_rel[:, edges(i, RING + k)], ACT.Copy).then_inc(staged[k], 1)
                    hold(eng, scored, SCORES1 * nth(i, k) + SCORES1 + 1)
                    hold(eng, masked, masked_before(i, k) - MASKED1)
                    eng.activation(hot[k % 2], m.other_rel[:, edges(i, k), :], ACT.Relu, bias=m.ones[:, 0:1]).then_inc(hot_made, 1)
                    eng.activation(ex[k % 2], gap[k % 2], ACT.Exp, scale=-1.0).then_inc(exped, 1)
                    stage_resets(*half(i, k + 2))

                def set_apart(i, k, ts):
                    for t in ts:
                        eng.wait_ge(summed, sums_before(i, k) - SUMS1 + OLD1 + t + 1)
                        for r in range(REL - (t < BY_DVE)):
                            eng.activation(apart[:, t, r * D:(r + 1) * D], feat[k][:, t, 0:D], ACT.Copy, scale=hot[k % 2][:, t, r:r + 1]).then_inc(masked, 1)

                def turn(i, last):
                    for k in range(RING):
                        eng.wait_ge(hot_made, nth(i, k) + 1)
                        eng.wait_ge(weighed, weighed_before(i, k) + 2)
                        set_apart(i, k, range(HALF // 2))
                        if k + 1 < RING or not last:
                            exponentials(*half(i, k + 1))
                        set_apart(i, k, range(HALF // 2, HALF))
                        hold(eng, summed, sums_before(i, k))
                        stage_keeps(*half(i, k + 1))
                        eng.wait_ge(rows_free, nth(i, k) + 1)
                        fill((k - 1) % RING)

                exponentials(0, 0)
                with eng.Fori(0, LOOPS - 1) as i:
                    turn(i, False)
                turn(LOOPS - 1, True)
                eng.wait_ge(summed, sums_before(LOOPS, 0))
                fill(RING - 1)

            @block.vector
            def _(eng):
                f = Steps(eng, begun)
                for h in range(2):
                    f.put(eng.memset(resets[h], -BIG))
                    f.put(eng.memset(all_keeps[h], 0.0))
                    f.put(eng.memset(sums[h], 0.0))
                f.put(eng.memset(fwd, -BIG))
                f.put(eng.memset(top[RING - 1], -BIG))
                eng.engine_nop().then_inc(rows_free, 3)
                eng.engine_nop().then_inc(scored, 1)
                eng.engine_nop().then_inc(weighed, RING * WEIGHED1)
                eng.engine_nop().then_inc(summed, SUMS1)
                eng.wait_ge(ed_in, 16)
                eng.wait_ge(ed_first_in, 16)
                for k in range(RH):
                    w = eng.tensor_tensor_scan(ed_all[:, :, k], m.keep[:, 0:T], ed_all[:, :, k], ed_first[:, k:k + 1], ALU.mult, ALU.add)
                    w.then_inc(ed_steps, 1)
                eng.wait_ge(ed_steps, RH)
                ed4 = ed_all.rearrange("p t (r a) -> p t r a", a=H1)
                eng.tensor_tensor(ed4, ed4, spread(m.other_rel[:, :, :], 3, [P, T, REL, H1]), ALU.add).then_inc(ed_steps, 1)
                eng.wait_ge(ed_steps, RH + 1)
                f.then(eng.tensor_reduce(ed, ed_all.rearrange("p t (r a) -> p t a r", a=H1), AX.X, ALU.max))
                f.then(eng.memset(rows[1][:, HALF - 1, :], 0.0))

                def score(i, k, step):
                    now, n = e[:, :, 1:COLS], RH * COLS
                    eng.wait_ge(scored, SCORES1 * nth(i, k) + step + 1)
                    if step == 0:
                        eng.wait_ge(landed[k], 16 * HALF * (i + 1))
                        eng.wait_ge(marks, nth(i, k) + 1)
                        ins = eng.tensor_tensor(score4, feat[k][:, :, D:HS], ed[:, edges(i, k), :], ALU.add)
                    elif step == 1:
                        ins = eng.scalar_tensor_tensor(out=score4, in0=score4, scalar=0.2, in1=score4, op0=ALU.mult, op1=ALU.max)
                    elif step == 2:
                        ins = eng.tensor_tensor(now.rearrange("p (r a) t -> p t r a", a=H1), spread(score4, 2, [P, HALF, REL, H1]),
                                                spread(m.other_rel[:, edges(i, k), :], 3, [P, HALF, REL, H1]), ALU.add)
                    else:
                        ins = maxima_step(eng, step - 3, resets[k % 2], e, fwd, top[k], gap[k % 2])
                    ins.then_inc(scored, 1)

                def weigh(i, k, step):
                    if step == 0:
                        eng.wait_ge(exped, nth(i, k) + 1)
                        eng.tensor_reduce(weight, ex[k % 2][:, :, 1:COLS].rearrange("p (r a) t -> p t a r", a=H1), AX.X, ALU.add).then_inc(weighed, 1)
                    elif step > 1:
                        eng.wait_ge(weighed, weighed_before(i, k) + step)
                        eng.wait_ge(hot_made, nth(i, k) + 1)
                        eng.tensor_tensor(apart[:, 0:BY_DVE, (REL - 1) * D:], feat[k][:, 0:BY_DVE, 0:D],
                                          hot[k % 2][:, 0:BY_DVE, REL - 1:REL].broadcast_to([P, BY_DVE, D]), ALU.mult).then_inc(weighed, 1)
                    else:
                        eng.wait_ge(weighed, weighed_before(i, k) + 1)
                        by_head = feat[k][:, :, 0:D].rearrange("p t (a d) -> p t a d", d=D1)
                        eng.tensor_tensor(by_head, by_head, spread(weight, 3, [P, HALF, H1, D1]), ALU.mult).then_inc(weighed, 1)

                def add_up(i, k, weighs=True, scores=True):
                    v = LoopSteps(eng, summed, sums_before(i, k))
                    h = k % 2
                    row, before = rows[h], rows[1 - h][:, HALF - 1, :]
                    eng.wait_ge(rows_free, nth(i, k) + 2)
                    eng.wait_ge(kept, 2 * nth(i, k) + 2)
                    v.put(eng.tensor_tensor(old.rearrange("p (a d) -> p a d", d=D1), before[:, 0:SUM].rearrange("p (a d) -> p a d", d=D1),
                                            ex[h][:, :, 0:1].broadcast_to([P, RH, D1]), ALU.mult))
                    v.wait()
                    v.then(eng.tensor_tensor(ex[h][:, :, 0], ex[h][:, :, 0], sums[1 - h][:, :, HALF], ALU.mult))
                    v.put(eng.tensor_tensor_scan(sums[h].rearrange("p a t -> p (a t)"), all_keeps[h], ex[h].rearrange("p a t -> p (a t)"), 0.0, ALU.mult, ALU.add))
                    for j in range(HALF):
                        eng.wait_ge(masked, masked_before(i, k) + REL * (j + 1) - min(j + 1, BY_DVE))
                        if j == 0:
                            eng.wait_ge(weighed, weighed_before(i, k) + WEIGHED1)
                        v.wait()
                        v.put(eng.scalar_tensor_tensor(out=row[:, j, 0:SUM], in0=row[:, j - 1, 0:SUM] if j else old, scalar=keeps[h][:, j:j + 1],
                                                       in1=apart[:, j, :], op0=ALU.mult, op1=ALU.add))
                        if scores and j < SCORES1:
                            score(*half(i, k + 2), j)
                        if weighs and j == BY_DVE:
                            weigh(*half(i, k + 1), 2)
                        if scores and j >= HALF - 2:
                            weigh(*half(i, k + 2), j - (HALF - 2))
                    v.wait()
                    assert v.n == SUMS1

                for k in range(2):
                    for step in range(SCORES1):
                        score(0, k, step)
                for step in range(WEIGHED1):
                    weigh(0, 0, step)
                for step in range(2):
                    weigh(0, 1, step)
                with eng.Fori(0, LOOPS - 1) as i:
                    for k in range(RING):
                        add_up(i, k)
                for k in range(RING):
                    add_up(LOOPS - 1, k, weighs=k + 1 < RING, scores=k + 2 < RING)
                eng.wait_ge(filled, 2 * nth(LOOPS, 0) + 2)
                f.then(eng.tensor_copy(m.lane_end[:, 0:R1], rows[1][:, HALF - 1, :]))


def carry_sums(nc, m, states, chunks, heads):
    with phase(nc, f"carry_sums_{heads}") as sem:
        A = Arena(m)
        W, C, H, DH = chunks * P, chunks, heads, P // heads
        R = W + 2 * C * H
        wide = [A(3, P) for _ in range(C)]
        run = [A(3, P + 1) for _ in range(C)]
        ex = [A(2, P) for _ in range(C)]
        add = [A(2, P) for _ in range(C)]
        row = A(R)
        new_max = A(C * H)
        dm = A(2, C * H)
        part = A(W + C * H)
        ps = m.psum

        row_in, fixed = sem("first_rows_landed"), sem("first_rows_fixed")
        vec = sem("vector_steps")
        wide_made, turned = sem("states_spread"), sem("states_turned")
        exps_of, exped = sem("exponents"), sem("exponentials")
        run_made, back = sem("lanes_summed"), sem("lane_sums_turned")
        merge_of, merge_exp = sem("merge_exponents"), sem("merge_exponentials")
        merged = sem("rows_merged")

        def head(k, t):
            return t.rearrange("p (a d) -> p a d", d=DH)[:, :, 0]

        with nc.Block() as block:

            @block.gpsimd
            def _(eng):
                eng.indirect_dma_start(out=row, out_offset=None, in_=states,
                                       in_offset=bass.IndirectOffsetOnAxis(ap=m.first_end[:, 0:1], axis=0)).then_inc(row_in, 16)
                eng.wait_ge(merged, 1)
                eng.indirect_dma_start(out=states, out_offset=bass.IndirectOffsetOnAxis(ap=m.first_fix[:, 0:1], axis=0),
                                       in_=row, in_offset=None).then_inc(fixed, 16)
                eng.wait_ge(fixed, 16)

            @block.tensor
            def _(eng):
                for c in range(C):
                    eng.wait_ge(wide_made, c + 1)
                    for k in range(3):
                        t = eng.transpose(ps[:, c, k * P:(k + 1) * P], wide[c][:, k, :], m.ident[:, :])
                    t.then_inc(turned, 1)
                for c in range(C):
                    eng.wait_ge(run_made, c + 1)
                    for k in range(3):
                        t = eng.transpose(ps[:, 4 + c, k * P:(k + 1) * P], run[c][:, k, 0:P], m.ident[:, :])
                    t.then_inc(back, 1)

            @block.scalar
            def _(eng):
                for c in range(C):
                    eng.wait_ge(exps_of, c + 1)
                    eng.activation(ex[c], ex[c], ACT.Exp).then_inc(exped, 1)
                eng.wait_ge(merge_of, 1)
                eng.activation(dm, dm, ACT.Exp).then_inc(merge_exp, 1)

            @block.vector
            def _(eng):
                v = Steps(eng, vec)
                end = m.lane_end
                for c in range(C):
                    v.put(eng.tensor_copy(wide[c][:, 0, :], end[:, c * P:(c + 1) * P]))
                    for k in range(2):
                        at = W + k * C * H + c * H
                        v.put(eng.tensor_copy(wide[c][:, 1 + k, :].rearrange("p (a d) -> p a d", d=DH), spread(end[:, at:at + H], 2, [P, H, DH])))
                    v.put(eng.memset(run[c][:, 0:2, 0:1], 0.0))
                    v.put(eng.memset(run[c][:, 2, 0:1], -BIG))
                    v.wait()
                    eng.engine_nop().then_inc(wide_made, 1)
                for c in range(C):
                    eng.wait_ge(turned, c + 1)
                    v.then(eng.tensor_tensor_scan(run[c][:, 2, 1:P + 1], m.whole_neg[:, :], ps[:, c, 2 * P:3 * P], -BIG, ALU.add, ALU.max))
                    v.put(eng.tensor_tensor(ex[c][:, 1, :], ps[:, c, 2 * P:3 * P], run[c][:, 2, 1:P + 1], ALU.subtract))
                    v.then(eng.tensor_tensor(ex[c][:, 0, :], run[c][:, 2, 0:P], m.whole_neg[:, :], ALU.add))
                    v.then(eng.tensor_tensor(ex[c][:, 0, :], ex[c][:, 0, :], run[c][:, 2, 1:P + 1], ALU.subtract))
                    eng.engine_nop().then_inc(exps_of, 1)
                for c in range(C):
                    eng.wait_ge(exped, c + 1)
                    for k in range(2):
                        v.put(eng.tensor_tensor(add[c][:, k, :], ps[:, c, k * P:(k + 1) * P], ex[c][:, 1, :], ALU.mult))
                    v.wait()
                    for k in range(2):
                        v.put(eng.tensor_tensor_scan(run[c][:, k, 1:P + 1], ex[c][:, 0, :], add[c][:, k, :], 0.0, ALU.mult, ALU.add))
                    v.wait()
                    eng.engine_nop().then_inc(run_made, 1)
                eng.wait_ge(row_in, 16)
                for c in range(C):
                    eng.wait_ge(back, c + 1)
                    v.put(eng.tensor_tensor(new_max[:, c * H:(c + 1) * H], row[:, W + C * H + c * H:W + C * H + (c + 1) * H],
                                            head(c, ps[:, 4 + c, 2 * P:3 * P]), ALU.max))
                v.wait()
                v.put(eng.tensor_tensor(dm[:, 0, :], row[:, W + C * H:R], new_max, ALU.subtract))
                for c in range(C):
                    v.put(eng.tensor_tensor(dm[:, 1, c * H:(c + 1) * H], head(c, ps[:, 4 + c, 2 * P:3 * P]), new_max[:, c * H:(c + 1) * H], ALU.subtract))
                v.wait()
                eng.engine_nop().then_inc(merge_of, 1)
                eng.wait_ge(merge_exp, 1)
                v.put(eng.tensor_tensor(row[:, 0:W].rearrange("p (a d) -> p a d", d=DH), row[:, 0:W].rearrange("p (a d) -> p a d", d=DH),
                                        spread(dm[:, 0, :], 2, [P, C * H, DH]), ALU.mult))
                v.put(eng.tensor_tensor(row[:, W:W + C * H], row[:, W:W + C * H], dm[:, 0, :], ALU.mult))
                for c in range(C):
                    v.put(eng.tensor_tensor(part[:, c * P:(c + 1) * P].rearrange("p (a d) -> p a d", d=DH),
                                            ps[:, 4 + c, 0:P].rearrange("p (a d) -> p a d", d=DH),
                                            spread(dm[:, 1, c * H:(c + 1) * H], 2, [P, H, DH]), ALU.mult))
                    v.put(eng.tensor_tensor(part[:, W + c * H:W + (c + 1) * H], head(c, ps[:, 4 + c, P:2 * P]), dm[:, 1, c * H:(c + 1) * H], ALU.mult))
                v.wait()
                v.put(eng.tensor_tensor(row[:, 0:W + C * H], row[:, 0:W + C * H], part, ALU.add))
                v.put(eng.tensor_copy(row[:, W + C * H:R], new_max))
                v.wait()
                eng.engine_nop().then_inc(merged, 1)


def layer1_nodes(nc, m, I):
    with phase(nc, "layer1_nodes") as sem:
        A = Arena(m)
        SUM, MAX = REL * D, REL * D + RH
        st = A(NB, R1)
        fac = A(NB, RH)
        den = A(NB, RH)
        y = A(NB, D)
        st_n = A(NB, 6)
        mv_n = A(NB, 2)
        sd_n = A(NB)
        q2 = A(NB, D)
        kv = [A(2, D) for _ in range(2)]
        ps = m.psum

        def r(name):
            return m.rows[:, ROWS.index(name), :]

        def w(name):
            return m.wt[:, TRANSPOSED.index(name), :]

        state_in = sem("states_landed")
        vec = sem("vector_steps")
        expo, exped = sem("exponents"), sem("exponentials")
        varn, rootn = sem("node_variance"), sem("node_root")
        x_made = sem("x_made")
        x_t, x_k = sem("x_turned"), sem("x_kept")
        qkv_sum, q_made, kv_made = sem("qkv_summed"), sem("queries_made"), sem("keys_values_made")
        stored = [sem(f"keys_values_stored{k}") for k in range(2)]
        q_stored, scattered = sem("queries_stored"), sem("queries_scattered")

        with nc.Block() as block:

            @block.gpsimd
            def _(eng):
                for b in range(NB):
                    eng.indirect_dma_start(out=st[:, b, :], out_offset=None, in_=m.rows1,
                                           in_offset=bass.IndirectOffsetOnAxis(ap=m.end[:, b:b + 1], axis=0)).then_inc(state_in, 16)
                eng.wait_ge(q_made, NB)
                for b in range(NB):
                    eng.indirect_dma_start(out=m.seg_rows, out_offset=bass.IndirectOffsetOnAxis(ap=m.start[:, b:b + 1], axis=0),
                                           in_=q2[:, b, :], in_offset=None).then_inc(scattered, 16)
                eng.wait_ge(scattered, 16 * NB)

            @block.sync
            def _(eng):
                for b in range(NB):
                    eng.wait_ge(kv_made, b + 1)
                    eng.dma_start(m.table2.rearrange("(b p) f -> b p f", p=P)[b], kv[b % 2].rearrange("p a f -> p (a f)")).then_inc(stored[b % 2], 16)
                eng.wait_ge(q_made, NB)
                eng.dma_start(m.query2.rearrange("(b p) f -> p b f", p=P), q2[:, :, :]).then_inc(q_stored, 16)
                eng.wait_ge(q_stored, 16)
                for k in range(2):
                    eng.wait_ge(stored[k], 16 * len(range(k, NB, 2)))

            @block.tensor
            def _(eng):
                eng.wait_ge(x_made, 1)
                turn_out(eng, ps, m.xN, x_t, x_k, m.ident[:, :], 0)
                for b in range(NB):
                    eng.wait_ge(x_k, b // 4 + 1)
                    if b >= 2:
                        eng.wait_ge(q_made, b - 1)
                        eng.wait_ge(kv_made, b - 1)
                    xb = m.xT[:, b * P:b * P + P]
                    for k, name in enumerate(("L2_gnn_q_w", "L2_gnn_k_w", "L2_gnn_v_w")):
                        bank = 2 + b % 2 + 2 * (k > 0)
                        t = eng.matmul(ps[:, bank, k * P:(k + 1) * P], xb, w(name), start=True, stop=True)
                    t.then_inc(qkv_sum, 1)

            @block.scalar
            def _(eng):
                eng.wait_ge(expo, 1)
                eng.activation(fac, fac, ACT.Exp).then_inc(exped, 1)
                for n in range(2):
                    eng.wait_ge(varn, n + 1)
                    eng.activation(sd_n, mv_n[:, :, 1], ACT.Sqrt, bias=m.eps[:, 0:1]).then_inc(rootn, 1)
                turn_in(eng, ps, m.xT, x_t, x_k, 0)
                for b in range(NB):
                    eng.wait_ge(qkv_sum, b + 1)
                    if b >= 2:
                        eng.wait_ge(stored[b % 2], 16 * (b // 2))
                    eng.activation(kv[b % 2].rearrange("p a f -> p (a f)"), ps[:, 4 + b % 2, P:3 * P], ACT.Copy).then_inc(kv_made, 1)

            @block.vector
            def _(eng):
                v = Steps(eng, vec)
                eng.wait_ge(state_in, 16 * NB)
                v.then(eng.tensor_scalar(fac, st[:, :, MAX:R1], 0.0, None, ALU.min))
                eng.engine_nop().then_inc(expo, 1)
                eng.wait_ge(exped, 1)
                v.then(eng.tensor_tensor(den, st[:, :, SUM:MAX], fac, ALU.mult))
                v.then(eng.tensor_scalar(den, den, 1e-8, None, ALU.add))
                v.then(eng.reciprocal(den, den))
                v.then(eng.tensor_tensor(fac, fac, den, ALU.mult))
                acc = st[:, :, 0:SUM]
                v.then(eng.tensor_tensor(acc.rearrange("p b (a d) -> p b a d", d=D1), acc.rearrange("p b (a d) -> p b a d", d=D1),
                                         spread(fac, 3, [P, NB, RH, D1]), ALU.mult))
                v.then(eng.tensor_tensor(y, st[:, :, 0:D], st[:, :, D:2 * D], ALU.add))
                for k in range(2, REL):
                    v.then(eng.tensor_tensor(y, y, st[:, :, k * D:(k + 1) * D], ALU.add))
                v.then(eng.tensor_tensor(y, y, spread(r("L1_gnn_bias"), 1, [P, NB, D]), ALU.add))
                v.then(eng.tensor_tensor(y, y, m.xN[:, :, :], ALU.add))
                for n in range(2):
                    for b in range(NB):
                        v.put(eng.bn_stats(st_n[:, b, :], y[:, b, :]))
                    v.wait()
                    for b in range(NB):
                        v.put(eng.bn_aggr(mv_n[:, b, :], st_n[:, b, :]))
                    v.wait()
                    eng.engine_nop().then_inc(varn, 1)
                    eng.wait_ge(rootn, n + 1)
                    v.then(eng.reciprocal(sd_n, sd_n))
                    to = y if n == 0 else m.xN
                    for b in range(NB):
                        v.put(eng.tensor_scalar(to[:, b, :], y[:, b, :], mv_n[:, b, 0:1], sd_n[:, b:b + 1], ALU.subtract, ALU.mult))
                    v.wait()
                    if n == 0:
                        v.then(eng.tensor_tensor(y, y, spread(r("L1_gnn_ln_gamma"), 1, [P, NB, D]), ALU.mult))
                        v.then(eng.tensor_tensor(y, y, spread(r("L1_gnn_ln_beta"), 1, [P, NB, D]), ALU.add))
                        v.then(eng.tensor_tensor(y, y, m.xN[:, :, :], ALU.add))
                eng.engine_nop().then_inc(x_made, 1)
                for b in range(NB):
                    eng.wait_ge(qkv_sum, b + 1)
                    v.then(eng.tensor_tensor(q2[:, b, :], ps[:, 2 + b % 2, 0:P], r("L2_gnn_q_b"), ALU.add))
                    v.then(eng.tensor_scalar(q2[:, b, :], q2[:, b, :], float(D2) ** -0.5, None, ALU.mult))
                    eng.engine_nop().then_inc(q_made, 1)


SCORES2 = 2 + 4
OLD2 = 3
SUMS2 = OLD2 + HALF


def layer2_edges(nc, m, I):
    with phase(nc, "layer2_edges") as sem:
        A = Arena(m)
        kv = [A(HALF, 2 * D) for _ in range(RING)]
        q = [A(HALF, D) for _ in range(RING)]
        rows = [A(HALF, R2) for _ in range(2)]
        prod = A(HALF, D)
        e, fwd = A(H2, COLS), A(H2, COLS)
        top = [A(H2, COLS) for _ in range(2)]
        gap = [A(H2, COLS) for _ in range(2)]
        ex = [A(H2, COLS) for _ in range(2)]
        old = A(D + H2)
        carry_keeps = [A(HALF) for _ in range(2)]
        keeps = [A(HALF) for _ in range(2)]
        resets = [A(H2 * COLS + 1) for _ in range(2)]
        idx = [A(HALF, dt=I32) for _ in range(RING)]
        SUM, MAX = D, D + H2

        q_first, q_in = sem("first_queries_landed"), [sem(f"queries_landed{k}") for k in range(RING)]
        begun = sem("buffers_begun")
        carried = sem("queries_carried")
        scored, summed = sem("score_steps"), sem("sum_steps")
        exped, filled = sem("exponentials"), sem("state_columns_filled")
        marks, kept = sem("resets_staged"), sem("keeps_staged")
        staged = [sem(f"indices_staged{k}") for k in range(RING)]
        landed = [sem(f"keys_values_landed{k}") for k in range(RING)]
        free = [sem(f"keys_values_used{k}") for k in range(RING)]
        stored, rows_free = sem("states_stored"), sem("states_free")

        def carried_before(i, k):
            return i * (RING * HALF) + k * HALF + 1

        def scores_before(i, k):
            return i * (RING * SCORES2) + k * SCORES2 + 1

        def sums_before(i, k):
            return i * (RING * SUMS2) + (k + 1) * SUMS2

        def edges(i, k):
            return bass.ds(i * (RING * HALF) + k * HALF, HALF)

        with nc.Block() as block:

            @block.sync
            def _(eng):
                def load(i, k):
                    eng.dma_start(q[k % RING], lanes(m.seg_rows)[:, edges(i, k), :]).then_inc(q_in[k % RING], 16)

                def turn(i, last):
                    for k in range(RING):
                        hold(eng, carried, carried_before(i, k) + 1)
                        if k == 0 or not last:
                            load(i, k + RING - 1)
                        hold(eng, summed, sums_before(i, k) + SUMS2)
                        eng.dma_start(lanes(m.rows2)[:, edges(i, k), :], rows[k % 2]).then_inc(stored, 16)
                        hold(eng, stored, 16 * RING * i + 16 * k + 16)
                        eng.nop().then_inc(rows_free, 1)

                for k in range(RING - 1):
                    load(0, k)
                with eng.Fori(0, LOOPS - 1) as i:
                    turn(i, False)
                turn(LOOPS - 1, True)

            @block.gpsimd
            def _(eng):
                eng.indirect_dma_start(out=q[RING - 1][:, HALF - 1, :], out_offset=None, in_=m.query2,
                                       in_offset=bass.IndirectOffsetOnAxis(ap=m.lane_first[:, 0:1], axis=0)).then_inc(q_first, 16)
                with eng.Fori(0, LOOPS) as i:
                    for k in range(RING):
                        hold(eng, staged[k], i + 1)
                        hold(eng, free[k], i + 1)
                        for j in range(HALF):
                            eng.indirect_dma_start(out=kv[k][:, j, :], out_offset=None, in_=m.table2,
                                                   in_offset=bass.IndirectOffsetOnAxis(ap=idx[k][:, j:j + 1], axis=0)).then_inc(landed[k], 16)

            @block.scalar
            def _(eng):
                def stage_marks(k, at):
                    eng.activation(resets[k % 2][:, 0:H2 * COLS].rearrange("p (a t) -> p a t", t=COLS)[:, :, 1:COLS],
                                   spread(m.reset[:, at], 1, [P, H2, HALF]), ACT.Copy).then_inc(marks, 1)
                    eng.activation(carry_keeps[k % 2], m.keep[:, at], ACT.Copy).then_inc(marks, 1)

                for k in range(RING):
                    eng.activation(idx[k], m.src[:, k * HALF:(k + 1) * HALF], ACT.Copy).then_inc(staged[k], 1)
                eng.wait_ge(begun, 5)
                for k in range(2):
                    stage_marks(k, edges(0, k))
                with eng.Fori(0, LOOPS) as i:
                    for k in range(RING):
                        h = k % 2
                        hold(eng, landed[k], 16 * HALF * (i + 1))
                        eng.activation(idx[k], m.src[:, edges(i, RING + k)], ACT.Copy).then_inc(staged[k], 1)
                        hold(eng, scored, scores_before(i, k) + SCORES2)
                        eng.activation(ex[h], gap[h], ACT.Exp, scale=-1.0).then_inc(exped, 1)
                        stage_marks(k, edges(i, k + 2))
                        hold(eng, summed, sums_before(i, k) - SUMS2 + OLD2)
                        eng.activation(keeps[h], m.keep[:, edges(i, k)], ACT.Copy).then_inc(kept, 1)
                        eng.wait_ge(rows_free, i * RING + k + 1)
                        eng.wait_ge(exped, i * RING + k + 1)
                        eng.activation(rows[h][:, :, SUM:MAX], ex[h][:, :, 1:COLS].rearrange("p a t -> p t a"), ACT.Copy).then_inc(filled, 1)
                        eng.activation(rows[h][:, :, MAX:R2], top[h][:, :, 1:COLS].rearrange("p a t -> p t a"), ACT.Copy).then_inc(filled, 1)

            @block.vector
            def _(eng):
                f = Steps(eng, begun)
                for h in range(2):
                    f.put(eng.memset(resets[h], -BIG))
                f.put(eng.memset(fwd, -BIG))
                f.put(eng.memset(rows[1][:, HALF - 1, 0:MAX], 0.0))
                f.put(eng.memset(rows[1][:, HALF - 1, MAX:R2], -BIG))
                f.wait()
                for k in range(RING):
                    eng.engine_nop().then_inc(free[k], 1)
                eng.engine_nop().then_inc(rows_free, 2)
                eng.engine_nop().then_inc(carried, 1)
                eng.engine_nop().then_inc(scored, 1)
                eng.engine_nop().then_inc(summed, SUMS2)
                eng.wait_ge(q_first, 16)

                def half(i, k):
                    return (i + k // RING, k % RING)

                def carry(i, k, j):
                    if j == 0:
                        eng.wait_ge(q_in[k], 16 * i + 16)
                        eng.wait_ge(marks, 2 * RING * i + 2 * k + 2)
                    eng.wait_ge(carried, carried_before(i, k) + j)
                    eng.scalar_tensor_tensor(out=q[k][:, j, :], in0=q[k][:, j - 1, :] if j else q[k - 1][:, HALF - 1, :],
                                             scalar=carry_keeps[k % 2][:, j:j + 1], in1=q[k][:, j, :], op0=ALU.mult, op1=ALU.add).then_inc(carried, 1)

                def score(i, k, step):
                    eng.wait_ge(scored, scores_before(i, k) + step)
                    if step == 0:
                        eng.wait_ge(landed[k], 16 * HALF * (i + 1))
                        eng.wait_ge(carried, carried_before(i, k) + HALF)
                        ins = eng.tensor_tensor(prod, q[k], kv[k][:, :, 0:D], ALU.mult)
                    elif step == 1:
                        ins = eng.tensor_reduce(e[:, :, 1:COLS].rearrange("p a t -> p t a"), prod.rearrange("p t (a d) -> p t a d", d=D2), AX.X, ALU.add)
                    else:
                        ins = maxima_step(eng, step - 2, resets[k % 2], e, fwd, top[k % 2], gap[k % 2])
                    ins.then_inc(scored, 1)

                def add_up(i, k, scores=True, carries=True):
                    v = LoopSteps(eng, summed, sums_before(i, k))
                    h = k % 2
                    row, before = rows[h], rows[1 - h][:, HALF - 1, :]
                    eng.wait_ge(exped, i * RING + k + 1)
                    eng.wait_ge(rows_free, i * RING + k + 1)
                    v.put(eng.tensor_tensor(row[:, :, 0:D].rearrange("p t (a d) -> p t a d", d=D2),
                                            kv[k][:, :, D:2 * D].rearrange("p t (a d) -> p t a d", d=D2),
                                            spread(ex[h][:, :, 1:COLS].rearrange("p a t -> p t a"), 3, [P, HALF, H2, D2]), ALU.mult))
                    v.put(eng.tensor_tensor(old[:, 0:SUM].rearrange("p (a d) -> p a d", d=D2), before[:, 0:SUM].rearrange("p (a d) -> p a d", d=D2),
                                            ex[h][:, :, 0:1].broadcast_to([P, H2, D2]), ALU.mult))
                    v.then(eng.tensor_tensor(old[:, SUM:MAX], before[:, SUM:MAX], ex[h][:, :, 0], ALU.mult))
                    eng.nop(nofuse=True).then_inc(free[k], 1)
                    eng.wait_ge(kept, i * RING + k + 1)
                    eng.wait_ge(filled, 2 * RING * i + 2 * k + 2)
                    for j in range(HALF):
                        v.wait()
                        v.put(eng.scalar_tensor_tensor(out=row[:, j, 0:MAX], in0=row[:, j - 1, 0:MAX] if j else old, scalar=keeps[h][:, j:j + 1],
                                                       in1=row[:, j, 0:MAX], op0=ALU.mult, op1=ALU.add))
                        if carries:
                            carry(*half(i, k + 2), j)
                        if scores and 2 <= j < 2 + SCORES2:
                            score(*half(i, k + 1), j - 2)
                    v.wait()
                    assert v.n == SUMS2

                for k in range(2):
                    for j in range(HALF):
                        carry(0, k, j)
                for step in range(SCORES2):
                    score(0, 0, step)
                with eng.Fori(0, LOOPS - 1) as i:
                    for k in range(RING):
                        add_up(i, k)
                for k in range(RING):
                    add_up(LOOPS - 1, k, scores=k + 1 < RING, carries=k + 2 < RING)
                f.then(eng.tensor_copy(m.lane_end[:, 0:R2], rows[1][:, HALF - 1, :]))


def layer2_nodes(nc, m, I):
    with phase(nc, "layer2_nodes") as sem:
        A = Arena(m)
        st = A(NB, R2)
        big = A(4 * NP)
        q, y = (big[:, j * NP:(j + 1) * NP].rearrange("p (b f) -> p b f", f=D) for j in range(2))
        aT, sT = (big[:, j * NP:(j + 1) * NP] for j in range(2, 4))
        kvn = A(NB, 2 * D)
        hid = [kvn[:, 8 * k:8 * k + 8, :].rearrange("p b f -> p (b f)").rearrange("p (j n) -> p j n", j=FF) for k in range(2)]
        out = kvn[:, 16:20, :].rearrange("p b f -> p (b f)").rearrange("p (a b f) -> p a b f", a=2, f=D)
        own = A(NB, H2)
        top = A(NB, H2)
        ex = A(2, NB * H2)
        den = A(NB, H2)
        st_b = A(len(REALCH), 6)
        mv_b = A(2)
        sd_b, scale, shift = A(1), A(1), A(1)
        st_n = A(NB, 6)
        mv_n = A(NB, 2)
        sd_n = A(NB)
        ps = m.psum
        SUM, MAX = D, D + H2
        aN = st[:, :, 0:D]
        bT = aT

        def c(name):
            k = COLUMNS.index(name)
            return m.cols[:, k:k + 1]

        state_in, own_in = sem("states_landed"), sem("own_rows_landed")
        vec = sem("vector_steps")
        expo, exped = sem("exponents"), sem("exponentials")
        a_made, a_t, a_k = sem("values_made"), sem("values_turned"), sem("values_kept")
        o_sum, s_made = sem("output_summed"), sem("sum_made")
        var1, root1, scale1, b_made = sem("variance1"), sem("root1"), sem("scale1"), sem("normed1")
        l1_sum, hid_made, leaky, l2_sum, s2_made = sem("hidden_summed"), sem("hidden_made"), sem("hidden_leaky"), sem("second_summed"), sem("sum2_made")
        var2, root2, scale2, b2_made = sem("variance2"), sem("root2"), sem("scale2"), sem("normed2")
        n_t, y_made = sem("normed_turned"), sem("y_made")
        varn, rootn, x_made = sem("node_variance"), sem("node_root"), sem("x_made")
        x_t, x_k = sem("x_turned"), sem("x_kept")
        t_sum, t_made = sem("table_summed"), sem("table_made")
        stored = [sem(f"table_stored{k}") for k in range(2)]
        NCH = len(CHUNKS)

        with nc.Block() as block:

            @block.gpsimd
            def _(eng):
                for b in range(NB):
                    eng.indirect_dma_start(out=st[:, b, :], out_offset=None, in_=m.rows2,
                                           in_offset=bass.IndirectOffsetOnAxis(ap=m.end[:, b:b + 1], axis=0)).then_inc(state_in, 16)

            @block.sync
            def _(eng):
                eng.dma_start(q, m.query2.rearrange("(b p) f -> p b f", p=P)).then_inc(own_in, 16)
                eng.dma_start(kvn, m.table2.rearrange("(b p) f -> p b f", p=P)).then_inc(own_in, 16)
                for k, (at, n) in enumerate(CHUNKS):
                    eng.wait_ge(t_made, k + 1)
                    eng.dma_start(m.table3.rearrange("(b p) f -> p b f", p=P)[:, at // P:(at + n) // P, :], out2(out, k, n)).then_inc(stored[k % 2], 16)
                for k in range(2):
                    eng.wait_ge(stored[k], 16 * len(range(k, NCH, 2)))

            @block.tensor
            def _(eng):
                eng.wait_ge(a_made, 1)
                turn_out(eng, ps, aN, a_t, a_k, m.ident[:, :], 0)
                for k, (at, n) in enumerate(CHUNKS):
                    eng.wait_ge(a_k, k + 1)
                    if k >= 2:
                        eng.wait_ge(s_made, k - 1)
                    eng.matmul(ps[:, 2 + k % 2, 0:n], m.wt[:, TRANSPOSED.index("L2_gnn_out_w"), :], aT[:, at:at + n], start=True, stop=True).then_inc(o_sum, 1)
                eng.wait_ge(a_k, NCH)
                eng.wait_ge(s_made, NCH)
                for k, (at, n) in enumerate(CHUNKS):
                    eng.wait_ge(b_made, k + 1)
                    for j in range(FF):
                        if k:
                            eng.wait_ge(hid_made, FF * (k - 1) + j + 1)
                        eng.matmul(ps[:, j, 0:n], m.wt[:, LIN1 + j, :], bT[:, at:at + n], start=True, stop=True).then_inc(l1_sum, 1)
                    eng.wait_ge(leaky, k + 1)
                    if k >= 2:
                        eng.wait_ge(s2_made, k - 1)
                    for j in range(FF):
                        t = eng.matmul(ps[:, 4 + k % 2, 0:n], m.wt[:, LIN2 + j, :], hid[k % 2][:, j, 0:n], start=(j == 0), stop=(j == FF - 1))
                    t.then_inc(l2_sum, 1)
                for k, (at, n) in enumerate(CHUNKS):
                    eng.wait_ge(b2_made, k + 1)
                    if k >= 2:
                        eng.wait_ge(y_made, k - 1)
                    for b in range(n // P):
                        t = eng.transpose(ps[:, 6 + k % 2, b * P:(b + 1) * P], sT[:, at + b * P:at + (b + 1) * P], m.ident[:, :])
                    t.then_inc(n_t, 1)
                eng.wait_ge(x_made, 1)
                eng.wait_ge(hid_made, FF * NCH)
                turn_out(eng, ps, m.xN, x_t, x_k, m.ident[:, :], 0)
                for k, (at, n) in enumerate(CHUNKS):
                    eng.wait_ge(x_k, k + 1)
                    if k >= 2:
                        eng.wait_ge(t_made, k - 1)
                    for b in range(n // P):
                        t = eng.matmul(ps[:, 2 + k % 2, b * P:(b + 1) * P], m.xT[:, at + b * P:at + (b + 1) * P], m.w3[:, 1, :], start=True, stop=True)
                    t.then_inc(t_sum, 1)

            @block.scalar
            def _(eng):
                eng.wait_ge(expo, 1)
                eng.activation(ex, ex, ACT.Exp).then_inc(exped, 1)
                turn_in(eng, ps, aT, a_t, a_k, 0)
                eng.wait_ge(var1, 1)
                eng.activation(sd_b, mv_b[:, 1:2], ACT.Sqrt, bias=m.eps[:, 0:1]).then_inc(root1, 1)
                eng.wait_ge(scale1, 1)
                for k, (at, n) in enumerate(CHUNKS):
                    eng.activation(bT[:, at:at + n], sT[:, at:at + n], ACT.Identity, bias=shift, scale=scale).then_inc(b_made, 1)
                for k, (at, n) in enumerate(CHUNKS):
                    if k >= 2:
                        eng.wait_ge(l2_sum, k - 1)
                    for j in range(FF):
                        eng.wait_ge(l1_sum, FF * k + j + 1)
                        eng.activation(hid[k % 2][:, j, 0:n], ps[:, j, 0:n], ACT.Identity, bias=m.lin1_b[:, j:j + 1]).then_inc(hid_made, 1)
                eng.wait_ge(var2, 1)
                eng.activation(sd_b, mv_b[:, 1:2], ACT.Sqrt, bias=m.eps[:, 0:1]).then_inc(root2, 1)
                eng.wait_ge(scale2, 1)
                for k, (at, n) in enumerate(CHUNKS):
                    eng.activation(sT[:, at:at + n], sT[:, at:at + n], ACT.Identity, bias=shift, scale=scale).then_inc(b2_made, 1)
                eng.wait_ge(varn, 1)
                eng.activation(sd_n, mv_n[:, :, 1], ACT.Sqrt, bias=m.eps[:, 0:1]).then_inc(rootn, 1)
                turn_in(eng, ps, m.xT, x_t, x_k, 0)
                for k, (at, n) in enumerate(CHUNKS):
                    eng.wait_ge(t_sum, k + 1)
                    if k >= 2:
                        eng.wait_ge(stored[k % 2], 16 * (k // 2))
                    eng.activation(out2(out, k, n), ps[:, 2 + k % 2, 0:n].rearrange("p (b f) -> p b f", f=D), ACT.Copy).then_inc(t_made, 1)

            @block.vector
            def _(eng):
                v = Steps(eng, vec)
                eng.wait_ge(own_in, 32)
                v.then(eng.tensor_tensor(q, q, kvn[:, :, 0:D], ALU.mult))
                v.then(eng.tensor_reduce(own, q.rearrange("p b (a d) -> p b a d", d=D2), AX.X, ALU.add))
                eng.wait_ge(state_in, 16 * NB)
                v.then(eng.tensor_tensor(top, own, st[:, :, MAX:R2], ALU.max))
                ex4 = ex.rearrange("p k (b a) -> p k b a", a=H2)
                v.put(eng.tensor_tensor(ex4[:, 0, :, :], st[:, :, MAX:R2], top, ALU.subtract))
                v.then(eng.tensor_tensor(ex4[:, 1, :, :], own, top, ALU.subtract))
                eng.engine_nop().then_inc(expo, 1)
                eng.wait_ge(exped, 1)
                v.then(eng.tensor_tensor(den, st[:, :, SUM:MAX], ex4[:, 0, :, :], ALU.mult))
                v.then(eng.tensor_tensor(den, den, ex4[:, 1, :, :], ALU.add))
                v.then(eng.tensor_scalar(den, den, 1e-16, None, ALU.add))
                v.then(eng.reciprocal(den, den))
                for k in range(2):
                    v.put(eng.tensor_tensor(ex4[:, k, :, :], ex4[:, k, :, :], den, ALU.mult))
                v.wait()
                for k, x in ((0, aN), (1, kvn[:, :, D:2 * D])):
                    x4 = x.rearrange("p b (a d) -> p b a d", d=D2)
                    v.put(eng.tensor_tensor(x4, x4, spread(ex4[:, k, :, :], 3, [P, NB, H2, D2]), ALU.mult))
                v.wait()
                v.then(eng.tensor_tensor(aN, aN, kvn[:, :, D:2 * D], ALU.add))
                eng.engine_nop().then_inc(a_made, 1)
                for k, (at, n) in enumerate(CHUNKS):
                    eng.wait_ge(o_sum, k + 1)
                    eng.scalar_tensor_tensor(out=sT[:, at:at + n], in0=ps[:, 2 + k % 2, 0:n], scalar=c("L2_gnn_out_b"), in1=m.xT[:, at:at + n],
                                             op0=ALU.add, op1=ALU.add).then_inc(s_made, 1)

                def norm(made, var, root, scaled, gamma, beta):
                    for k, (at, n) in enumerate(REALCH):
                        eng.wait_ge(made, k + 1)
                        v.put(eng.bn_stats(st_b[:, k, :], sT[:, at:at + n]))
                    v.wait()
                    eng.bn_aggr(mv_b, st_b).then_inc(var, 1)
                    eng.wait_ge(root, 1)
                    v.then(eng.reciprocal(sd_b, sd_b))
                    v.then(eng.tensor_tensor(scale, sd_b, c(gamma), ALU.mult))
                    v.then(eng.tensor_tensor(sd_b, mv_b[:, 0:1], scale, ALU.mult))
                    eng.tensor_tensor(shift, c(beta), sd_b, ALU.subtract).then_inc(scaled, 1)
                    eng.wait_ge(scaled, 1)

                norm(s_made, var1, root1, scale1, "L2_gnn_g1", "L2_gnn_b1")
                for k in range(NCH + 1):
                    if k < NCH:
                        hk = hid[k % 2][:, :, 0:CHUNKS[k][1]]
                        eng.wait_ge(hid_made, FF * (k + 1))
                        eng.scalar_tensor_tensor(out=hk, in0=hk, scalar=0.01, in1=hk, op0=ALU.mult, op1=ALU.max).then_inc(leaky, 1)
                    if k == 0:
                        continue
                    at, n = CHUNKS[k - 1]
                    eng.wait_ge(l2_sum, k)
                    eng.scalar_tensor_tensor(out=sT[:, at:at + n], in0=ps[:, 4 + (k - 1) % 2, 0:n], scalar=c("L2_gnn_lin2_b"), in1=bT[:, at:at + n],
                                             op0=ALU.add, op1=ALU.add).then_inc(s2_made, 1)
                norm(s2_made, var2, root2, scale2, "L2_gnn_g2", "L2_gnn_b2")
                for k, (at, n) in enumerate(CHUNKS):
                    eng.wait_ge(n_t, k + 1)
                    b0, b1 = at // P, (at + n) // P
                    eng.tensor_tensor(y[:, b0:b1, :], ps[:, 6 + k % 2, 0:n].rearrange("p (b f) -> p b f", f=D), m.xN[:, b0:b1, :], ALU.add).then_inc(y_made, 1)
                eng.wait_ge(y_made, NCH)
                for b in range(NB):
                    v.put(eng.bn_stats(st_n[:, b, :], y[:, b, :]))
                v.wait()
                for b in range(NB):
                    v.put(eng.bn_aggr(mv_n[:, b, :], st_n[:, b, :]))
                v.wait()
                eng.engine_nop().then_inc(varn, 1)
                eng.wait_ge(rootn, 1)
                v.then(eng.reciprocal(sd_n, sd_n))
                for b in range(NB):
                    v.put(eng.tensor_scalar(m.xN[:, b, :], y[:, b, :], mv_n[:, b, 0:1], sd_n[:, b:b + 1], ALU.subtract, ALU.mult))
                v.wait()
                eng.engine_nop().then_inc(x_made, 1)


def out2(out, k, n):
    return out[:, k % 2, 0:n // P, :]


PER_TURN3 = 2 * 2 * HALF + 3


def layer3_edges(nc, m, I):
    with phase(nc, "layer3_edges") as sem:
        A = Arena(m)
        feat = [A(HALF, D) for _ in range(2)]
        rows = [A(HALF, D) for _ in range(2)]
        resets, vals = A(BODY), A(BODY)
        idx = [A(HALF, dt=I32) for _ in range(2)]
        begun = sem("states_begun")
        steps = sem("edge_steps")
        staged = [sem(f"indices_staged{h}") for h in range(2)]
        landed = [sem(f"rows_landed{h}") for h in range(2)]
        free = [sem(f"rows_used{h}") for h in range(2)]
        stored = [sem(f"states_stored{h}") for h in range(2)]
        rows_free = [sem(f"states_free{h}") for h in range(2)]

        with nc.Block() as block:

            @block.sync
            def _(eng):
                with eng.Fori(0, TURNS) as i:
                    for h in range(2):
                        hold(eng, steps, i * PER_TURN3 + 3 + (h + 1) * 2 * HALF)
                        eng.dma_start(lanes(m.rows3)[:, bass.ds(i * BODY + h * HALF, HALF), :], rows[h]).then_inc(stored[h], 16)
                        hold(eng, stored[h], 16 * i + 16)
                        eng.nop().then_inc(rows_free[h], 1)

            @block.gpsimd
            def _(eng):
                with eng.Fori(0, TURNS) as i:
                    for h in range(2):
                        hold(eng, staged[h], i + 1)
                        hold(eng, free[h], i + 1)
                        for j in range(HALF):
                            eng.indirect_dma_start(out=feat[h][:, j, :], out_offset=None, in_=m.table3,
                                                   in_offset=bass.IndirectOffsetOnAxis(ap=idx[h][:, j:j + 1], axis=0)).then_inc(landed[h], 16)

            @block.scalar
            def _(eng):
                for h in range(2):
                    eng.activation(idx[h], m.src[:, h * HALF:(h + 1) * HALF], ACT.Copy).then_inc(staged[h], 1)
                with eng.Fori(0, TURNS) as i:
                    for h in range(2):
                        hold(eng, landed[h], 16 * HALF * (i + 1))
                        eng.activation(idx[h], m.src[:, bass.ds(i * BODY + BODY + h * HALF, HALF)], ACT.Copy).then_inc(staged[h], 1)

            @block.vector
            def _(eng):
                for h in range(2):
                    eng.engine_nop().then_inc(free[h], 1)
                    eng.engine_nop().then_inc(rows_free[h], 1)
                f = Steps(eng, begun)
                f.then(eng.memset(rows[1][:, HALF - 1, :], -BIG))
                eng.engine_nop().then_inc(steps, 1)
                with eng.Fori(0, TURNS) as i:
                    v = LoopSteps(eng, steps, i * PER_TURN3 + 1)
                    v.wait()
                    eng.nop(nofuse=True)
                    v.put(eng.tensor_copy(resets, m.reset[:, bass.ds(i * BODY, BODY)]))
                    v.put(eng.tensor_copy(vals, m.val[:, bass.ds(i * BODY, BODY)]))
                    v.wait()
                    for h in range(2):
                        eng.wait_ge(landed[h], 16 * HALF * (i + 1))
                        for j in range(HALF):
                            s = h * HALF + j
                            v.put(eng.scalar_tensor_tensor(out=feat[h][:, j, :], in0=m.edge_w[:, :], scalar=vals[:, s:s + 1],
                                                           in1=feat[h][:, j, :], op0=ALU.mult, op1=ALU.add))
                        v.wait()
                        eng.wait_ge(rows_free[h], i + 1)
                        for j in range(HALF):
                            s = h * HALF + j
                            v.then(eng.scalar_tensor_tensor(out=rows[h][:, j, :], in0=rows[h][:, j - 1, :] if j else rows[1 - h][:, HALF - 1, :],
                                                            scalar=resets[:, s:s + 1], in1=feat[h][:, j, :], op0=ALU.add, op1=ALU.max))
                        assert v.n == 2 + (h + 1) * 2 * HALF
                        eng.nop(nofuse=True).then_inc(free[h], 1)
                    v.put(eng.engine_nop())
                eng.wait_ge(steps, TURNS * PER_TURN3 + 1)
                f.then(eng.tensor_copy(m.lane_end[:, 0:D], rows[1][:, HALF - 1, :]))


def layer3_nodes(nc, m, I, result):
    with phase(nc, "layer3_nodes") as sem:
        A = Arena(m)
        lane_max = A(P + 1)
        row = A(D)
        agg = A(NB, D)
        aT, hT = A(NP), A(NP)
        y = A(NB, D)
        st_n = A(NB, 6)
        mv_n = A(NB, 2)
        sd_n = A(NB)
        ps = m.psum

        def r(name):
            return m.rows[:, ROWS.index(name), :]

        row_in, fixed, agg_in = sem("first_rows_landed"), sem("first_rows_fixed"), sem("maxima_landed")
        vec = sem("vector_steps")
        l_t, l_made, l_back, merged = sem("lanes_turned"), sem("lane_maxima"), sem("lane_maxima_turned"), sem("rows_merged")
        d_sum, a_made, a_t, a_k = sem("target_part_summed"), sem("agg_made"), sem("agg_turned"), sem("agg_kept")
        h_sum, h_made, y_sum, y_made = sem("hidden_summed"), sem("hidden_made"), sem("y_summed"), sem("y_made")
        varn, rootn, x_made, out_done = sem("node_variance"), sem("node_root"), sem("x_made"), sem("result_stored")
        NCH = len(CHUNKS)

        with nc.Block() as block:

            @block.gpsimd
            def _(eng):
                eng.indirect_dma_start(out=row, out_offset=None, in_=m.rows3,
                                       in_offset=bass.IndirectOffsetOnAxis(ap=m.first_end[:, 0:1], axis=0)).then_inc(row_in, 16)
                eng.wait_ge(merged, 1)
                eng.indirect_dma_start(out=m.rows3, out_offset=bass.IndirectOffsetOnAxis(ap=m.first_fix[:, 0:1], axis=0),
                                       in_=row, in_offset=None).then_inc(fixed, 16)
                eng.wait_ge(fixed, 16)
                for b in range(NB):
                    eng.indirect_dma_start(out=agg[:, b, :], out_offset=None, in_=m.rows3,
                                           in_offset=bass.IndirectOffsetOnAxis(ap=m.end[:, b:b + 1], axis=0)).then_inc(agg_in, 16)

            @block.sync
            def _(eng):
                eng.wait_ge(x_made, 1)
                eng.dma_start(result[0:(NB - 1) * P, :].rearrange("(b p) f -> p b f", p=P), m.xN[:, 0:NB - 1, :]).then_inc(out_done, 16)
                eng.dma_start(result[(NB - 1) * P:N, :], m.xN[0:TAIL, NB - 1, :]).then_inc(out_done, 16)
                eng.wait_ge(out_done, 32)

            @block.tensor
            def _(eng):
                eng.transpose(ps[:, 6, 0:P], m.lane_end[:, 0:D], m.ident[:, :]).then_inc(l_t, 1)
                eng.wait_ge(l_made, 1)
                eng.transpose(ps[:, 7, 0:P], lane_max[:, 0:P], m.ident[:, :]).then_inc(l_back, 1)
                for k, (at, n) in enumerate(CHUNKS):
                    if k >= 2:
                        eng.wait_ge(a_made, k - 1)
                    for b in range(n // P):
                        t = eng.matmul(ps[:, 2 + k % 2, b * P:(b + 1) * P], m.xT[:, at + b * P:at + (b + 1) * P], m.w3[:, 0, :], start=True, stop=True)
                    t.then_inc(d_sum, 1)
                eng.wait_ge(a_made, NCH)
                turn_out(eng, ps, agg, a_t, a_k, m.ident[:, :], 0)
                for k, (at, n) in enumerate(CHUNKS):
                    eng.wait_ge(a_k, k + 1)
                    if k >= 2:
                        eng.wait_ge(h_made, k - 1)
                    eng.matmul(ps[:, 4 + k % 2, 0:n], m.w3[:, 2, :], m.xT[:, at:at + n], start=True, stop=False)
                    eng.matmul(ps[:, 4 + k % 2, 0:n], m.w3[:, 3, :], aT[:, at:at + n], start=False, stop=True).then_inc(h_sum, 1)
                for k, (at, n) in enumerate(CHUNKS):
                    eng.wait_ge(h_made, k + 1)
                    if k >= 2:
                        eng.wait_ge(y_made, k - 1)
                    for b in range(n // P):
                        t = eng.matmul(ps[:, 2 + k % 2, b * P:(b + 1) * P], hT[:, at + b * P:at + (b + 1) * P], m.w3[:, 4, :], start=True, stop=True)
                    t.then_inc(y_sum, 1)

            @block.scalar
            def _(eng):
                turn_in(eng, ps, aT, a_t, a_k, 0)
                k3 = COLUMNS.index("L3_gnn_b1")
                for k, (at, n) in enumerate(CHUNKS):
                    eng.wait_ge(h_sum, k + 1)
                    eng.activation(hT[:, at:at + n], ps[:, 4 + k % 2, 0:n], ACT.Relu, bias=m.cols[:, k3:k3 + 1]).then_inc(h_made, 1)
                eng.wait_ge(varn, 1)
                eng.activation(sd_n, mv_n[:, :, 1], ACT.Sqrt, bias=m.eps[:, 0:1]).then_inc(rootn, 1)

            @block.vector
            def _(eng):
                v = Steps(eng, vec)
                v.put(eng.memset(lane_max[:, 0:1], -BIG))
                eng.wait_ge(l_t, 1)
                v.then(eng.tensor_tensor_scan(lane_max[:, 1:P + 1], m.whole_neg[:, :], ps[:, 6, 0:P], -BIG, ALU.add, ALU.max))
                eng.engine_nop().then_inc(l_made, 1)
                eng.wait_ge(row_in, 16)
                eng.wait_ge(l_back, 1)
                eng.tensor_tensor(row, row, ps[:, 7, 0:P], ALU.max).then_inc(merged, 1)
                eng.wait_ge(agg_in, 16 * NB)
                for k, (at, n) in enumerate(CHUNKS):
                    b0, b1 = at // P, (at + n) // P
                    a = agg[:, b0:b1, :]
                    eng.wait_ge(d_sum, k + 1)
                    v.then(eng.tensor_tensor(a, a, ps[:, 2 + k % 2, 0:n].rearrange("p (b f) -> p b f", f=D), ALU.add))
                    v.then(eng.tensor_tensor(a, a, spread(r("L3_gnn_bm"), 1, [P, b1 - b0, D]), ALU.add))
                    eng.tensor_tensor(a, a, spread(m.has[:, b0:b1], 2, [P, b1 - b0, D]), ALU.mult).then_inc(a_made, 1)
                v.then(eng.tensor_tensor(m.xN[:, :, :], m.xN[:, :, :], spread(r("L3_gnn_b2"), 1, [P, NB, D]), ALU.add))
                for k, (at, n) in enumerate(CHUNKS):
                    eng.wait_ge(y_sum, k + 1)
                    b0, b1 = at // P, (at + n) // P
                    eng.tensor_tensor(y[:, b0:b1, :], ps[:, 2 + k % 2, 0:n].rearrange("p (b f) -> p b f", f=D), m.xN[:, b0:b1, :], ALU.add).then_inc(y_made, 1)
                eng.wait_ge(y_made, NCH)
                for b in range(NB):
                    v.put(eng.bn_stats(st_n[:, b, :], y[:, b, :]))
                v.wait()
                for b in range(NB):
                    v.put(eng.bn_aggr(mv_n[:, b, :], st_n[:, b, :]))
                v.wait()
                eng.engine_nop().then_inc(varn, 1)
                eng.wait_ge(rootn, 1)
                v.then(eng.reciprocal(sd_n, sd_n))
                for b in range(NB):
                    v.put(eng.tensor_scalar(m.xN[:, b, :], y[:, b, :], mv_n[:, b, 0:1], sd_n[:, b:b + 1], ALU.subtract, ALU.mult))
                v.wait()
                eng.engine_nop().then_inc(x_made, 1)


def gnn_resnorm_stack(nc, I, out):
    with ExitStack() as ctx:
        m = allocate(nc, ctx)
        setup_phase(nc, m, I)
        layer0_edges(nc, m, I)
        layer0_nodes(nc, m, I)
        layer1_edges(nc, m, I)
        carry_sums(nc, m, m.rows1, REL, H1)
        layer1_nodes(nc, m, I)
        layer2_edges(nc, m, I)
        carry_sums(nc, m, m.rows2, 1, H2)
        layer2_nodes(nc, m, I)
        layer3_edges(nc, m, I)
        layer3_nodes(nc, m, I, out)


_INS = ['x', 'src', 'dst', 'edge_type_4', 'edge_weight'] + [
    'L0_gnn_' + n for n in ('W1w', 'W1b', 'U1w', 'U1b', 'W2w', 'W2b', 'U2w', 'U2b', 'W3w', 'W3b', 'U3w', 'U3b', 'bn_g',
                            'bn_b', 'm_w0', 'm_b0', 'm_bng', 'm_bnb', 'm_w1', 'm_b1')] + [
    'L1_gnn_' + n for n in ('W', 'attn_src', 'attn_dst', 'bias', 'ln_gamma', 'ln_beta')] + [
    'L2_gnn_' + n for n in ('q_w', 'q_b', 'k_w', 'v_w', 'out_w', 'out_b', 'g1', 'b1', 'lin1_w', 'lin1_b', 'lin2_w',
                            'lin2_b', 'g2', 'b2')] + [
    'L3_gnn_' + n for n in ('Wm', 'bm', 'W1', 'b1', 'W2', 'b2')]
_OUTS = [((3125, 128), 'float32')]


def kernel(**inputs):
    import numpy as _np
    import concourse.bacc as _bacc
    from concourse import mybir as _mybir
    from concourse.bass_utils import run_bass_kernel_spmd as _run

    nc = _bacc.Bacc("TRN2", target_bir_lowering=False, num_devices=1)
    arrays, I, outs = {}, {}, []
    for name in _INS:
        a = _np.ascontiguousarray(inputs[name])
        arrays[f"in_{name}_dram"] = a
        I[name] = nc.dram_tensor(f"in_{name}_dram", a.shape, _mybir.dt.from_np(a.dtype), kind="ExternalInput").ap()
    for i, (shape, dtype) in enumerate(_OUTS):
        dt = _mybir.dt.from_np(_np.dtype(dtype))
        outs.append(nc.dram_tensor(f"out_{i}_dram", shape, dt, kind="ExternalOutput").ap())
    gnn_resnorm_stack(nc, I, outs[0])
    r = _run(nc, [arrays], core_ids=[0])
    got = tuple(r.results[0][f"out_{i}_dram"] for i in range(len(_OUTS)))
    return got[0]
```

```python
from contextlib import ExitStack, contextmanager

import concourse.bass as bass
from concourse import mybir

F32 = mybir.dt.float32
BF16 = mybir.dt.bfloat16
I32 = mybir.dt.int32
ALU = mybir.AluOpType
ACT = mybir.ActivationFunctionType
AX = mybir.AxisListType

P = 128
N, D, E = 3125, 128, 100000
NB = -(-N // P)
NP = NB * P
TAIL = N - (NB - 1) * P
HALF = 14
BODY = 2 * HALF
TURNS = 28
T = BODY * TURNS
EP = P * T
LAST = E - (P - 1) * T
assert EP >= E and 0 < LAST <= T
RING = 4
LOOPS = T // (RING * HALF)
AHEAD = RING * HALF
assert T == LOOPS * RING * HALF
SEVEN = 7
TABS = 4
REL, H1, D1 = 4, 4, 32
RH = REL * H1
H2, D2 = 8, 16
FF = 4
R1 = REL * D + 2 * RH
R2 = D + 2 * H2
HS = D + H1
BIG = 1e30
EPS = 1e-5
CHUNKS = [(c, min(512, NP - c)) for c in range(0, NP, 512)]
REALCH = [(c, min(512, N - c)) for c in range(0, N, 512)]

TRANSPOSED = ["L0_gnn_W1w", "L0_gnn_U1w", "L0_gnn_W2w", "L0_gnn_U2w", "L0_gnn_W3w", "L0_gnn_U3w",
              "L0_gnn_m_w0", "L0_gnn_m_w1", "L2_gnn_q_w", "L2_gnn_k_w", "L2_gnn_v_w", "L2_gnn_out_w"]
LIN1 = len(TRANSPOSED)
LIN2 = LIN1 + FF
SLOTS = LIN2 + FF
COLUMNS = ["L0_gnn_W1b", "L0_gnn_U1b", "L0_gnn_W2b", "L0_gnn_U2b", "L0_gnn_W3b", "L0_gnn_U3b",
           "L0_gnn_bn_g", "L0_gnn_bn_b", "L0_gnn_m_b0", "L0_gnn_m_bng", "L0_gnn_m_bnb",
           "L2_gnn_out_b", "L2_gnn_g1", "L2_gnn_b1", "L2_gnn_lin2_b", "L2_gnn_g2", "L2_gnn_b2",
           "L3_gnn_b1"]
ROWS = ["L0_gnn_m_b1", "L1_gnn_bias", "L1_gnn_ln_gamma", "L1_gnn_ln_beta", "L2_gnn_q_b", "L3_gnn_bm", "L3_gnn_b2"]


class Memory:
    pass


def spread(ap, axis, shape):
    return ap.unsqueeze(axis).broadcast_to(shape)


def hold(eng, sem, value):
    eng.wait_ge(sem, value)
    eng.nop(nofuse=True)


@contextmanager
def phase(nc, of):
    sems = []

    def sem(name):
        sems.append(nc.alloc_semaphore(f"{of}_{name}"))
        return sems[-1]

    yield sem
    nc.clear_and_free_semaphores(sems)
    nc.all_engine_barrier()


def lanes(rows):
    return rows[0:EP, :].rearrange("(p t) f -> p t f", p=P)


def allocate(nc, ctx):
    m = Memory()

    def sb(name, shape, dt=F32):
        return ctx.enter_context(nc.sbuf_tensor(name, shape, dt))

    def dram(name, shape, dt=F32):
        return nc.dram_tensor(name, shape, dt, kind="Internal").ap()

    m.src = sb("src", [P, T + AHEAD], I32)
    m.src_rel = sb("src_rel", [P, T + AHEAD], I32)
    m.val = sb("val", [P, T])
    m.keep = sb("keep", [P, T + BODY])
    m.reset = sb("reset", [P, T + BODY])
    m.other_rel = sb("other_rel", [P, T, REL], BF16)
    m.lane_first = sb("lane_first", [P, 1], I32)
    m.first_end = sb("first_end", [P, 1], I32)
    m.first_fix = sb("first_fix", [P, 1], I32)
    m.whole_neg = sb("whole_neg", [P, P])
    m.start = sb("start", [P, NB], I32)
    m.end = sb("end", [P, NB], I32)
    m.has = sb("has", [P, NB])
    m.xN = sb("xN", [P, NB, D])
    m.xT = sb("xT", [P, NP])
    m.ident = sb("ident", [P, P])
    m.spare = sb("spare", [P, 1])
    m.lower = sb("lower", [P, P])
    m.tri = sb("tri", [P, P])
    m.ones = sb("ones", [P, P])
    m.eps = sb("eps", [P, 1])
    m.wt = sb("wt", [P, SLOTS, P])
    m.cols = sb("cols", [P, len(COLUMNS)])
    m.lin1_b = sb("lin1_b", [P, FF])
    m.rows = sb("rows", [P, len(ROWS), D])
    m.w_rel = sb("w_rel", [P, REL, D])
    m.w3 = sb("w3", [P, 5, D])
    m.edge_w = sb("edge_w", [P, D])
    m.lane_end = sb("lane_end", [P, R1])
    m.arena = sb("arena", [P, 35040])
    m.psum = ctx.enter_context(nc.psum_tensor("psum", [P, 8, 512], F32))

    m.seg_rows = dram("seg_rows", [EP + NP, D])
    m.seg_dst = dram("seg_dst", [EP + NP, RH])
    m.tabs = [dram(f"tab{j}", [NP + P, D]) for j in range(TABS)]
    m.rows1 = dram("rows1", [EP + 1 + P, R1])
    m.rows2 = dram("rows2", [EP + 1 + P, R2])
    m.rows3 = dram("rows3", [EP + 1 + P, D])
    m.table1 = dram("table1", [NP * REL, HS])
    m.dst1 = dram("dst1", [NP, RH])
    m.query2 = dram("query2", [NP, D])
    m.table2 = dram("table2", [NP, 2 * D])
    m.table3 = dram("table3", [NP, D])
    return m


class Arena:

    def __init__(self, m):
        self.m, self.at = m, 0

    def __call__(self, *shape, dt=F32):
        n = 1
        for s in shape:
            n *= s
        words = n if dt != BF16 else -(-n // 2)
        ap = self.m.arena[:, self.at:self.at + words]
        self.at += words
        assert self.at <= 35040, self.at
        if dt != F32:
            ap = ap.bitcast(dt)
        if len(shape) == 2:
            ap = ap.rearrange("p (a b) -> p a b", b=shape[1])
        if len(shape) == 3:
            ap = ap.rearrange("p (a b c) -> p a b c", b=shape[1], c=shape[2])
        return ap


def setup_phase(nc, m, I):
    with phase(nc, "setup_phase") as sem:
        A = Arena(m)
        dst = A(T, dt=I32)
        typ = A(T, dt=I32)
        dstf = A(T)
        typf = A(T)
        lo_i = A(T, dt=I32)
        hi_i = A(T, dt=I32)
        lo = A(T, dt=BF16)
        hi = A(T, dt=BF16)
        same = A(T)
        prev_last = A(1, dt=I32)
        prev_lastf = A(1)
        iota = A(P, dt=BF16)
        iota_i = A(P, dt=I32)
        nul = A(P, dt=BF16)
        spare_start = A(NB)
        spare_row = A(1)
        lane_base = A(1)
        hot_lo = [A(HALF, P, dt=BF16) for _ in range(2)]
        hot_hi = [A(HALF, NB, dt=BF16) for _ in range(2)]
        deg, tot, incl, end1, tmp, ones_nb = (A(NB) for _ in range(6))
        count, firstf, whole = A(1), A(1), A(1)
        zeros = A(BODY * D)
        neutral = A(R1 + D)
        w_nat = A(SLOTS, P)

        fixed = sem("fixed_parts_set")
        const = sem("constants_made")
        l_dst, l_edge, l_x, l_prev = sem("dst_loaded"), sem("edges_loaded"), sem("x_loaded"), sem("prev_loaded")
        l_w, l_small = sem("weights_loaded"), sem("small_loaded")
        zeroed, tabs_zeroed = sem("scratch_zeroed"), sem("tables_zeroed")
        prep = sem("edge_parts")
        hot_free = [sem(f"hot_free{h}") for h in range(2)]
        hot_made = [sem(f"hot_made{h}") for h in range(2)]
        deg_done, cum_done, whole_done = sem("degrees_counted"), sem("degrees_summed"), sem("whole_spread")
        wt_done, wt_kept = sem("weights_turned"), sem("weights_kept")
        xt_done, xt_kept = sem("x_turned"), sem("x_kept")
        scattered = sem("x_scattered")
        ps = m.psum
        WGROUPS = SLOTS // 4

        (S_DSTF, S_LOI, S_HII, S_LO, S_HI, S_PREV) = range(1, 7)

        with nc.Block() as block:

            @block.gpsimd
            def _(eng):
                eng.memset(zeros, 0.0).then_inc(const, 1)
                eng.iota(iota_i, [[1, P]], base=0, channel_multiplier=0).then_inc(const, 1)
                eng.memset(nul, 0.0).then_inc(const, 1)
                eng.memset(m.ones[:, :], 1.0).then_inc(const, 1)
                eng.wait_ge(const, 4)
                eng.affine_select(out=m.ident[:, :], in_=m.ones[:, :], compare_op=ALU.is_equal, fill=0.0, base=0,
                                  pattern=[[-1, P]], channel_multiplier=1).then_inc(const, 1)
                eng.affine_select(out=m.lower[:, :], in_=m.ones[:, :], compare_op=ALU.is_gt, fill=0.0, base=0,
                                  pattern=[[-1, P]], channel_multiplier=1).then_inc(const, 1)
                eng.affine_select(out=m.tri[:, :], in_=m.ones[:, :], compare_op=ALU.is_ge, fill=0.0, base=0,
                                  pattern=[[1, P]], channel_multiplier=-1).then_inc(const, 1)
                eng.iota(spare_start, [[P, NB]], base=EP, channel_multiplier=1,
                         allow_small_or_imprecise_dtypes=True).then_inc(const, 1)
                eng.iota(m.spare[:, :], [[1, 1]], base=NP, channel_multiplier=1,
                         allow_small_or_imprecise_dtypes=True).then_inc(const, 1)
                eng.iota(spare_row, [[1, 1]], base=EP + 1, channel_multiplier=1,
                         allow_small_or_imprecise_dtypes=True).then_inc(const, 1)
                eng.iota(lane_base, [[1, 1]], base=-1, channel_multiplier=T,
                         allow_small_or_imprecise_dtypes=True).then_inc(const, 1)
                eng.memset(m.eps[:, :], EPS).then_inc(const, 1)
                eng.memset(ones_nb, 1.0).then_inc(const, 1)
                eng.memset(neutral[:, 0:R1], 0.0).then_inc(const, 1)
                eng.wait_ge(const, 14)
                eng.memset(neutral[:, R1 - RH:R1 + D], -BIG).then_inc(const, 1)
                eng.wait_ge(l_x, 32)
                eng.wait_ge(zeroed, 16 * ZEROS)
                eng.wait_ge(prep, S_START)
                for b in range(NB):
                    eng.indirect_dma_start(out=m.seg_rows[:, :],
                                           out_offset=bass.IndirectOffsetOnAxis(ap=m.start[:, b:b + 1], axis=0),
                                           in_=m.xN[:, b, :], in_offset=None).then_inc(scattered, 16)
                eng.wait_ge(scattered, 16 * NB)

            @block.sync
            def _(eng):
                eng.wait_ge(fixed, 6)
                for tile, name, s in ((dst, "dst", l_dst), (m.src[:, 0:T], "src", l_edge),
                                      (typ, "edge_type_4", l_edge), (m.val[:, :], "edge_weight", l_edge)):
                    eng.dma_start(tile[0:112, :], I[name][0:112 * T].rearrange("(p t) -> p t", t=T)).then_inc(s, 16)
                    eng.dma_start(tile[112:127, :], I[name][112 * T:127 * T].rearrange("(p t) -> p t", t=T)).then_inc(s, 16)
                    eng.dma_start(tile[127:128, 0:LAST], I[name][127 * T:E].rearrange("(p t) -> p t", p=1)).then_inc(s, 16)
                eng.dma_start(prev_last[1:P, :], I["dst"][0:(P - 1) * T].rearrange("(p t) -> p t", t=T)[:, T - 1:T],
                              allow_slow_non_contiguous=True).then_inc(l_prev, 16)
                eng.dma_start(m.xN[:, 0:NB - 1, :], I["x"][0:(NB - 1) * P, :].rearrange("(b p) f -> p b f", p=P)).then_inc(l_x, 16)
                eng.dma_start(m.xN[0:TAIL, NB - 1, :], I["x"][(NB - 1) * P:N, :]).then_inc(l_x, 16)
                eng.wait_ge(const, 15)
                eng.dma_start(m.rows1[EP:EP + 1, :], neutral[0:1, 0:R1]).then_inc(zeroed, 16)
                eng.dma_start(m.rows2[EP:EP + 1, :], neutral[0:1, R1 - RH - D - H2:R1 - RH + H2]).then_inc(zeroed, 16)
                eng.dma_start(m.rows3[EP:EP + 1, :], neutral[0:1, R1:R1 + D]).then_inc(zeroed, 16)

                for rows, width in ((m.rows1, R1), (m.rows2, R2), (m.rows3, D)):
                    eng.dma_start(rows[EP + 1:EP + 1 + P, :], zeros[:, 0:width]).then_inc(zeroed, 16)

            @block.scalar
            def _(eng):
                for s, name in enumerate(TRANSPOSED):
                    eng.dma_start(w_nat[:, s, :], I[name]).then_inc(l_w, 16)
                eng.dma_start(w_nat[:, LIN1:LIN2, :], I["L2_gnn_lin1_w"].rearrange("(j o) i -> o j i", o=P)).then_inc(l_w, 16)
                eng.dma_start(w_nat[:, LIN2:SLOTS, :], I["L2_gnn_lin2_w"].rearrange("o (j i) -> o j i", i=P)).then_inc(l_w, 16)
                eng.wait_ge(const, 1)
                eng.wait_ge(l_dst, 48)
                with eng.Fori(0, TURNS) as i:
                    eng.dma_start(lanes(m.seg_rows)[:, bass.ds(i * BODY, BODY), :].rearrange("p t f -> p (t f)"), zeros).then_inc(zeroed, 16)
                for c, name in enumerate(COLUMNS):
                    eng.dma_start(m.cols[:, c:c + 1], I[name].rearrange("(p a) -> p a", a=1), allow_slow_non_contiguous=True).then_inc(l_small, 16)
                eng.dma_start(m.lin1_b[:, :], I["L2_gnn_lin1_b"].rearrange("(j p) -> p j", p=P), allow_slow_non_contiguous=True).then_inc(l_small, 16)
                for r, name in enumerate(ROWS):
                    eng.dma_start(m.rows[:, r, :], I[name].partition_broadcast(P)).then_inc(l_small, 16)
                eng.dma_start(m.w_rel[:, :, :], I["L1_gnn_W"].rearrange("r i o -> i r o")).then_inc(l_small, 16)
                for k, (name, at) in enumerate((("L3_gnn_Wm", 0), ("L3_gnn_Wm", D), ("L3_gnn_W1", 0), ("L3_gnn_W1", D), ("L3_gnn_W2", 0))):
                    eng.dma_start(m.w3[:, k, :], I[name][at:at + D, :]).then_inc(l_small, 16)
                eng.dma_start(m.edge_w[:, :], I["L3_gnn_Wm"][2 * D, :].partition_broadcast(P)).then_inc(l_small, 16)
                for g in range(WGROUPS):
                    eng.wait_ge(wt_done, g + 1)
                    eng.activation(m.wt[:, 4 * g:4 * g + 4, :], ps[:, g, :].rearrange("p (a b) -> p a b", b=P), ACT.Copy).then_inc(wt_kept, 1)
                for k, (c, w) in enumerate(CHUNKS):
                    eng.wait_ge(xt_done, k + 1)
                    eng.activation(m.xT[:, c:c + w], ps[:, k % 2, 0:w], ACT.Copy).then_inc(xt_kept, 1)
                eng.wait_ge(l_small, 16 * SMALL)
                eng.wait_ge(zeroed, 16 * ZEROS)
                for j in range(TABS):
                    eng.dma_start(m.tabs[j][0:NP, :].rearrange("(p r) f -> p (r f)", p=P), zeros[:, 0:NB * D]).then_inc(tabs_zeroed, 16)
                eng.wait_ge(tabs_zeroed, 16 * TABS)

            @block.tensor
            def _(eng):
                eng.wait_ge(const, 15)
                eng.matmul(ps[:, 7, 0:NB], nul, nul[:, 0:NB], start=True, stop=False)
                for h in range(2):
                    eng.nop().then_inc(hot_free[h], 1)
                with eng.Fori(0, TURNS) as i:
                    for h in range(2):
                        eng.wait_ge(hot_made[h], 2 * i + 2)
                        for j in range(HALF):
                            t = eng.matmul(ps[:, 7, 0:NB], hot_lo[h][:, j, :], hot_hi[h][:, j, :], start=False, stop=False,
                                           skip_group_check=True)
                        t.then_inc(hot_free[h], 1)
                eng.matmul(ps[:, 7, 0:NB], nul, nul[:, 0:NB], start=False, stop=True).then_inc(deg_done, 1)
                eng.wait_ge(prep, S_DEG)
                eng.matmul(ps[:, 6, 0:NB], m.tri[:, :], deg, start=True, stop=True)
                eng.matmul(ps[:, 6, 64:64 + NB], m.ones[:, :], deg, start=True, stop=True).then_inc(cum_done, 1)
                eng.wait_ge(prep, S_WHOLE)
                eng.matmul(ps[:, 5, 0:P], whole.broadcast_to([P, P]), m.ident[:, :], start=True, stop=True).then_inc(whole_done, 1)
                eng.wait_ge(l_w, 16 * (len(TRANSPOSED) + 2))
                for g in range(WGROUPS):
                    for k in range(4):
                        t = eng.transpose(ps[:, g, k * P:k * P + P], w_nat[:, 4 * g + k, :], m.ident[:, :])
                    t.then_inc(wt_done, 1)
                eng.wait_ge(l_x, 32)
                for k, (c, w) in enumerate(CHUNKS):
                    eng.wait_ge(wt_kept, 2)
                    if k >= 2:
                        eng.wait_ge(xt_kept, k - 1)
                    for b in range(w // P):
                        t = eng.transpose(ps[:, k % 2, b * P:b * P + P], m.xN[:, c // P + b, :], m.ident[:, :])
                    t.then_inc(xt_done, 1)

            @block.vector
            def _(eng):
                eng.memset(dst[96:P, LAST:T], NP - 1).then_inc(fixed, 1)
                eng.memset(m.src[:, LAST:T + AHEAD], 0).then_inc(fixed, 1)
                eng.memset(typ[96:P, LAST:T], 0).then_inc(fixed, 1)
                eng.memset(m.val[96:P, LAST:T], 0.0).then_inc(fixed, 1)
                eng.memset(prev_last, -1).then_inc(fixed, 1)
                eng.memset(m.xN[:, NB - 1, :], 0.0).then_inc(fixed, 1)
                eng.wait_ge(l_dst, 48)
                eng.tensor_copy(dstf, dst).then_inc(prep, 1)
                eng.tensor_scalar(lo_i, dst, P - 1, None, ALU.bitwise_and).then_inc(prep, 1)
                eng.tensor_scalar(hi_i, dst, 7, None, ALU.logical_shift_right).then_inc(prep, 1)
                eng.wait_ge(prep, S_LOI)
                eng.tensor_copy(lo, lo_i).then_inc(prep, 1)
                eng.wait_ge(prep, S_HII)
                eng.tensor_copy(hi, hi_i).then_inc(prep, 1)
                eng.wait_ge(const, 15)
                eng.tensor_copy(iota, iota_i).then_inc(prep, 1)
                eng.wait_ge(prep, S_PREV)
                with eng.Fori(0, TURNS) as i:
                    for h in range(2):
                        eng.wait_ge(hot_free[h], i + 1)
                        eng.tensor_tensor(hot_lo[h], spread(iota, 1, [P, HALF, P]),
                                          spread(lo[:, bass.ds(i * BODY + h * HALF, HALF)], 2, [P, HALF, P]), ALU.is_equal).then_inc(hot_made[h], 1)
                        eng.tensor_tensor(hot_hi[h], spread(iota[:, 0:NB], 1, [P, HALF, NB]),
                                          spread(hi[:, bass.ds(i * BODY + h * HALF, HALF)], 2, [P, HALF, NB]), ALU.is_equal).then_inc(hot_made[h], 1)
                n = S_PREV

                def step(ins):
                    nonlocal n
                    n += 1
                    ins.then_inc(prep, 1)
                    eng.wait_ge(prep, n)
                    return n

                eng.wait_ge(deg_done, 1)
                assert step(eng.tensor_copy(deg, ps[:, 7, 0:NB])) == S_DEG
                eng.wait_ge(cum_done, 1)
                step(eng.tensor_copy(tot, ps[:, 6, 64:64 + NB]))
                step(eng.tensor_tensor_scan(incl, ones_nb, tot, 0.0, ALU.mult, ALU.add))
                step(eng.tensor_tensor(incl, incl, tot, ALU.subtract))
                step(eng.tensor_tensor(end1, ps[:, 6, 0:NB], incl, ALU.add))
                step(eng.tensor_scalar(m.has[:, :], deg, 1.0, None, ALU.min))
                step(eng.tensor_tensor(tmp, end1, deg, ALU.subtract))
                step(eng.tensor_tensor(tmp, tmp, spare_start, ALU.subtract))
                step(eng.tensor_tensor(tmp, tmp, m.has[:, :], ALU.mult))
                assert step(eng.tensor_tensor(m.start[:, :], tmp, spare_start, ALU.add)) == S_START
                step(eng.scalar_tensor_tensor(out=tmp, in0=end1, scalar=float(-1 - EP), in1=m.has[:, :], op0=ALU.add, op1=ALU.mult))
                step(eng.tensor_scalar(m.end[:, :], tmp, float(EP), None, ALU.add))
                eng.wait_ge(l_prev, 16)
                step(eng.tensor_copy(prev_lastf, prev_last))
                assert step(eng.tensor_tensor(whole, dstf[:, T - 1:T], prev_lastf, ALU.is_equal)) == S_WHOLE
                step(eng.tensor_tensor(m.keep[:, 1:T], dstf[:, 1:T], dstf[:, 0:T - 1], ALU.is_equal))
                step(eng.tensor_tensor(m.keep[:, 0:1], dstf[:, 0:1], prev_lastf, ALU.is_equal))
                step(eng.memset(m.keep[:, T:T + BODY], 0.0))
                step(eng.tensor_scalar(m.reset[:, :], m.keep[:, :], -1.0, BIG, ALU.add, ALU.mult))
                step(eng.tensor_scalar(same, dstf, dstf[:, 0:1], None, ALU.is_equal))
                step(eng.tensor_reduce(count, same, AX.X, ALU.add))
                step(eng.tensor_tensor(firstf, count, lane_base, ALU.add))
                step(eng.tensor_copy(m.first_end[:, :], firstf))
                step(eng.tensor_tensor(firstf, firstf, spare_row, ALU.subtract))
                step(eng.tensor_tensor(firstf, firstf, m.keep[:, 0:1], ALU.mult))
                step(eng.tensor_tensor(m.first_fix[:, :], firstf, spare_row, ALU.add))
                step(eng.tensor_copy(m.lane_first[:, :], dst[:, 0:1]))
                eng.wait_ge(l_edge, 16 * 9)
                step(eng.tensor_copy(same, m.src[:, 0:T]))
                step(eng.tensor_copy(typf, typ))
                step(eng.scalar_tensor_tensor(out=m.src_rel[:, 0:T], in0=same, scalar=float(REL), in1=typf, op0=ALU.mult, op1=ALU.add))
                step(eng.memset(m.src_rel[:, T:T + AHEAD], 0))
                for r in range(REL):
                    step(eng.tensor_scalar(m.other_rel[:, :, r], typf, float(r), -BIG, ALU.not_equal, ALU.mult))
                eng.wait_ge(whole_done, 1)
                step(eng.tensor_scalar(m.whole_neg[:, :], ps[:, 5, 0:P], -1.0, BIG, ALU.add, ALU.mult))


S_DEG = 7
S_START = 16
S_WHOLE = 20
ZEROS = TURNS + 6
SMALL = len(COLUMNS) + 1 + len(ROWS) + 1 + 5 + 1


def layer0_edges(nc, m, I):
    with phase(nc, "layer0_edges") as sem:
        A = Arena(m)
        xr = [A(HALF, D) for _ in range(2)]
        xv = [A(SEVEN, D) for _ in range(2)]
        eq = [A(SEVEN, P) for _ in range(2)]
        before = A(SEVEN, P)
        rows = [A(SEVEN, D) for _ in range(4)]
        idx = [A(SEVEN, dt=I32) for _ in range(4)]
        srcs = A(BODY)
        vals = A(BODY)
        keeps = A(BODY)
        to_spare = A(BODY)
        rank = A(SEVEN)
        ranks = A(SEVEN)
        ps = m.psum

        def spread_bank(u):
            return ps[:, 2 * (u % 2):2 * (u % 2) + 2, :].rearrange("p a (b c) -> p (a b) c", c=P)[:, 0:SEVEN, :]

        def sum_bank(u):
            return ps[:, 4 + 2 * (u % 2):6 + 2 * (u % 2), :].rearrange("p a (b c) -> p (a b) c", c=P)[:, 0:SEVEN, :]

        first = sem("lane_first_row")
        landed = [sem(f"x_rows_landed{h}") for h in range(2)]
        carried = sem("x_carried")
        staged = sem("marks_staged")
        vals_staged = sem("weights_staged")
        weighed = sem("x_weighed")
        sources = sem("sources_spread")
        eq_made = sem("eq_made")
        ranked = sem("ranks")
        summed = sem("rows_summed")
        kept = sem("rows_kept")
        added = [sem(f"added{j}") for j in range(TABS)]
        UN = BODY // SEVEN
        RANK = 5

        zeros = A(T * 4)
        cleared = sem("zeros_set")
        dst_cleared = sem("dst_scores_cleared")
        unit_added = sem("units_added")

        with nc.Block() as block:

            @block.sync
            def _(eng):
                def load(h, t):
                    eng.dma_start(xr[h], lanes(m.seg_rows)[:, t, :]).then_inc(landed[h], 16)

                load(0, bass.ds(0, HALF))
                with eng.Fori(0, TURNS - 1) as i:
                    hold(eng, carried, i * BODY + 2)
                    hold(eng, weighed, i * BODY + 1)
                    load(1, bass.ds(i * BODY + HALF, HALF))
                    hold(eng, carried, i * BODY + HALF + 2)
                    hold(eng, weighed, i * BODY + HALF + 1)
                    load(0, bass.ds(i * BODY + BODY, HALF))
                hold(eng, carried, (TURNS - 1) * BODY + 2)
                hold(eng, weighed, (TURNS - 1) * BODY + 1)
                load(1, bass.ds((TURNS - 1) * BODY + HALF, HALF))
                eng.wait_ge(cleared, 1)
                for k in range(RH // 4):
                    eng.dma_start(m.seg_dst[0:EP, :].rearrange("(p t) f -> p (t f)", p=P)[:, k * T * 4:(k + 1) * T * 4],
                                  zeros[:, 0:T * 4]).then_inc(dst_cleared, 16)
                eng.wait_ge(dst_cleared, 16 * (RH // 4))

            @block.gpsimd
            def _(eng):
                eng.indirect_dma_start(out=xr[1][:, HALF - 1, :], out_offset=None, in_=I["x"],
                                       in_offset=bass.IndirectOffsetOnAxis(ap=m.lane_first[:, 0:1], axis=0)).then_inc(first, 16)
                eng.wait_ge(cleared, 1)
                for j in range(TABS):
                    eng.dma_start(m.tabs[j][NP:NP + P, :], zeros[:, 0:D]).then_inc(added[j], 16)
                with eng.Fori(0, TURNS) as i:
                    for u in range(UN):
                        eng.wait_ge(kept, i * UN + u + 3)
                        eng.wait_ge(ranked, (i * UN + u + 1) * RANK + 1)
                        for k in range(SEVEN):
                            s = u * SEVEN + k
                            j = s % TABS
                            hold(eng, added[j], 16 * (i * (BODY // TABS) + s // TABS) + 16)
                            if k == TABS - 1:
                                eng.nop().then_inc(unit_added, 1)
                            eng.indirect_dma_start(out=m.tabs[j], out_offset=bass.IndirectOffsetOnAxis(ap=idx[u][:, k:k + 1], axis=0),
                                                   in_=rows[u][:, k, :], in_offset=None, compute_op=ALU.add).then_inc(added[j], 16)
                for j in range(TABS):
                    eng.wait_ge(added[j], 16 + 16 * (TURNS * BODY // TABS))

            @block.vector
            def _(eng):
                eng.memset(zeros, 0.0).then_inc(cleared, 1)
                eng.engine_nop().then_inc(unit_added, UN)
                eng.engine_nop().then_inc(carried, 1)
                eng.engine_nop().then_inc(ranked, 1)
                eng.engine_nop().then_inc(eq_made, 2)
                eng.wait_ge(first, 16)
                with eng.Fori(0, TURNS) as i:
                    eng.wait_ge(carried, i * BODY + 1)
                    hold(eng, ranked, i * UN * RANK + 1)
                    eng.tensor_copy(keeps, m.keep[:, bass.ds(i * BODY, BODY)]).then_inc(staged, 1)
                    eng.tensor_copy(srcs, m.src[:, bass.ds(i * BODY, BODY)]).then_inc(staged, 1)
                    eng.wait_ge(staged, 3 * i + 2)
                    eng.tensor_scalar(to_spare, srcs, -1.0, m.spare[:, 0:1], ALU.mult, ALU.add).then_inc(staged, 1)
                    eng.wait_ge(staged, 3 * i + 3)
                    for u in range(UN):
                        h = u // 2
                        if u % 2 == 0:
                            eng.wait_ge(landed[h], 16 * i + 16)
                        for k in range(SEVEN):
                            s = u * SEVEN + k
                            j = s % HALF
                            prev = xr[h][:, j - 1, :] if j else xr[1 - h][:, HALF - 1, :]
                            eng.wait_ge(carried, i * BODY + s + 1)
                            eng.scalar_tensor_tensor(out=xr[h][:, j, :], in0=prev, scalar=keeps[:, s:s + 1], in1=xr[h][:, j, :],
                                                     op0=ALU.mult, op1=ALU.add).then_inc(carried, 1)
                        eng.wait_ge(sources, i * UN + u + 1)
                        eng.wait_ge(summed, i * UN + u + 1)
                        eng.tensor_tensor(eq[u % 2], spread_bank(u), spread(srcs[:, u * SEVEN:(u + 1) * SEVEN], 2, [P, SEVEN, P]),
                                          ALU.is_equal).then_inc(eq_made, 1)
                        eng.wait_ge(eq_made, i * UN + u + 3)
                        eng.wait_ge(ranked, (i * UN + u) * RANK + 1)
                        at = (i * UN + u) * RANK
                        eng.tensor_tensor(before, eq[u % 2], spread(m.lower[:, :], 1, [P, SEVEN, P]), ALU.mult).then_inc(ranked, 1)
                        eng.wait_ge(ranked, at + 2)
                        eng.tensor_reduce(rank, before, AX.X, ALU.add).then_inc(ranked, 1)
                        eng.wait_ge(ranked, at + 3)
                        eng.tensor_scalar(ranks, rank, 1.0, None, ALU.min).then_inc(ranked, 1)
                        eng.wait_ge(ranked, at + 4)
                        eng.tensor_tensor(ranks, ranks, to_spare[:, u * SEVEN:(u + 1) * SEVEN], ALU.mult).then_inc(ranked, 1)
                        eng.wait_ge(ranked, at + 5)
                        eng.wait_ge(unit_added, i * UN + u + 2)
                        eng.tensor_tensor(idx[u], ranks, srcs[:, u * SEVEN:(u + 1) * SEVEN], ALU.add).then_inc(ranked, 1)

            @block.tensor
            def _(eng):
                eng.nop().then_inc(summed, 2)
                with eng.Fori(0, TURNS) as i:
                    eng.wait_ge(staged, 3 * i + 3)
                    for u in range(UN + 1):
                        if u < UN:
                            eng.wait_ge(eq_made, i * UN + u + 1)
                            for k in range(SEVEN):
                                s = u * SEVEN + k
                                t = eng.matmul(spread_bank(u)[:, k, :], srcs[:, s:s + 1].broadcast_to([P, P]), m.ident[:, :], start=True, stop=True)
                            t.then_inc(sources, 1)
                        if u > 0:
                            v = u - 1
                            eng.wait_ge(eq_made, i * UN + v + 3)
                            eng.wait_ge(weighed, i * BODY + (v + 1) * SEVEN + 1)
                            eng.wait_ge(kept, i * UN + v + 1)
                            for k in range(SEVEN):
                                t = eng.matmul(sum_bank(v)[:, k, :], eq[v % 2][:, k, :], xv[v % 2][:, k, :], start=True, stop=True)
                            t.then_inc(summed, 1)

            @block.scalar
            def _(eng):
                eng.nop().then_inc(weighed, 1)
                eng.nop().then_inc(kept, 2)
                with eng.Fori(0, TURNS) as i:
                    eng.activation(vals, m.val[:, bass.ds(i * BODY, BODY)], ACT.Copy).then_inc(vals_staged, 1)
                    eng.wait_ge(vals_staged, i + 1)
                    for u in range(UN + 1):
                        if u < UN:
                            eng.wait_ge(carried, i * BODY + (u + 1) * SEVEN + 1)
                            for k in range(SEVEN):
                                s = u * SEVEN + k
                                eng.activation(xv[u % 2][:, k, :], xr[s // HALF][:, s % HALF, :], ACT.Copy, scale=vals[:, s:s + 1]).then_inc(weighed, 1)
                        if u > 0:
                            v = u - 1
                            eng.wait_ge(summed, i * UN + v + 3)
                            eng.wait_ge(unit_added, i * UN + v + 2)
                            eng.activation(rows[v], sum_bank(v), ACT.Copy).then_inc(kept, 1)


TAB_TILES = 4


class Steps:

    def __init__(self, eng, sem, start=0):
        self.eng, self.sem, self.n = eng, sem, start

    def put(self, ins):
        ins.then_inc(self.sem, 1)
        self.n += 1

    def wait(self):
        self.eng.wait_ge(self.sem, self.n)

    def then(self, ins):
        self.put(ins)
        self.wait()


def blocks(k):
    return CHUNKS[k][0] // P, (CHUNKS[k][0] + CHUNKS[k][1]) // P


def in_turns(stages):
    for step in range(len(CHUNKS) + len(stages) - 1):
        for late, stage in reversed(list(enumerate(stages))):
            if stage and 0 <= step - late < len(CHUNKS):
                stage(step - late)


def layer0_nodes(nc, m, I):
    with phase(nc, "layer0_nodes") as sem:
        A = Arena(m)
        big = A(8 * NP)
        agg = [big[:, j * NP:(j + 1) * NP].rearrange("p (b f) -> p b f", f=D) for j in range(TABS)]
        aggT, uT, rT, oT = (big[:, j * NP:(j + 1) * NP] for j in range(4, 8))
        fT, hT, gT, h2T = (big[:, j * NP:(j + 1) * NP] for j in (1, 2, 3, 1))
        y = agg[0]
        bias = A(3)
        st_b = A(len(REALCH), 6)
        mv_b = A(2)
        sd_b, scale, shift = A(1), A(1), A(1)
        st_n = A(NB, 6)
        mv_n = A(NB, 2)
        sd_n = A(NB)
        attn = A(2, REL * D)
        fold = A(REL * D)
        w_att = A(2 * RH)
        ed = A(NB, RH)
        tab = [A(REL, HS) for _ in range(TAB_TILES)]
        ps = m.psum
        wt, col = m.wt, m.cols

        def c(name):
            k = COLUMNS.index(name)
            return col[:, k:k + 1]

        def w(name):
            return wt[:, TRANSPOSED.index(name), :]

        tabs_in = [sem(f"tables_landed{k}") for k in range(len(CHUNKS))]
        attn_in = sem("attention_landed")
        vec = sem("vector_steps")
        agg_made = sem("agg_made")
        agg_t, agg_k = sem("agg_turned"), sem("agg_kept")
        u_sum, u_made = sem("u_summed"), sem("u_made")
        r_sum, r_made, rx_made = sem("r_summed"), sem("r_made"), sem("rx_made")
        f_sum, f_made, o_made = sem("f_summed"), sem("f_made"), sem("o_made")
        var1, root1, scale1 = sem("variance1"), sem("root1"), sem("scale1")
        h_made = sem("h_made")
        g_sum, g_made = sem("g_summed"), sem("g_made")
        var2, root2, scale2 = sem("variance2"), sem("root2"), sem("scale2")
        h2_made = sem("h2_made")
        y_sum, y_made = sem("y_summed"), sem("y_made")
        varn, rootn, x_made = sem("node_variance"), sem("node_root"), sem("x_made")
        x_t, x_k = sem("x_turned2"), sem("x_kept2")
        att_made = sem("attention_folded")
        tab_sum, tab_h, tab_e = sem("table_summed"), sem("table_features"), sem("table_scores")
        ed_made = sem("dst_scores")
        stored = [sem(f"table_stored{k}") for k in range(TAB_TILES)]
        ed_stored, scattered = sem("dst_scores_stored"), sem("dst_scores_scattered")
        NCH = len(CHUNKS)

        with nc.Block() as block:

            @block.sync
            def _(eng):
                for k, name in enumerate(("L1_gnn_attn_src", "L1_gnn_attn_dst")):
                    eng.dma_start(attn[:, k, :], I[name].rearrange("r h d -> (r h d)").partition_broadcast(P)).then_inc(attn_in, 16)
                for k, (at, n) in enumerate(CHUNKS):
                    for j in range(TABS):
                        eng.dma_start(agg[j][:, at // P:(at + n) // P, :], m.tabs[j][at:at + n, :].rearrange("(b p) f -> p b f", p=P)).then_inc(tabs_in[k], 16)
                for b in range(NB):
                    eng.wait_ge(tab_h, b + 1)
                    eng.wait_ge(tab_e, b + 1)
                    eng.dma_start(m.table1.rearrange("(b p r) f -> b p r f", p=P, r=REL)[b], tab[b % TAB_TILES]).then_inc(stored[b % TAB_TILES], 16)
                eng.wait_ge(ed_made, NB)
                eng.dma_start(m.dst1.rearrange("(b p) f -> p b f", p=P), ed).then_inc(ed_stored, 16)
                eng.wait_ge(ed_stored, 16)
                for k in range(TAB_TILES):
                    eng.wait_ge(stored[k], 16 * len(range(k, NB, TAB_TILES)))

            @block.gpsimd
            def _(eng):
                for b in range(NB):
                    eng.wait_ge(ed_made, b + 1)
                    eng.indirect_dma_start(out=m.seg_dst, out_offset=bass.IndirectOffsetOnAxis(ap=m.start[:, b:b + 1], axis=0),
                                           in_=ed[:, b, :], in_offset=None).then_inc(scattered, 16)
                eng.wait_ge(scattered, 16 * NB)

            @block.tensor
            def _(eng):
                def turn_sum(k):
                    eng.wait_ge(agg_made, k + 1)
                    if k >= 2:
                        eng.wait_ge(agg_k, k - 1)
                    for n, b in enumerate(range(*blocks(k))):
                        t = eng.transpose(ps[:, k % 2, n * P:(n + 1) * P], agg[0][:, b, :], m.ident[:, :])
                    t.then_inc(agg_t, 1)

                def gates(k):
                    at, n = CHUNKS[k]
                    u, r = ps[:, 2 + k % 2, 0:n], ps[:, 4 + k % 2, 0:n]
                    if k >= 2:
                        eng.wait_ge(u_made, k - 1)
                        eng.wait_ge(r_made, k - 1)
                    eng.matmul(u, w("L0_gnn_U1w"), m.xT[:, at:at + n], start=True, stop=False)
                    eng.matmul(r, w("L0_gnn_U2w"), m.xT[:, at:at + n], start=True, stop=False)
                    eng.wait_ge(agg_k, k + 1)
                    eng.matmul(u, w("L0_gnn_W1w"), aggT[:, at:at + n], start=False, stop=True).then_inc(u_sum, 1)
                    eng.matmul(r, w("L0_gnn_W2w"), aggT[:, at:at + n], start=False, stop=True).then_inc(r_sum, 1)

                in_turns((turn_sum, gates))
                for k, (at, n) in enumerate(CHUNKS):
                    f = ps[:, 6 + k % 2, 0:n]
                    if k >= 2:
                        eng.wait_ge(f_made, k - 1)
                    eng.matmul(f, w("L0_gnn_W3w"), aggT[:, at:at + n], start=True, stop=False)
                    eng.wait_ge(rx_made, k + 1)
                    eng.matmul(f, w("L0_gnn_U3w"), rT[:, at:at + n], start=False, stop=True).then_inc(f_sum, 1)
                eng.wait_ge(agg_k, NCH)
                for k, (at, n) in enumerate(CHUNKS):
                    eng.wait_ge(h_made, k + 1)
                    if k >= 2:
                        eng.wait_ge(g_made, k - 1)
                    eng.matmul(ps[:, k % 2, 0:n], w("L0_gnn_m_w0"), hT[:, at:at + n], start=True, stop=True).then_inc(g_sum, 1)
                eng.wait_ge(u_made, NCH)
                def second_map(k):
                    eng.wait_ge(h2_made, k + 1)
                    if k >= 2:
                        eng.wait_ge(y_made, k - 1)
                    for n, b in enumerate(range(*blocks(k))):
                        t = eng.matmul(ps[:, 2 + k % 2, n * P:(n + 1) * P], h2T[:, b * P:(b + 1) * P], w("L0_gnn_m_w1"), start=True, stop=True)
                    t.then_inc(y_sum, 1)

                def turn(k):
                    eng.wait_ge(x_made, k + 1)
                    if k >= 2:
                        eng.wait_ge(x_k, k - 1)
                    for n, b in enumerate(range(*blocks(k))):
                        t = eng.transpose(ps[:, k % 2, n * P:(n + 1) * P], m.xN[:, b, :], m.ident[:, :])
                    t.then_inc(x_t, 1)

                def tables(k):
                    eng.wait_ge(x_k, k + 1)
                    for b in range(*blocks(k)):
                        if b >= 2:
                            eng.wait_ge(tab_h, b - 1)
                            eng.wait_ge(ed_made, b - 1)
                        xb = m.xT[:, b * P:b * P + P]
                        eng.matmul(ps[:, 4 + b % 2, :], xb, m.w_rel[:, :, :].rearrange("p r f -> p (r f)"), start=True, stop=True)
                        eng.matmul(ps[:, 6 + b % 2, 0:2 * RH], xb, w_att, start=True, stop=True).then_inc(tab_sum, 1)

                eng.wait_ge(g_made, NCH)
                eng.wait_ge(r_made, NCH)
                eng.wait_ge(f_made, NCH)
                eng.wait_ge(att_made, 1)
                in_turns((second_map, None, None, turn, tables))

            @block.scalar
            def _(eng):
                def turned_sum(k):
                    at, n = CHUNKS[k]
                    eng.wait_ge(agg_t, k + 1)
                    eng.activation(aggT[:, at:at + n], ps[:, k % 2, 0:n], ACT.Copy).then_inc(agg_k, 1)

                def gates(k):
                    at, n = CHUNKS[k]
                    eng.wait_ge(u_sum, k + 1)
                    eng.activation(uT[:, at:at + n], ps[:, 2 + k % 2, 0:n], ACT.Relu, bias=bias[:, 0:1]).then_inc(u_made, 1)
                    eng.wait_ge(r_sum, k + 1)
                    eng.activation(rT[:, at:at + n], ps[:, 4 + k % 2, 0:n], ACT.Relu, bias=bias[:, 1:2]).then_inc(r_made, 1)

                eng.wait_ge(vec, 3)
                in_turns((turned_sum, gates))
                for k, (at, n) in enumerate(CHUNKS):
                    eng.wait_ge(f_sum, k + 1)
                    eng.activation(fT[:, at:at + n], ps[:, 6 + k % 2, 0:n], ACT.Tanh, bias=bias[:, 2:3]).then_inc(f_made, 1)
                eng.wait_ge(var1, 1)
                eng.activation(sd_b, mv_b[:, 1:2], ACT.Sqrt, bias=m.eps[:, 0:1]).then_inc(root1, 1)
                eng.wait_ge(scale1, 1)
                for k, (at, n) in enumerate(CHUNKS):
                    eng.activation(hT[:, at:at + n], oT[:, at:at + n], ACT.Relu, bias=shift, scale=scale).then_inc(h_made, 1)
                for k, (at, n) in enumerate(CHUNKS):
                    eng.wait_ge(g_sum, k + 1)
                    eng.activation(gT[:, at:at + n], ps[:, k % 2, 0:n], ACT.Identity, bias=c("L0_gnn_m_b0")).then_inc(g_made, 1)
                eng.wait_ge(var2, 1)
                eng.activation(sd_b, mv_b[:, 1:2], ACT.Sqrt, bias=m.eps[:, 0:1]).then_inc(root2, 1)
                eng.wait_ge(scale2, 1)
                for k, (at, n) in enumerate(CHUNKS):
                    eng.activation(h2T[:, at:at + n], gT[:, at:at + n], ACT.Relu, bias=shift, scale=scale).then_inc(h2_made, 1)

                def root(k):
                    b0, b1 = blocks(k)
                    eng.wait_ge(varn, k + 1)
                    eng.activation(sd_n[:, b0:b1], mv_n[:, b0:b1, 1], ACT.Sqrt, bias=m.eps[:, 0:1]).then_inc(rootn, 1)

                def turned(k):
                    at, n = CHUNKS[k]
                    eng.wait_ge(x_t, k + 1)
                    eng.activation(m.xT[:, at:at + n], ps[:, k % 2, 0:n], ACT.Copy).then_inc(x_k, 1)

                def tables(k):
                    for b in range(*blocks(k)):
                        eng.wait_ge(tab_sum, b + 1)
                        if b >= TAB_TILES:
                            eng.wait_ge(stored[b % TAB_TILES], 16 * (b // TAB_TILES))
                        eng.activation(tab[b % TAB_TILES][:, :, 0:D], ps[:, 4 + b % 2, :].rearrange("p (r f) -> p r f", f=D), ACT.Copy).then_inc(tab_h, 1)

                in_turns((root, None, turned, tables))

            @block.vector
            def _(eng):
                v = Steps(eng, vec)
                for k, (a, b) in enumerate((("W1b", "U1b"), ("W2b", "U2b"), ("W3b", "U3b"))):
                    v.put(eng.tensor_tensor(bias[:, k:k + 1], c("L0_gnn_" + a), c("L0_gnn_" + b), ALU.add))
                eng.wait_ge(attn_in, 32)
                for k in range(2):
                    v.then(eng.tensor_tensor(fold, m.w_rel[:, :, :].rearrange("p r f -> p (r f)"), attn[:, k, :], ALU.mult))
                    v.then(eng.tensor_reduce(w_att[:, k * RH:(k + 1) * RH], fold.rearrange("p (a d) -> p a d", d=D1), AX.X, ALU.add))
                eng.engine_nop().then_inc(att_made, 1)
                v.then(eng.tensor_tensor(m.xN[:, :, :], m.xN[:, :, :], spread(m.rows[:, ROWS.index("L0_gnn_m_b1"), :], 1, [P, NB, D]), ALU.add))
                for k, (at, n) in enumerate(CHUNKS):
                    a = [t[:, at // P:(at + n) // P, :] for t in agg]
                    eng.wait_ge(tabs_in[k], 16 * TABS)
                    v.put(eng.tensor_tensor(a[0], a[0], a[1], ALU.add))
                    v.then(eng.tensor_tensor(a[2], a[2], a[3], ALU.add))
                    eng.tensor_tensor(a[0], a[0], a[2], ALU.add).then_inc(agg_made, 1)
                for k, (at, n) in enumerate(CHUNKS):
                    eng.wait_ge(r_made, k + 1)
                    eng.tensor_tensor(rT[:, at:at + n], rT[:, at:at + n], m.xT[:, at:at + n], ALU.mult).then_inc(rx_made, 1)
                def moments(made, x, k):
                    at, n = REALCH[k]
                    eng.wait_ge(made, k + 1)
                    v.put(eng.bn_stats(st_b[:, k, :], x[:, at:at + n]))

                def norm(var, root, scaled, g, b):
                    v.wait()
                    eng.bn_aggr(mv_b, st_b).then_inc(var, 1)
                    eng.wait_ge(root, 1)
                    v.then(eng.reciprocal(sd_b, sd_b))
                    v.then(eng.tensor_tensor(scale, sd_b, c(g), ALU.mult))
                    v.then(eng.tensor_tensor(sd_b, mv_b[:, 0:1], scale, ALU.mult))
                    eng.tensor_tensor(shift, c(b), sd_b, ALU.subtract).then_inc(scaled, 1)
                    eng.wait_ge(scaled, 1)

                for k, (at, n) in enumerate(CHUNKS):
                    f, o, x, u = (t[:, at:at + n] for t in (fT, oT, m.xT, uT))
                    eng.wait_ge(f_made, k + 1)
                    v.then(eng.tensor_tensor(f, f, x, ALU.subtract))
                    v.then(eng.tensor_tensor(f, f, u, ALU.mult))
                    eng.tensor_tensor(o, f, x, ALU.add).then_inc(o_made, 1)
                    moments(o_made, oT, k)
                norm(var1, root1, scale1, "L0_gnn_bn_g", "L0_gnn_bn_b")
                for k in range(NCH):
                    moments(g_made, gT, k)
                norm(var2, root2, scale2, "L0_gnn_m_bng", "L0_gnn_m_bnb")

                def outputs(k):
                    b0, b1 = blocks(k)
                    eng.wait_ge(y_sum, k + 1)
                    eng.tensor_tensor(y[:, b0:b1, :], ps[:, 2 + k % 2, 0:CHUNKS[k][1]].rearrange("p (b f) -> p b f", f=D), m.xN[:, b0:b1, :], ALU.add).then_inc(y_made, 1)
                    eng.wait_ge(y_made, k + 1)
                    for b in range(b0, b1):
                        v.put(eng.bn_stats(st_n[:, b, :], y[:, b, :]))
                    v.wait()
                    for b in range(b0, b1):
                        v.put(eng.bn_aggr(mv_n[:, b, :], st_n[:, b, :]))
                    v.wait()
                    eng.engine_nop().then_inc(varn, 1)

                def norm_behind(k):
                    b0, b1 = blocks(k)
                    eng.wait_ge(rootn, k + 1)
                    v.then(eng.reciprocal(sd_n[:, b0:b1], sd_n[:, b0:b1]))
                    for b in range(b0, b1):
                        v.put(eng.tensor_scalar(m.xN[:, b, :], y[:, b, :], mv_n[:, b, 0:1], sd_n[:, b:b + 1], ALU.subtract, ALU.mult))
                    v.wait()
                    eng.engine_nop().then_inc(x_made, 1)

                def scores(k):
                    for b in range(*blocks(k)):
                        eng.wait_ge(tab_sum, b + 1)
                        if b >= TAB_TILES:
                            eng.wait_ge(stored[b % TAB_TILES], 16 * (b // TAB_TILES))
                        sc = ps[:, 6 + b % 2, 0:2 * RH]
                        eng.tensor_copy(tab[b % TAB_TILES][:, :, D:HS], sc[:, 0:RH].rearrange("p (r h) -> p r h", h=H1)).then_inc(tab_e, 1)
                        eng.tensor_copy(ed[:, b, :], sc[:, RH:2 * RH]).then_inc(ed_made, 1)

                in_turns((outputs, None, norm_behind, None, scores))


class LoopSteps(Steps):

    def __init__(self, eng, sem, before):
        Steps.__init__(self, eng, sem)
        self.before = before

    def wait(self):
        self.eng.wait_ge(self.sem, self.before + self.n)


FLOOR = -1e28
COLS = HALF + 1


def maxima_step(eng, step, resets, e, fwd, top, gap):
    n = fwd.shape[1] * COLS

    def flat(t):
        return t.rearrange("p a t -> p (a t)")

    if step == 0:
        return eng.tensor_copy(e[:, :, 0:1], fwd[:, :, HALF:COLS])
    if step == 1:
        return eng.tensor_tensor_scan(flat(fwd), resets[:, 0:n], flat(e), -BIG, ALU.add, ALU.max)
    if step == 2:
        return eng.tensor_tensor_scan(flat(top)[:, ::-1], resets[:, 1:n + 1][:, ::-1], flat(fwd)[:, ::-1], -BIG, ALU.add, ALU.max)
    return eng.scalar_tensor_tensor(out=gap, in0=top, scalar=FLOOR, in1=e, op0=ALU.max, op1=ALU.subtract)


SCORES1 = 3 + 4
OLD1 = 3
SUMS1 = OLD1 + HALF
BY_DVE = 9
MASKED1 = REL * HALF - BY_DVE
WEIGHED1 = 3


def layer1_edges(nc, m, I):
    with phase(nc, "layer1_edges") as sem:
        A = Arena(m)
        states = A(2 * HALF * R1)
        rows = [states[:, h * HALF * R1:(h + 1) * HALF * R1].rearrange("p (t f) -> p t f", f=R1) for h in range(2)]
        ed_all = states[:, 0:T * RH].rearrange("p (t f) -> p t f", f=RH)
        ed = A(T, H1)
        apart = A(HALF, REL * D)
        feat = [A(HALF, HS) for _ in range(RING - 1)]
        W = HALF * HS
        feat.append(m.xT[:, 0:W].rearrange("p (t f) -> p t f", f=HS))
        e, fwd, *top = ([m.xT[:, W + k * RH * COLS:W + (k + 1) * RH * COLS].rearrange("p (a t) -> p a t", t=COLS) for k in range(5)]
                        + [A(RH, COLS)])
        gap = [A(RH, COLS) for _ in range(2)]
        ex = [A(RH, COLS) for _ in range(2)]
        sums = [A(RH, COLS) for _ in range(2)]
        weight = A(HALF, H1)
        score4 = A(HALF, H1)
        old = m.lane_end[:, 0:REL * D]
        keeps = [A(HALF) for _ in range(2)]
        all_keeps = [A(RH * COLS) for _ in range(2)]
        resets = [A(RH * COLS + 1) for _ in range(2)]
        hot = [A(HALF, REL) for _ in range(2)]
        idx = [A(HALF, dt=I32) for _ in range(RING)]
        ed_first = A(RH)
        SUM, MAX = REL * D, REL * D + RH

        ed_in, ed_first_in = [sem(f"dst_scores_landed{c}") for c in range(2)], sem("first_scores_landed")
        begun, ed_steps = sem("buffers_begun"), sem("dst_scores_steps")
        scored, weighed, summed = sem("score_steps"), sem("weight_steps"), sem("sum_steps")
        exped, hot_made, masked, filled = sem("exponentials"), sem("relations_staged"), sem("features_apart"), sem("state_columns_filled")
        marks, kept = sem("resets_staged"), sem("keeps_staged")
        staged = [sem(f"indices_staged{k}") for k in range(RING)]
        landed = [sem(f"features_landed{k}") for k in range(RING)]
        stored, rows_free = sem("states_stored"), sem("states_free")

        def nth(i, k):
            return i * RING + k

        def half(i, k):
            return (i + k // RING, k % RING)

        def sums_before(i, k):
            return i * (RING * SUMS1) + (k + 1) * SUMS1

        def weighed_before(i, k):
            return i * (RING * WEIGHED1) + (RING + k) * WEIGHED1

        def masked_before(i, k):
            return i * (RING * MASKED1) + (RING + k) * MASKED1

        def edges(i, k):
            return bass.ds(i * (RING * HALF) + k * HALF, HALF)

        def inner(t):
            return t[:, :, 1:COLS].rearrange("p a t -> p t a")

        with nc.Block() as block:

            @block.sync
            def _(eng):
                for c in range(2):
                    eng.dma_start(ed_all[:, c * T // 2:(c + 1) * T // 2, :], lanes(m.seg_dst)[:, c * T // 2:(c + 1) * T // 2, :]).then_inc(ed_in[c], 16)
                with eng.Fori(0, LOOPS) as i:
                    for k in range(RING):
                        hold(eng, summed, sums_before(i, k) + SUMS1)
                        hold(eng, filled, 2 * nth(i, k) + 4)
                        eng.dma_start(lanes(m.rows1)[:, edges(i, k), :], rows[k % 2]).then_inc(stored, 16)
                        hold(eng, stored, 16 * RING * i + 16 * k + 16)
                        eng.nop().then_inc(rows_free, 1)

            @block.gpsimd
            def _(eng):
                eng.indirect_dma_start(out=ed_first, out_offset=None, in_=m.dst1,
                                       in_offset=bass.IndirectOffsetOnAxis(ap=m.lane_first[:, 0:1], axis=0)).then_inc(ed_first_in, 16)
                with eng.Fori(0, LOOPS) as i:
                    for k in range(RING):
                        hold(eng, staged[k], i + 1)
                        hold(eng, masked, masked_before(i, k) - (RING - 1) * MASKED1)
                        hold(eng, weighed, weighed_before(i, k) - (RING - 1) * WEIGHED1)
                        for j in range(HALF):
                            eng.indirect_dma_start(out=feat[k][:, j, :], out_offset=None, in_=m.table1,
                                                   in_offset=bass.IndirectOffsetOnAxis(ap=idx[k][:, j:j + 1], axis=0)).then_inc(landed[k], 16)

            @block.scalar
            def _(eng):
                def over_heads(t):
                    return t[:, 0:RH * COLS].rearrange("p (a t) -> p a t", t=COLS)[:, :, 1:COLS]

                def stage_resets(i, k):
                    eng.activation(over_heads(resets[k % 2]), spread(m.reset[:, edges(i, k)], 1, [P, RH, HALF]), ACT.Copy).then_inc(marks, 1)

                def stage_keeps(i, k):
                    eng.activation(over_heads(all_keeps[k % 2]), spread(m.keep[:, edges(i, k)], 1, [P, RH, HALF]), ACT.Copy).then_inc(kept, 1)
                    eng.activation(keeps[k % 2], m.keep[:, edges(i, k)], ACT.Copy).then_inc(kept, 1)

                def fill(k):
                    eng.activation(rows[k % 2][:, :, SUM:MAX], inner(sums[k % 2]), ACT.Copy).then_inc(filled, 1)
                    eng.activation(rows[k % 2][:, :, MAX:R1], inner(top[k]), ACT.Copy).then_inc(filled, 1)

                for k in range(RING):
                    eng.activation(idx[k], m.src_rel[:, k * HALF:(k + 1) * HALF], ACT.Copy).then_inc(staged[k], 1)
                eng.nop().then_inc(masked, RING * MASKED1)
                eng.wait_ge(begun, 8)
                for k in range(2):
                    stage_resets(0, k)
                stage_keeps(0, 0)

                def exponentials(i, k):
                    hold(eng, landed[k], 16 * HALF * (i + 1))
                    eng.activation(idx[k], m.src_rel[:, edges(i, RING + k)], ACT.Copy).then_inc(staged[k], 1)
                    hold(eng, scored, SCORES1 * nth(i, k) + SCORES1 + 1)
                    hold(eng, masked, masked_before(i, k) - MASKED1)
                    eng.activation(hot[k % 2], m.other_rel[:, edges(i, k), :], ACT.Relu, bias=m.ones[:, 0:1]).then_inc(hot_made, 1)
                    eng.activation(ex[k % 2], gap[k % 2], ACT.Exp, scale=-1.0).then_inc(exped, 1)
                    stage_resets(*half(i, k + 2))

                def set_apart(i, k, ts):
                    for t in ts:
                        eng.wait_ge(summed, sums_before(i, k) - SUMS1 + OLD1 + t + 1)
                        for r in range(REL - (t < BY_DVE)):
                            eng.activation(apart[:, t, r * D:(r + 1) * D], feat[k][:, t, 0:D], ACT.Copy, scale=hot[k % 2][:, t, r:r + 1]).then_inc(masked, 1)

                def turn(i, last):
                    for k in range(RING):
                        eng.wait_ge(hot_made, nth(i, k) + 1)
                        eng.wait_ge(weighed, weighed_before(i, k) + 2)
                        set_apart(i, k, range(HALF // 2))
                        if k + 1 < RING or not last:
                            exponentials(*half(i, k + 1))
                        set_apart(i, k, range(HALF // 2, HALF))
                        hold(eng, summed, sums_before(i, k))
                        stage_keeps(*half(i, k + 1))
                        eng.wait_ge(rows_free, nth(i, k) + 1)
                        fill((k - 1) % RING)

                exponentials(0, 0)
                with eng.Fori(0, LOOPS - 1) as i:
                    turn(i, False)
                turn(LOOPS - 1, True)
                eng.wait_ge(summed, sums_before(LOOPS, 0))
                fill(RING - 1)

            @block.vector
            def _(eng):
                f = Steps(eng, begun)
                for h in range(2):
                    f.put(eng.memset(resets[h], -BIG))
                    f.put(eng.memset(all_keeps[h], 0.0))
                    f.put(eng.memset(sums[h], 0.0))
                f.put(eng.memset(fwd, -BIG))
                f.put(eng.memset(top[RING - 1], -BIG))
                eng.engine_nop().then_inc(rows_free, 3)
                eng.engine_nop().then_inc(scored, 1)
                eng.engine_nop().then_inc(weighed, RING * WEIGHED1)
                eng.engine_nop().then_inc(summed, SUMS1)
                eng.wait_ge(ed_first_in, 16)
                for c in range(2):
                    t0, t1 = c * T // 2, (c + 1) * T // 2
                    eng.wait_ge(ed_in[c], 16)
                    if c:
                        eng.wait_ge(ed_steps, RH)
                    for k in range(RH):
                        before = ed_all[:, t0 - 1, k:k + 1] if c else ed_first[:, k:k + 1]
                        eng.tensor_tensor_scan(ed_all[:, t0:t1, k], m.keep[:, t0:t1], ed_all[:, t0:t1, k], before, ALU.mult, ALU.add).then_inc(ed_steps, 1)
                eng.wait_ge(ed_steps, 2 * RH)
                ed4 = ed_all.rearrange("p t (r a) -> p t r a", a=H1)
                eng.tensor_tensor(ed4, ed4, spread(m.other_rel[:, :, :], 3, [P, T, REL, H1]), ALU.add).then_inc(ed_steps, 1)
                eng.wait_ge(ed_steps, 2 * RH + 1)
                f.then(eng.tensor_reduce(ed, ed_all.rearrange("p t (r a) -> p t a r", a=H1), AX.X, ALU.max))
                f.then(eng.memset(rows[1][:, HALF - 1, :], 0.0))

                def score(i, k, step):
                    now = e[:, :, 1:COLS]
                    eng.wait_ge(scored, SCORES1 * nth(i, k) + step + 1)
                    if step == 0:
                        eng.wait_ge(landed[k], 16 * HALF * (i + 1))
                        eng.wait_ge(marks, nth(i, k) + 1)
                        ins = eng.tensor_tensor(score4, feat[k][:, :, D:HS], ed[:, edges(i, k), :], ALU.add)
                    elif step == 1:
                        ins = eng.scalar_tensor_tensor(out=score4, in0=score4, scalar=0.2, in1=score4, op0=ALU.mult, op1=ALU.max)
                    elif step == 2:
                        ins = eng.tensor_tensor(now.rearrange("p (r a) t -> p t r a", a=H1), spread(score4, 2, [P, HALF, REL, H1]),
                                                spread(m.other_rel[:, edges(i, k), :], 3, [P, HALF, REL, H1]), ALU.add)
                    else:
                        ins = maxima_step(eng, step - 3, resets[k % 2], e, fwd, top[k], gap[k % 2])
                    ins.then_inc(scored, 1)

                def weigh(i, k, step):
                    if step == 0:
                        eng.wait_ge(exped, nth(i, k) + 1)
                        eng.tensor_reduce(weight, ex[k % 2][:, :, 1:COLS].rearrange("p (r a) t -> p t a r", a=H1), AX.X, ALU.add).then_inc(weighed, 1)
                    elif step > 1:
                        eng.wait_ge(weighed, weighed_before(i, k) + step)
                        eng.wait_ge(hot_made, nth(i, k) + 1)
                        eng.tensor_tensor(apart[:, 0:BY_DVE, (REL - 1) * D:], feat[k][:, 0:BY_DVE, 0:D],
                                          hot[k % 2][:, 0:BY_DVE, REL - 1:REL].broadcast_to([P, BY_DVE, D]), ALU.mult).then_inc(weighed, 1)
                    else:
                        eng.wait_ge(weighed, weighed_before(i, k) + 1)
                        by_head = feat[k][:, :, 0:D].rearrange("p t (a d) -> p t a d", d=D1)
                        eng.tensor_tensor(by_head, by_head, spread(weight, 3, [P, HALF, H1, D1]), ALU.mult).then_inc(weighed, 1)

                def add_up(i, k, weighs=True, scores=True):
                    v = LoopSteps(eng, summed, sums_before(i, k))
                    h = k % 2
                    row, before = rows[h], rows[1 - h][:, HALF - 1, :]
                    eng.wait_ge(rows_free, nth(i, k) + 2)
                    eng.wait_ge(kept, 2 * nth(i, k) + 2)
                    v.put(eng.tensor_tensor(old.rearrange("p (a d) -> p a d", d=D1), before[:, 0:SUM].rearrange("p (a d) -> p a d", d=D1),
                                            ex[h][:, :, 0:1].broadcast_to([P, RH, D1]), ALU.mult))
                    v.wait()
                    v.then(eng.tensor_tensor(ex[h][:, :, 0], ex[h][:, :, 0], sums[1 - h][:, :, HALF], ALU.mult))
                    v.put(eng.tensor_tensor_scan(sums[h].rearrange("p a t -> p (a t)"), all_keeps[h], ex[h].rearrange("p a t -> p (a t)"), 0.0, ALU.mult, ALU.add))
                    for j in range(HALF):
                        eng.wait_ge(masked, masked_before(i, k) + REL * (j + 1) - min(j + 1, BY_DVE))
                        if j == 0:
                            eng.wait_ge(weighed, weighed_before(i, k) + WEIGHED1)
                        v.wait()
                        v.put(eng.scalar_tensor_tensor(out=row[:, j, 0:SUM], in0=row[:, j - 1, 0:SUM] if j else old, scalar=keeps[h][:, j:j + 1],
                                                       in1=apart[:, j, :], op0=ALU.mult, op1=ALU.add))
                        if scores and j < SCORES1:
                            score(*half(i, k + 2), j)
                        if weighs and j == BY_DVE:
                            weigh(*half(i, k + 1), 2)
                        if scores and j >= HALF - 2:
                            weigh(*half(i, k + 2), j - (HALF - 2))
                    v.wait()
                    assert v.n == SUMS1

                for k in range(2):
                    for step in range(SCORES1):
                        score(0, k, step)
                for step in range(WEIGHED1):
                    weigh(0, 0, step)
                for step in range(2):
                    weigh(0, 1, step)
                with eng.Fori(0, LOOPS - 1) as i:
                    for k in range(RING):
                        add_up(i, k)
                for k in range(RING):
                    add_up(LOOPS - 1, k, weighs=k + 1 < RING, scores=k + 2 < RING)
                eng.wait_ge(filled, 2 * nth(LOOPS, 0) + 2)
                f.then(eng.tensor_copy(m.lane_end[:, 0:R1], rows[1][:, HALF - 1, :]))


def carry_sums(nc, m, states, chunks, heads):
    with phase(nc, f"carry_sums_{heads}") as sem:
        A = Arena(m)
        W, C, H, DH = chunks * P, chunks, heads, P // heads
        R = W + 2 * C * H
        wide = [A(3, P) for _ in range(C)]
        run = [A(3, P + 1) for _ in range(C)]
        ex = [A(2, P) for _ in range(C)]
        add = [A(2, P) for _ in range(C)]
        row = A(R)
        new_max = A(C * H)
        dm = A(2, C * H)
        part = A(W + C * H)
        ps = m.psum

        row_in, fixed = sem("first_rows_landed"), sem("first_rows_fixed")
        vec = sem("vector_steps")
        wide_made, turned = sem("states_spread"), sem("states_turned")
        exps_of, exped = sem("exponents"), sem("exponentials")
        run_made, back = sem("lanes_summed"), sem("lane_sums_turned")
        merge_of, merge_exp = sem("merge_exponents"), sem("merge_exponentials")
        merged = sem("rows_merged")

        def head(k, t):
            return t.rearrange("p (a d) -> p a d", d=DH)[:, :, 0]

        with nc.Block() as block:

            @block.gpsimd
            def _(eng):
                eng.indirect_dma_start(out=row, out_offset=None, in_=states,
                                       in_offset=bass.IndirectOffsetOnAxis(ap=m.first_end[:, 0:1], axis=0)).then_inc(row_in, 16)
                eng.wait_ge(merged, 1)
                eng.indirect_dma_start(out=states, out_offset=bass.IndirectOffsetOnAxis(ap=m.first_fix[:, 0:1], axis=0),
                                       in_=row, in_offset=None).then_inc(fixed, 16)
                eng.wait_ge(fixed, 16)

            @block.tensor
            def _(eng):
                for c in range(C):
                    eng.wait_ge(wide_made, c + 1)
                    for k in range(3):
                        t = eng.transpose(ps[:, c, k * P:(k + 1) * P], wide[c][:, k, :], m.ident[:, :])
                    t.then_inc(turned, 1)
                for c in range(C):
                    eng.wait_ge(run_made, c + 1)
                    for k in range(3):
                        t = eng.transpose(ps[:, 4 + c, k * P:(k + 1) * P], run[c][:, k, 0:P], m.ident[:, :])
                    t.then_inc(back, 1)

            @block.scalar
            def _(eng):
                for c in range(C):
                    eng.wait_ge(exps_of, c + 1)
                    eng.activation(ex[c], ex[c], ACT.Exp).then_inc(exped, 1)
                eng.wait_ge(merge_of, 1)
                eng.activation(dm, dm, ACT.Exp).then_inc(merge_exp, 1)

            @block.vector
            def _(eng):
                v = Steps(eng, vec)
                end = m.lane_end
                for c in range(C):
                    v.put(eng.tensor_copy(wide[c][:, 0, :], end[:, c * P:(c + 1) * P]))
                    for k in range(2):
                        at = W + k * C * H + c * H
                        v.put(eng.tensor_copy(wide[c][:, 1 + k, :].rearrange("p (a d) -> p a d", d=DH), spread(end[:, at:at + H], 2, [P, H, DH])))
                    v.put(eng.memset(run[c][:, 0:2, 0:1], 0.0))
                    v.put(eng.memset(run[c][:, 2, 0:1], -BIG))
                    v.wait()
                    eng.engine_nop().then_inc(wide_made, 1)
                for c in range(C):
                    eng.wait_ge(turned, c + 1)
                    v.then(eng.tensor_tensor_scan(run[c][:, 2, 1:P + 1], m.whole_neg[:, :], ps[:, c, 2 * P:3 * P], -BIG, ALU.add, ALU.max))
                    v.put(eng.tensor_tensor(ex[c][:, 1, :], ps[:, c, 2 * P:3 * P], run[c][:, 2, 1:P + 1], ALU.subtract))
                    v.then(eng.tensor_tensor(ex[c][:, 0, :], run[c][:, 2, 0:P], m.whole_neg[:, :], ALU.add))
                    v.then(eng.tensor_tensor(ex[c][:, 0, :], ex[c][:, 0, :], run[c][:, 2, 1:P + 1], ALU.subtract))
                    eng.engine_nop().then_inc(exps_of, 1)
                for c in range(C):
                    eng.wait_ge(exped, c + 1)
                    for k in range(2):
                        v.put(eng.tensor_tensor(add[c][:, k, :], ps[:, c, k * P:(k + 1) * P], ex[c][:, 1, :], ALU.mult))
                    v.wait()
                    for k in range(2):
                        v.put(eng.tensor_tensor_scan(run[c][:, k, 1:P + 1], ex[c][:, 0, :], add[c][:, k, :], 0.0, ALU.mult, ALU.add))
                    v.wait()
                    eng.engine_nop().then_inc(run_made, 1)
                eng.wait_ge(row_in, 16)
                for c in range(C):
                    eng.wait_ge(back, c + 1)
                    v.put(eng.tensor_tensor(new_max[:, c * H:(c + 1) * H], row[:, W + C * H + c * H:W + C * H + (c + 1) * H],
                                            head(c, ps[:, 4 + c, 2 * P:3 * P]), ALU.max))
                v.wait()
                v.put(eng.tensor_tensor(dm[:, 0, :], row[:, W + C * H:R], new_max, ALU.subtract))
                for c in range(C):
                    v.put(eng.tensor_tensor(dm[:, 1, c * H:(c + 1) * H], head(c, ps[:, 4 + c, 2 * P:3 * P]), new_max[:, c * H:(c + 1) * H], ALU.subtract))
                v.wait()
                eng.engine_nop().then_inc(merge_of, 1)
                eng.wait_ge(merge_exp, 1)
                v.put(eng.tensor_tensor(row[:, 0:W].rearrange("p (a d) -> p a d", d=DH), row[:, 0:W].rearrange("p (a d) -> p a d", d=DH),
                                        spread(dm[:, 0, :], 2, [P, C * H, DH]), ALU.mult))
                v.put(eng.tensor_tensor(row[:, W:W + C * H], row[:, W:W + C * H], dm[:, 0, :], ALU.mult))
                for c in range(C):
                    v.put(eng.tensor_tensor(part[:, c * P:(c + 1) * P].rearrange("p (a d) -> p a d", d=DH),
                                            ps[:, 4 + c, 0:P].rearrange("p (a d) -> p a d", d=DH),
                                            spread(dm[:, 1, c * H:(c + 1) * H], 2, [P, H, DH]), ALU.mult))
                    v.put(eng.tensor_tensor(part[:, W + c * H:W + (c + 1) * H], head(c, ps[:, 4 + c, P:2 * P]), dm[:, 1, c * H:(c + 1) * H], ALU.mult))
                v.wait()
                v.put(eng.tensor_tensor(row[:, 0:W + C * H], row[:, 0:W + C * H], part, ALU.add))
                v.put(eng.tensor_copy(row[:, W + C * H:R], new_max))
                v.wait()
                eng.engine_nop().then_inc(merged, 1)


def layer1_nodes(nc, m, I):
    with phase(nc, "layer1_nodes") as sem:
        A = Arena(m)
        SUM, MAX = REL * D, REL * D + RH
        st = A(NB, R1)
        fac = A(NB, RH)
        den = A(NB, RH)
        y = A(NB, D)
        st_n = A(NB, 6)
        mv_n = A(NB, 2)
        sd_n = A(NB)
        q2 = A(NB, D)
        kv = [A(4, 2 * D) for _ in range(2)]
        ps = m.psum

        def r(name):
            return m.rows[:, ROWS.index(name), :]

        def w(name):
            return m.wt[:, TRANSPOSED.index(name), :]

        kept_in = A(NB, D)
        shifted = A(NB, D)
        q_bias = A(D)
        NCH = len(CHUNKS)
        state_in = [sem(f"states_landed{k}") for k in range(NCH)]
        vec = sem("vector_steps")
        expo, exped = sem("exponents"), sem("exponentials")
        varn, rootn = [sem(f"node_variance{n}") for n in range(2)], [sem(f"node_root{n}") for n in range(2)]
        x_made = sem("x_made")
        x_t, x_k = sem("x_turned"), sem("x_kept")
        qkv_sum, q_made, kv_made = sem("qkv_summed"), sem("queries_made"), sem("keys_values_made")
        stored = [sem(f"keys_values_stored{k}") for k in range(2)]
        q_stored, scattered = sem("queries_stored"), sem("queries_scattered")

        with nc.Block() as block:

            @block.gpsimd
            def _(eng):
                for k in range(NCH):
                    for b in range(*blocks(k)):
                        eng.indirect_dma_start(out=st[:, b, :], out_offset=None, in_=m.rows1,
                                               in_offset=bass.IndirectOffsetOnAxis(ap=m.end[:, b:b + 1], axis=0)).then_inc(state_in[k], 16)
                for b in range(NB):
                    eng.wait_ge(q_made, b // 4 + 1)
                    eng.indirect_dma_start(out=m.seg_rows, out_offset=bass.IndirectOffsetOnAxis(ap=m.start[:, b:b + 1], axis=0),
                                           in_=q2[:, b, :], in_offset=None).then_inc(scattered, 16)
                eng.wait_ge(scattered, 16 * NB)

            @block.sync
            def _(eng):
                for k in range(NCH):
                    b0, b1 = blocks(k)
                    eng.wait_ge(kv_made, 2 * k + 2)
                    eng.dma_start(m.table2.rearrange("(b p) f -> p b f", p=P)[:, b0:b1, :], kv[k % 2][:, 0:b1 - b0, :]).then_inc(stored[k % 2], 16)
                eng.wait_ge(q_made, NCH)
                eng.dma_start(m.query2.rearrange("(b p) f -> p b f", p=P), q2[:, :, :]).then_inc(q_stored, 16)
                eng.wait_ge(q_stored, 16)
                for k in range(2):
                    eng.wait_ge(stored[k], 16 * len(range(k, NCH, 2)))

            @block.tensor
            def _(eng):
                def turn(k):
                    eng.wait_ge(x_made, k + 1)
                    if k >= 2:
                        eng.wait_ge(x_k, k - 1)
                    for n, b in enumerate(range(*blocks(k))):
                        t = eng.transpose(ps[:, k % 2, n * P:(n + 1) * P], m.xN[:, b, :], m.ident[:, :])
                    t.then_inc(x_t, 1)

                def maps(k):
                    eng.wait_ge(x_k, k + 1)
                    if k >= 2:
                        eng.wait_ge(q_made, k - 1)
                        eng.wait_ge(kv_made, 2 * k - 2)
                    for n, b in enumerate(range(*blocks(k))):
                        xb = m.xT[:, b * P:b * P + P]
                        eng.matmul(ps[:, 2 + k % 2, n * P:(n + 1) * P], xb, w("L2_gnn_q_w"), start=True, stop=True)
                        for j, name in enumerate(("L2_gnn_k_w", "L2_gnn_v_w")):
                            at = (2 * (n % 2) + j) * P
                            t = eng.matmul(ps[:, 4 + 2 * (k % 2) + n // 2, at:at + P], xb, w(name), start=True, stop=True)
                    t.then_inc(qkv_sum, 1)

                in_turns((turn, maps))

            @block.scalar
            def _(eng):
                def exponentials(k):
                    b0, b1 = blocks(k)
                    eng.wait_ge(expo, k + 1)
                    eng.activation(fac[:, b0:b1, :], fac[:, b0:b1, :], ACT.Exp).then_inc(exped, 1)

                def root(n, k):
                    b0, b1 = blocks(k)
                    eng.wait_ge(varn[n], k + 1)
                    eng.activation(sd_n[:, b0:b1], mv_n[:, b0:b1, 1], ACT.Sqrt, bias=m.eps[:, 0:1]).then_inc(rootn[n], 1)

                def turned(k):
                    at, n = CHUNKS[k]
                    eng.wait_ge(x_t, k + 1)
                    eng.activation(m.xT[:, at:at + n], ps[:, k % 2, 0:n], ACT.Copy).then_inc(x_k, 1)

                def keys_values(k):
                    eng.wait_ge(qkv_sum, k + 1)
                    if k >= 2:
                        eng.wait_ge(stored[k % 2], 16 * (k // 2))
                    for h in range(2):
                        n = min(max(blocks(k)[1] - blocks(k)[0] - 2 * h, 0), 2)
                        if n:
                            eng.activation(kv[k % 2][:, 2 * h:2 * h + n, :].rearrange("p b f -> p (b f)"),
                                           ps[:, 4 + 2 * (k % 2) + h, 0:n * 2 * D], ACT.Copy).then_inc(kv_made, 1)
                        else:
                            eng.nop().then_inc(kv_made, 1)

                in_turns((exponentials, lambda k: root(0, k), lambda k: root(1, k), turned, keys_values))

            @block.vector
            def _(eng):
                v = Steps(eng, vec)
                scale = float(D2) ** -0.5
                v.put(eng.tensor_tensor(kept_in, m.xN[:, :, :], spread(r("L1_gnn_bias"), 1, [P, NB, D]), ALU.add))
                v.put(eng.tensor_tensor(shifted, m.xN[:, :, :], spread(r("L1_gnn_ln_beta"), 1, [P, NB, D]), ALU.add))
                v.put(eng.tensor_scalar(q_bias, r("L2_gnn_q_b"), scale, None, ALU.mult))

                def exponents(k):
                    b0, b1 = blocks(k)
                    eng.wait_ge(state_in[k], 16 * (b1 - b0))
                    eng.tensor_scalar(fac[:, b0:b1, :], st[:, b0:b1, MAX:R1], 0.0, None, ALU.min).then_inc(expo, 1)

                def moments(n, k):
                    for b in range(*blocks(k)):
                        v.put(eng.bn_stats(st_n[:, b, :], y[:, b, :]))
                    v.wait()
                    for b in range(*blocks(k)):
                        v.put(eng.bn_aggr(mv_n[:, b, :], st_n[:, b, :]))
                    v.wait()
                    eng.engine_nop().then_inc(varn[n], 1)

                def relations(k):
                    b0, b1 = blocks(k)
                    f, d, yk = fac[:, b0:b1, :], den[:, b0:b1, :], y[:, b0:b1, :]
                    eng.wait_ge(exped, k + 1)
                    v.then(eng.tensor_tensor(d, st[:, b0:b1, SUM:MAX], f, ALU.mult))
                    v.then(eng.tensor_scalar(d, d, 1e-8, None, ALU.add))
                    v.then(eng.reciprocal(d, d))
                    v.then(eng.tensor_tensor(f, f, d, ALU.mult))
                    acc = st[:, b0:b1, 0:SUM].rearrange("p b (a d) -> p b a d", d=D1)
                    v.then(eng.tensor_tensor(acc, acc, spread(f, 3, [P, b1 - b0, RH, D1]), ALU.mult))
                    v.then(eng.tensor_tensor(yk, st[:, b0:b1, 0:D], kept_in[:, b0:b1, :], ALU.add))
                    for j in range(1, REL):
                        v.then(eng.tensor_tensor(yk, yk, st[:, b0:b1, j * D:(j + 1) * D], ALU.add))
                    moments(0, k)

                def norm(k):
                    b0, b1 = blocks(k)
                    eng.wait_ge(rootn[0], k + 1)
                    for b in range(b0, b1):
                        v.put(eng.scalar_tensor_tensor(out=y[:, b, :], in0=y[:, b, :], scalar=mv_n[:, b, 0:1], in1=r("L1_gnn_ln_gamma"),
                                                       op0=ALU.subtract, op1=ALU.mult))
                    v.then(eng.reciprocal(sd_n[:, b0:b1], sd_n[:, b0:b1]))
                    for b in range(b0, b1):
                        v.put(eng.scalar_tensor_tensor(out=y[:, b, :], in0=y[:, b, :], scalar=sd_n[:, b:b + 1], in1=shifted[:, b, :],
                                                       op0=ALU.mult, op1=ALU.add))
                    v.wait()
                    moments(1, k)

                def norm_behind(k):
                    b0, b1 = blocks(k)
                    eng.wait_ge(rootn[1], k + 1)
                    v.then(eng.reciprocal(sd_n[:, b0:b1], sd_n[:, b0:b1]))
                    for b in range(b0, b1):
                        v.put(eng.tensor_scalar(m.xN[:, b, :], y[:, b, :], mv_n[:, b, 0:1], sd_n[:, b:b + 1], ALU.subtract, ALU.mult))
                    v.wait()
                    eng.engine_nop().then_inc(x_made, 1)

                def queries(k):
                    b0, b1 = blocks(k)
                    eng.wait_ge(qkv_sum, k + 1)
                    eng.scalar_tensor_tensor(out=q2[:, b0:b1, :], in0=ps[:, 2 + k % 2, 0:CHUNKS[k][1]].rearrange("p (b f) -> p b f", f=D), scalar=scale,
                                             in1=spread(q_bias, 1, [P, b1 - b0, D]), op0=ALU.mult, op1=ALU.add).then_inc(q_made, 1)

                in_turns((exponents, relations, norm, norm_behind, queries))


SCORES2 = 2 + 4
OLD2 = 3
SUMS2 = OLD2 + HALF


def layer2_edges(nc, m, I):
    with phase(nc, "layer2_edges") as sem:
        A = Arena(m)
        kv = [A(HALF, 2 * D) for _ in range(RING)]
        q = [A(HALF, D) for _ in range(RING)]
        rows = [A(HALF, R2) for _ in range(2)]
        prod = A(HALF, D)
        e, fwd = A(H2, COLS), A(H2, COLS)
        top = [A(H2, COLS) for _ in range(2)]
        gap = [A(H2, COLS) for _ in range(2)]
        ex = [A(H2, COLS) for _ in range(2)]
        old = A(D + H2)
        carry_keeps = [A(HALF) for _ in range(2)]
        keeps = [A(HALF) for _ in range(2)]
        resets = [A(H2 * COLS + 1) for _ in range(2)]
        idx = [A(HALF, dt=I32) for _ in range(RING)]
        SUM, MAX = D, D + H2

        q_first, q_in = sem("first_queries_landed"), [sem(f"queries_landed{k}") for k in range(RING)]
        begun = sem("buffers_begun")
        carried = sem("queries_carried")
        scored, summed = sem("score_steps"), sem("sum_steps")
        exped, filled = sem("exponentials"), sem("state_columns_filled")
        marks, kept = sem("resets_staged"), sem("keeps_staged")
        staged = [sem(f"indices_staged{k}") for k in range(RING)]
        landed = [sem(f"keys_values_landed{k}") for k in range(RING)]
        free = [sem(f"keys_values_used{k}") for k in range(RING)]
        stored, rows_free = sem("states_stored"), sem("states_free")

        def carried_before(i, k):
            return i * (RING * HALF) + k * HALF + 1

        def scores_before(i, k):
            return i * (RING * SCORES2) + k * SCORES2 + 1

        def sums_before(i, k):
            return i * (RING * SUMS2) + (k + 1) * SUMS2

        def edges(i, k):
            return bass.ds(i * (RING * HALF) + k * HALF, HALF)

        with nc.Block() as block:

            @block.sync
            def _(eng):
                def load(i, k):
                    eng.dma_start(q[k % RING], lanes(m.seg_rows)[:, edges(i, k), :]).then_inc(q_in[k % RING], 16)

                def turn(i, last):
                    for k in range(RING):
                        hold(eng, carried, carried_before(i, k) + 1)
                        if k == 0 or not last:
                            load(i, k + RING - 1)
                        hold(eng, summed, sums_before(i, k) + SUMS2)
                        eng.dma_start(lanes(m.rows2)[:, edges(i, k), :], rows[k % 2]).then_inc(stored, 16)
                        hold(eng, stored, 16 * RING * i + 16 * k + 16)
                        eng.nop().then_inc(rows_free, 1)

                for k in range(RING - 1):
                    load(0, k)
                with eng.Fori(0, LOOPS - 1) as i:
                    turn(i, False)
                turn(LOOPS - 1, True)

            @block.gpsimd
            def _(eng):
                eng.indirect_dma_start(out=q[RING - 1][:, HALF - 1, :], out_offset=None, in_=m.query2,
                                       in_offset=bass.IndirectOffsetOnAxis(ap=m.lane_first[:, 0:1], axis=0)).then_inc(q_first, 16)
                with eng.Fori(0, LOOPS) as i:
                    for k in range(RING):
                        hold(eng, staged[k], i + 1)
                        hold(eng, free[k], i + 1)
                        for j in range(HALF):
                            eng.indirect_dma_start(out=kv[k][:, j, :], out_offset=None, in_=m.table2,
                                                   in_offset=bass.IndirectOffsetOnAxis(ap=idx[k][:, j:j + 1], axis=0)).then_inc(landed[k], 16)

            @block.scalar
            def _(eng):
                def stage_marks(k, at):
                    eng.activation(resets[k % 2][:, 0:H2 * COLS].rearrange("p (a t) -> p a t", t=COLS)[:, :, 1:COLS],
                                   spread(m.reset[:, at], 1, [P, H2, HALF]), ACT.Copy).then_inc(marks, 1)
                    eng.activation(carry_keeps[k % 2], m.keep[:, at], ACT.Copy).then_inc(marks, 1)

                for k in range(RING):
                    eng.activation(idx[k], m.src[:, k * HALF:(k + 1) * HALF], ACT.Copy).then_inc(staged[k], 1)
                eng.wait_ge(begun, 5)
                for k in range(2):
                    stage_marks(k, edges(0, k))
                with eng.Fori(0, LOOPS) as i:
                    for k in range(RING):
                        h = k % 2
                        hold(eng, landed[k], 16 * HALF * (i + 1))
                        eng.activation(idx[k], m.src[:, edges(i, RING + k)], ACT.Copy).then_inc(staged[k], 1)
                        hold(eng, scored, scores_before(i, k) + SCORES2)
                        eng.activation(ex[h], gap[h], ACT.Exp, scale=-1.0).then_inc(exped, 1)
                        stage_marks(k, edges(i, k + 2))
                        hold(eng, summed, sums_before(i, k) - SUMS2 + OLD2)
                        eng.activation(keeps[h], m.keep[:, edges(i, k)], ACT.Copy).then_inc(kept, 1)
                        eng.wait_ge(rows_free, i * RING + k + 1)
                        eng.wait_ge(exped, i * RING + k + 1)
                        eng.activation(rows[h][:, :, SUM:MAX], ex[h][:, :, 1:COLS].rearrange("p a t -> p t a"), ACT.Copy).then_inc(filled, 1)
                        eng.activation(rows[h][:, :, MAX:R2], top[h][:, :, 1:COLS].rearrange("p a t -> p t a"), ACT.Copy).then_inc(filled, 1)

            @block.vector
            def _(eng):
                f = Steps(eng, begun)
                for h in range(2):
                    f.put(eng.memset(resets[h], -BIG))
                f.put(eng.memset(fwd, -BIG))
                f.put(eng.memset(rows[1][:, HALF - 1, 0:MAX], 0.0))
                f.put(eng.memset(rows[1][:, HALF - 1, MAX:R2], -BIG))
                f.wait()
                for k in range(RING):
                    eng.engine_nop().then_inc(free[k], 1)
                eng.engine_nop().then_inc(rows_free, 2)
                eng.engine_nop().then_inc(carried, 1)
                eng.engine_nop().then_inc(scored, 1)
                eng.engine_nop().then_inc(summed, SUMS2)
                eng.wait_ge(q_first, 16)

                def half(i, k):
                    return (i + k // RING, k % RING)

                def carry(i, k, j):
                    if j == 0:
                        eng.wait_ge(q_in[k], 16 * i + 16)
                        eng.wait_ge(marks, 2 * RING * i + 2 * k + 2)
                    eng.wait_ge(carried, carried_before(i, k) + j)
                    eng.scalar_tensor_tensor(out=q[k][:, j, :], in0=q[k][:, j - 1, :] if j else q[k - 1][:, HALF - 1, :],
                                             scalar=carry_keeps[k % 2][:, j:j + 1], in1=q[k][:, j, :], op0=ALU.mult, op1=ALU.add).then_inc(carried, 1)

                def score(i, k, step):
                    eng.wait_ge(scored, scores_before(i, k) + step)
                    if step == 0:
                        eng.wait_ge(landed[k], 16 * HALF * (i + 1))
                        eng.wait_ge(carried, carried_before(i, k) + HALF)
                        ins = eng.tensor_tensor(prod, q[k], kv[k][:, :, 0:D], ALU.mult)
                    elif step == 1:
                        ins = eng.tensor_reduce(e[:, :, 1:COLS].rearrange("p a t -> p t a"), prod.rearrange("p t (a d) -> p t a d", d=D2), AX.X, ALU.add)
                    else:
                        ins = maxima_step(eng, step - 2, resets[k % 2], e, fwd, top[k % 2], gap[k % 2])
                    ins.then_inc(scored, 1)

                def add_up(i, k, scores=True, carries=True):
                    v = LoopSteps(eng, summed, sums_before(i, k))
                    h = k % 2
                    row, before = rows[h], rows[1 - h][:, HALF - 1, :]
                    eng.wait_ge(exped, i * RING + k + 1)
                    eng.wait_ge(rows_free, i * RING + k + 1)
                    v.put(eng.tensor_tensor(row[:, :, 0:D].rearrange("p t (a d) -> p t a d", d=D2),
                                            kv[k][:, :, D:2 * D].rearrange("p t (a d) -> p t a d", d=D2),
                                            spread(ex[h][:, :, 1:COLS].rearrange("p a t -> p t a"), 3, [P, HALF, H2, D2]), ALU.mult))
                    v.put(eng.tensor_tensor(old[:, 0:SUM].rearrange("p (a d) -> p a d", d=D2), before[:, 0:SUM].rearrange("p (a d) -> p a d", d=D2),
                                            ex[h][:, :, 0:1].broadcast_to([P, H2, D2]), ALU.mult))
                    v.then(eng.tensor_tensor(old[:, SUM:MAX], before[:, SUM:MAX], ex[h][:, :, 0], ALU.mult))
                    eng.nop(nofuse=True).then_inc(free[k], 1)
                    eng.wait_ge(kept, i * RING + k + 1)
                    eng.wait_ge(filled, 2 * RING * i + 2 * k + 2)
                    for j in range(HALF):
                        v.wait()
                        v.put(eng.scalar_tensor_tensor(out=row[:, j, 0:MAX], in0=row[:, j - 1, 0:MAX] if j else old, scalar=keeps[h][:, j:j + 1],
                                                       in1=row[:, j, 0:MAX], op0=ALU.mult, op1=ALU.add))
                        if carries:
                            carry(*half(i, k + 2), j)
                        if scores and 2 <= j < 2 + SCORES2:
                            score(*half(i, k + 1), j - 2)
                    v.wait()
                    assert v.n == SUMS2

                for k in range(2):
                    for j in range(HALF):
                        carry(0, k, j)
                for step in range(SCORES2):
                    score(0, 0, step)
                with eng.Fori(0, LOOPS - 1) as i:
                    for k in range(RING):
                        add_up(i, k)
                for k in range(RING):
                    add_up(LOOPS - 1, k, scores=k + 1 < RING, carries=k + 2 < RING)
                f.then(eng.tensor_copy(m.lane_end[:, 0:R2], rows[1][:, HALF - 1, :]))


def layer2_nodes(nc, m, I):
    with phase(nc, "layer2_nodes") as sem:
        A = Arena(m)
        st = A(NB, R2)
        big = A(4 * NP)
        q, y = (big[:, j * NP:(j + 1) * NP].rearrange("p (b f) -> p b f", f=D) for j in range(2))
        aT, sT = (big[:, j * NP:(j + 1) * NP] for j in range(2, 4))
        kvn = A(NB, 2 * D)
        hid = [kvn[:, 8 * k:8 * k + 8, :].rearrange("p b f -> p (b f)").rearrange("p (j n) -> p j n", j=FF) for k in range(2)]
        out = kvn[:, 16:20, :].rearrange("p b f -> p (b f)").rearrange("p (a b f) -> p a b f", a=2, f=D)
        own = A(NB, H2)
        top = A(NB, H2)
        ex = A(2, NB * H2)
        den = A(NB, H2)
        st_b = A(len(REALCH), 6)
        mv_b = A(2)
        sd_b, scale, shift = A(1), A(1), A(1)
        st_n = A(NB, 6)
        mv_n = A(NB, 2)
        sd_n = A(NB)
        ps = m.psum
        SUM, MAX = D, D + H2
        aN = st[:, :, 0:D]
        bT = aT

        def c(name):
            k = COLUMNS.index(name)
            return m.cols[:, k:k + 1]

        NCH = len(CHUNKS)
        state_in = [sem(f"states_landed{k}") for k in range(NCH)]
        own_in = [sem(f"own_rows_landed{k}") for k in range(NCH)]
        vec = sem("vector_steps")
        expo, exped = sem("exponents"), sem("exponentials")
        a_made, a_t, a_k = sem("values_made"), sem("values_turned"), sem("values_kept")
        o_sum, s_made = sem("output_summed"), sem("sum_made")
        var1, root1, scale1, b_made = sem("variance1"), sem("root1"), sem("scale1"), sem("normed1")
        l1_sum, hid_made, leaky, l2_sum, s2_made = sem("hidden_summed"), sem("hidden_made"), sem("hidden_leaky"), sem("second_summed"), sem("sum2_made")
        var2, root2, scale2, b2_made = sem("variance2"), sem("root2"), sem("scale2"), sem("normed2")
        n_t, y_made = sem("normed_turned"), sem("y_made")
        varn, rootn, x_made = sem("node_variance"), sem("node_root"), sem("x_made")
        x_t, x_k = sem("x_turned"), sem("x_kept")
        t_sum, t_made = sem("table_summed"), sem("table_made")
        stored = [sem(f"table_stored{k}") for k in range(2)]

        with nc.Block() as block:

            @block.gpsimd
            def _(eng):
                for k in range(NCH):
                    for b in range(*blocks(k)):
                        eng.indirect_dma_start(out=st[:, b, :], out_offset=None, in_=m.rows2,
                                               in_offset=bass.IndirectOffsetOnAxis(ap=m.end[:, b:b + 1], axis=0)).then_inc(state_in[k], 16)

            @block.sync
            def _(eng):
                for k in range(NCH):
                    b0, b1 = blocks(k)
                    eng.dma_start(q[:, b0:b1, :], m.query2.rearrange("(b p) f -> p b f", p=P)[:, b0:b1, :]).then_inc(own_in[k], 16)
                    eng.dma_start(kvn[:, b0:b1, :], m.table2.rearrange("(b p) f -> p b f", p=P)[:, b0:b1, :]).then_inc(own_in[k], 16)
                for k, (at, n) in enumerate(CHUNKS):
                    eng.wait_ge(t_made, k + 1)
                    eng.dma_start(m.table3.rearrange("(b p) f -> p b f", p=P)[:, at // P:(at + n) // P, :], out2(out, k, n)).then_inc(stored[k % 2], 16)
                for k in range(2):
                    eng.wait_ge(stored[k], 16 * len(range(k, NCH, 2)))

            @block.tensor
            def _(eng):
                def values(k):
                    eng.wait_ge(a_made, k + 1)
                    if k >= 2:
                        eng.wait_ge(a_k, k - 1)
                    for n, b in enumerate(range(*blocks(k))):
                        t = eng.transpose(ps[:, k % 2, n * P:(n + 1) * P], aN[:, b, :], m.ident[:, :])
                    t.then_inc(a_t, 1)

                def output_map(k):
                    at, n = CHUNKS[k]
                    eng.wait_ge(a_k, k + 1)
                    if k >= 2:
                        eng.wait_ge(s_made, k - 1)
                    eng.matmul(ps[:, 2 + k % 2, 0:n], m.wt[:, TRANSPOSED.index("L2_gnn_out_w"), :], aT[:, at:at + n], start=True, stop=True).then_inc(o_sum, 1)

                in_turns((values, output_map))
                eng.wait_ge(a_k, NCH)
                eng.wait_ge(s_made, NCH)
                for nk in range(NCH + 1):
                    if nk < NCH:
                        at, n = CHUNKS[nk]
                        eng.wait_ge(b_made, nk + 1)
                        for j in range(FF):
                            if nk:
                                eng.wait_ge(hid_made, FF * (nk - 1) + j + 1)
                            eng.matmul(ps[:, j, 0:n], m.wt[:, LIN1 + j, :], bT[:, at:at + n], start=True, stop=True).then_inc(l1_sum, 1)
                    if nk == 0:
                        continue
                    k = nk - 1
                    at, n = CHUNKS[k]
                    eng.wait_ge(leaky, k + 1)
                    if k >= 2:
                        eng.wait_ge(s2_made, k - 1)
                    for j in range(FF):
                        t = eng.matmul(ps[:, 4 + k % 2, 0:n], m.wt[:, LIN2 + j, :], hid[k % 2][:, j, 0:n], start=(j == 0), stop=(j == FF - 1))
                    t.then_inc(l2_sum, 1)
                def back(k):
                    eng.wait_ge(b2_made, k + 1)
                    if k >= 2:
                        eng.wait_ge(y_made, k - 1)
                    for n, b in enumerate(range(*blocks(k))):
                        t = eng.transpose(ps[:, 6 + k % 2, n * P:(n + 1) * P], sT[:, b * P:(b + 1) * P], m.ident[:, :])
                    t.then_inc(n_t, 1)

                def turn(k):
                    eng.wait_ge(x_made, k + 1)
                    if k >= 2:
                        eng.wait_ge(x_k, k - 1)
                    for n, b in enumerate(range(*blocks(k))):
                        t = eng.transpose(ps[:, k % 2, n * P:(n + 1) * P], m.xN[:, b, :], m.ident[:, :])
                    t.then_inc(x_t, 1)

                def table(k):
                    eng.wait_ge(x_k, k + 1)
                    if k >= 2:
                        eng.wait_ge(t_made, k - 1)
                    for n, b in enumerate(range(*blocks(k))):
                        t = eng.matmul(ps[:, 2 + k % 2, n * P:(n + 1) * P], m.xT[:, b * P:(b + 1) * P], m.w3[:, 1, :], start=True, stop=True)
                    t.then_inc(t_sum, 1)

                eng.wait_ge(hid_made, FF * NCH)
                in_turns((back, None, None, turn, table))

            @block.scalar
            def _(eng):
                def exponentials(k):
                    b0, b1 = blocks(k)
                    eng.wait_ge(expo, k + 1)
                    eng.activation(ex[:, :, b0 * H2:b1 * H2], ex[:, :, b0 * H2:b1 * H2], ACT.Exp).then_inc(exped, 1)

                def values(k):
                    at, n = CHUNKS[k]
                    eng.wait_ge(a_t, k + 1)
                    eng.activation(aT[:, at:at + n], ps[:, k % 2, 0:n], ACT.Copy).then_inc(a_k, 1)

                in_turns((exponentials, None, values))
                eng.wait_ge(var1, 1)
                eng.activation(sd_b, mv_b[:, 1:2], ACT.Sqrt, bias=m.eps[:, 0:1]).then_inc(root1, 1)
                eng.wait_ge(scale1, 1)
                for k, (at, n) in enumerate(CHUNKS):
                    eng.activation(bT[:, at:at + n], sT[:, at:at + n], ACT.Identity, bias=shift, scale=scale).then_inc(b_made, 1)
                for k, (at, n) in enumerate(CHUNKS):
                    if k >= 2:
                        eng.wait_ge(l2_sum, k - 1)
                    for j in range(FF):
                        eng.wait_ge(l1_sum, FF * k + j + 1)
                        eng.activation(hid[k % 2][:, j, 0:n], ps[:, j, 0:n], ACT.Identity, bias=m.lin1_b[:, j:j + 1]).then_inc(hid_made, 1)
                eng.wait_ge(var2, 1)
                eng.activation(sd_b, mv_b[:, 1:2], ACT.Sqrt, bias=m.eps[:, 0:1]).then_inc(root2, 1)
                eng.wait_ge(scale2, 1)
                for k, (at, n) in enumerate(CHUNKS):
                    eng.activation(sT[:, at:at + n], sT[:, at:at + n], ACT.Identity, bias=shift, scale=scale).then_inc(b2_made, 1)

                def root(k):
                    b0, b1 = blocks(k)
                    eng.wait_ge(varn, k + 1)
                    eng.activation(sd_n[:, b0:b1], mv_n[:, b0:b1, 1], ACT.Sqrt, bias=m.eps[:, 0:1]).then_inc(rootn, 1)

                def turned(k):
                    at, n = CHUNKS[k]
                    eng.wait_ge(x_t, k + 1)
                    eng.activation(m.xT[:, at:at + n], ps[:, k % 2, 0:n], ACT.Copy).then_inc(x_k, 1)

                def table(k):
                    n = CHUNKS[k][1]
                    eng.wait_ge(t_sum, k + 1)
                    if k >= 2:
                        eng.wait_ge(stored[k % 2], 16 * (k // 2))
                    eng.activation(out2(out, k, n), ps[:, 2 + k % 2, 0:n].rearrange("p (b f) -> p b f", f=D), ACT.Copy).then_inc(t_made, 1)

                in_turns((root, None, turned, table))

            @block.vector
            def _(eng):
                v = Steps(eng, vec)
                ex4 = ex.rearrange("p k (b a) -> p k b a", a=H2)

                def own_scores(k):
                    b0, b1 = blocks(k)
                    qk = q[:, b0:b1, :]
                    eng.wait_ge(own_in[k], 32)
                    v.then(eng.tensor_tensor(qk, qk, kvn[:, b0:b1, 0:D], ALU.mult))
                    v.then(eng.tensor_reduce(own[:, b0:b1, :], qk.rearrange("p b (a d) -> p b a d", d=D2), AX.X, ALU.add))

                def exponents(k):
                    b0, b1 = blocks(k)
                    eng.wait_ge(state_in[k], 16 * (b1 - b0))
                    t = top[:, b0:b1, :]
                    v.then(eng.tensor_tensor(t, own[:, b0:b1, :], st[:, b0:b1, MAX:R2], ALU.max))
                    v.put(eng.tensor_tensor(ex4[:, 0, b0:b1, :], st[:, b0:b1, MAX:R2], t, ALU.subtract))
                    v.then(eng.tensor_tensor(ex4[:, 1, b0:b1, :], own[:, b0:b1, :], t, ALU.subtract))
                    eng.engine_nop().then_inc(expo, 1)

                def values(k):
                    b0, b1 = blocks(k)
                    d, a, own_values = den[:, b0:b1, :], aN[:, b0:b1, :], kvn[:, b0:b1, D:2 * D]
                    eng.wait_ge(exped, k + 1)
                    v.then(eng.tensor_tensor(d, st[:, b0:b1, SUM:MAX], ex4[:, 0, b0:b1, :], ALU.mult))
                    v.then(eng.tensor_tensor(d, d, ex4[:, 1, b0:b1, :], ALU.add))
                    v.then(eng.tensor_scalar(d, d, 1e-16, None, ALU.add))
                    v.then(eng.reciprocal(d, d))
                    for j in range(2):
                        v.put(eng.tensor_tensor(ex4[:, j, b0:b1, :], ex4[:, j, b0:b1, :], d, ALU.mult))
                    v.wait()
                    for j, x in ((0, a), (1, own_values)):
                        x4 = x.rearrange("p b (a d) -> p b a d", d=D2)
                        v.put(eng.tensor_tensor(x4, x4, spread(ex4[:, j, b0:b1, :], 3, [P, b1 - b0, H2, D2]), ALU.mult))
                    v.wait()
                    eng.tensor_tensor(a, a, own_values, ALU.add).then_inc(a_made, 1)

                def sums(k):
                    at, n = CHUNKS[k]
                    eng.wait_ge(o_sum, k + 1)
                    eng.scalar_tensor_tensor(out=sT[:, at:at + n], in0=ps[:, 2 + k % 2, 0:n], scalar=c("L2_gnn_out_b"), in1=m.xT[:, at:at + n],
                                             op0=ALU.add, op1=ALU.add).then_inc(s_made, 1)
                    moments(s_made, k)

                def moments(made, k):
                    at, n = REALCH[k]
                    eng.wait_ge(made, k + 1)
                    v.put(eng.bn_stats(st_b[:, k, :], sT[:, at:at + n]))

                in_turns((own_scores, exponents, values, None, sums))

                def norm(var, root, scaled, gamma, beta):
                    v.wait()
                    eng.bn_aggr(mv_b, st_b).then_inc(var, 1)
                    eng.wait_ge(root, 1)
                    v.then(eng.reciprocal(sd_b, sd_b))
                    v.then(eng.tensor_tensor(scale, sd_b, c(gamma), ALU.mult))
                    v.then(eng.tensor_tensor(sd_b, mv_b[:, 0:1], scale, ALU.mult))
                    eng.tensor_tensor(shift, c(beta), sd_b, ALU.subtract).then_inc(scaled, 1)
                    eng.wait_ge(scaled, 1)

                norm(var1, root1, scale1, "L2_gnn_g1", "L2_gnn_b1")
                for k in range(NCH + 1):
                    if k < NCH:
                        hk = hid[k % 2][:, :, 0:CHUNKS[k][1]]
                        eng.wait_ge(hid_made, FF * (k + 1))
                        eng.scalar_tensor_tensor(out=hk, in0=hk, scalar=0.01, in1=hk, op0=ALU.mult, op1=ALU.max).then_inc(leaky, 1)
                    if k == 0:
                        continue
                    at, n = CHUNKS[k - 1]
                    eng.wait_ge(l2_sum, k)
                    eng.scalar_tensor_tensor(out=sT[:, at:at + n], in0=ps[:, 4 + (k - 1) % 2, 0:n], scalar=c("L2_gnn_lin2_b"), in1=bT[:, at:at + n],
                                             op0=ALU.add, op1=ALU.add).then_inc(s2_made, 1)
                    moments(s2_made, k - 1)
                norm(var2, root2, scale2, "L2_gnn_g2", "L2_gnn_b2")

                def outputs(k):
                    b0, b1 = blocks(k)
                    eng.wait_ge(n_t, k + 1)
                    eng.tensor_tensor(y[:, b0:b1, :], ps[:, 6 + k % 2, 0:CHUNKS[k][1]].rearrange("p (b f) -> p b f", f=D), m.xN[:, b0:b1, :], ALU.add).then_inc(y_made, 1)
                    eng.wait_ge(y_made, k + 1)
                    for b in range(b0, b1):
                        v.put(eng.bn_stats(st_n[:, b, :], y[:, b, :]))
                    v.wait()
                    for b in range(b0, b1):
                        v.put(eng.bn_aggr(mv_n[:, b, :], st_n[:, b, :]))
                    v.wait()
                    eng.engine_nop().then_inc(varn, 1)

                def norm_behind(k):
                    b0, b1 = blocks(k)
                    eng.wait_ge(rootn, k + 1)
                    v.then(eng.reciprocal(sd_n[:, b0:b1], sd_n[:, b0:b1]))
                    for b in range(b0, b1):
                        v.put(eng.tensor_scalar(m.xN[:, b, :], y[:, b, :], mv_n[:, b, 0:1], sd_n[:, b:b + 1], ALU.subtract, ALU.mult))
                    v.wait()
                    eng.engine_nop().then_inc(x_made, 1)

                in_turns((outputs, None, norm_behind))


def out2(out, k, n):
    return out[:, k % 2, 0:n // P, :]


PER_TURN3 = 2 * 2 * HALF + 3


def layer3_edges(nc, m, I):
    with phase(nc, "layer3_edges") as sem:
        A = Arena(m)
        feat = [A(HALF, D) for _ in range(2)]
        rows = [A(HALF, D) for _ in range(2)]
        resets, vals = A(BODY), A(BODY)
        idx = [A(HALF, dt=I32) for _ in range(2)]
        begun = sem("states_begun")
        steps = sem("edge_steps")
        staged = [sem(f"indices_staged{h}") for h in range(2)]
        landed = [sem(f"rows_landed{h}") for h in range(2)]
        free = [sem(f"rows_used{h}") for h in range(2)]
        stored = [sem(f"states_stored{h}") for h in range(2)]
        rows_free = [sem(f"states_free{h}") for h in range(2)]

        with nc.Block() as block:

            @block.sync
            def _(eng):
                with eng.Fori(0, TURNS) as i:
                    for h in range(2):
                        hold(eng, steps, i * PER_TURN3 + 3 + (h + 1) * 2 * HALF)
                        eng.dma_start(lanes(m.rows3)[:, bass.ds(i * BODY + h * HALF, HALF), :], rows[h]).then_inc(stored[h], 16)
                        hold(eng, stored[h], 16 * i + 16)
                        eng.nop().then_inc(rows_free[h], 1)

            @block.gpsimd
            def _(eng):
                with eng.Fori(0, TURNS) as i:
                    for h in range(2):
                        hold(eng, staged[h], i + 1)
                        hold(eng, free[h], i + 1)
                        for j in range(HALF):
                            eng.indirect_dma_start(out=feat[h][:, j, :], out_offset=None, in_=m.table3,
                                                   in_offset=bass.IndirectOffsetOnAxis(ap=idx[h][:, j:j + 1], axis=0)).then_inc(landed[h], 16)

            @block.scalar
            def _(eng):
                for h in range(2):
                    eng.activation(idx[h], m.src[:, h * HALF:(h + 1) * HALF], ACT.Copy).then_inc(staged[h], 1)
                with eng.Fori(0, TURNS) as i:
                    for h in range(2):
                        hold(eng, landed[h], 16 * HALF * (i + 1))
                        eng.activation(idx[h], m.src[:, bass.ds(i * BODY + BODY + h * HALF, HALF)], ACT.Copy).then_inc(staged[h], 1)

            @block.vector
            def _(eng):
                for h in range(2):
                    eng.engine_nop().then_inc(free[h], 1)
                    eng.engine_nop().then_inc(rows_free[h], 1)
                f = Steps(eng, begun)
                f.then(eng.memset(rows[1][:, HALF - 1, :], -BIG))
                eng.engine_nop().then_inc(steps, 1)
                with eng.Fori(0, TURNS) as i:
                    v = LoopSteps(eng, steps, i * PER_TURN3 + 1)
                    v.wait()
                    eng.nop(nofuse=True)
                    v.put(eng.tensor_copy(resets, m.reset[:, bass.ds(i * BODY, BODY)]))
                    v.put(eng.tensor_copy(vals, m.val[:, bass.ds(i * BODY, BODY)]))
                    v.wait()
                    for h in range(2):
                        eng.wait_ge(landed[h], 16 * HALF * (i + 1))
                        for j in range(HALF):
                            s = h * HALF + j
                            v.put(eng.scalar_tensor_tensor(out=feat[h][:, j, :], in0=m.edge_w[:, :], scalar=vals[:, s:s + 1],
                                                           in1=feat[h][:, j, :], op0=ALU.mult, op1=ALU.add))
                        v.wait()
                        eng.wait_ge(rows_free[h], i + 1)
                        for j in range(HALF):
                            s = h * HALF + j
                            v.then(eng.scalar_tensor_tensor(out=rows[h][:, j, :], in0=rows[h][:, j - 1, :] if j else rows[1 - h][:, HALF - 1, :],
                                                            scalar=resets[:, s:s + 1], in1=feat[h][:, j, :], op0=ALU.add, op1=ALU.max))
                        assert v.n == 2 + (h + 1) * 2 * HALF
                        eng.nop(nofuse=True).then_inc(free[h], 1)
                    v.put(eng.engine_nop())
                eng.wait_ge(steps, TURNS * PER_TURN3 + 1)
                f.then(eng.tensor_copy(m.lane_end[:, 0:D], rows[1][:, HALF - 1, :]))


def layer3_nodes(nc, m, I, result):
    with phase(nc, "layer3_nodes") as sem:
        A = Arena(m)
        lane_max = A(P + 1)
        row = A(D)
        own = A(NB, D)
        agg = A(NB, D)
        aT, hT = A(NP), A(NP)
        y = A(NB, D)
        st_n = A(NB, 6)
        mv_n = A(NB, 2)
        sd_n = A(NB)
        ps = m.psum

        def r(name):
            return m.rows[:, ROWS.index(name), :]

        NCH = len(CHUNKS)
        row_in, fixed = sem("first_rows_landed"), sem("first_rows_fixed")
        agg_in = [sem(f"maxima_landed{k}") for k in range(NCH)]
        vec = sem("vector_steps")
        l_t, l_made, l_back, merged = sem("lanes_turned"), sem("lane_maxima"), sem("lane_maxima_turned"), sem("rows_merged")
        d_sum, d_made, a_made, a_t, a_k = sem("target_part_summed"), sem("target_part_made"), sem("agg_made"), sem("agg_turned"), sem("agg_kept")
        h_sum, h_made, y_sum, y_made = sem("hidden_summed"), sem("hidden_made"), sem("y_summed"), sem("y_made")
        varn, rootn, x_made, out_done = sem("node_variance"), sem("node_root"), sem("x_made"), sem("result_stored")

        with nc.Block() as block:

            @block.gpsimd
            def _(eng):
                eng.indirect_dma_start(out=row, out_offset=None, in_=m.rows3,
                                       in_offset=bass.IndirectOffsetOnAxis(ap=m.first_end[:, 0:1], axis=0)).then_inc(row_in, 16)
                eng.wait_ge(merged, 1)
                eng.indirect_dma_start(out=m.rows3, out_offset=bass.IndirectOffsetOnAxis(ap=m.first_fix[:, 0:1], axis=0),
                                       in_=row, in_offset=None).then_inc(fixed, 16)
                eng.wait_ge(fixed, 16)
                for k in range(NCH):
                    for b in range(*blocks(k)):
                        eng.indirect_dma_start(out=agg[:, b, :], out_offset=None, in_=m.rows3,
                                               in_offset=bass.IndirectOffsetOnAxis(ap=m.end[:, b:b + 1], axis=0)).then_inc(agg_in[k], 16)

            @block.sync
            def _(eng):
                for k in range(NCH):
                    b0, b1 = blocks(k)
                    eng.wait_ge(x_made, k + 1)
                    if b1 < NB:
                        eng.dma_start(result[b0 * P:b1 * P, :].rearrange("(b p) f -> p b f", p=P), m.xN[:, b0:b1, :]).then_inc(out_done, 16)
                    else:
                        eng.dma_start(result[b0 * P:N, :], m.xN[0:TAIL, b0, :]).then_inc(out_done, 16)
                eng.wait_ge(out_done, 16 * NCH)

            @block.tensor
            def _(eng):
                def turn(k):
                    eng.wait_ge(a_made, k + 1)
                    if k >= 2:
                        eng.wait_ge(a_k, k - 1)
                    for n, b in enumerate(range(*blocks(k))):
                        t = eng.transpose(ps[:, k % 2, n * P:(n + 1) * P], agg[:, b, :], m.ident[:, :])
                    t.then_inc(a_t, 1)

                def hidden(k):
                    at, n = CHUNKS[k]
                    if k >= 2:
                        eng.wait_ge(h_made, k - 1)
                    eng.matmul(ps[:, 4 + k % 2, 0:n], m.w3[:, 2, :], m.xT[:, at:at + n], start=True, stop=False)
                    eng.wait_ge(a_k, k + 1)
                    eng.matmul(ps[:, 4 + k % 2, 0:n], m.w3[:, 3, :], aT[:, at:at + n], start=False, stop=True).then_inc(h_sum, 1)

                def outputs(k):
                    eng.wait_ge(h_made, k + 1)
                    if k >= 2:
                        eng.wait_ge(y_made, k - 1)
                    for n, b in enumerate(range(*blocks(k))):
                        t = eng.matmul(ps[:, 6 + k % 2, n * P:(n + 1) * P], hT[:, b * P:(b + 1) * P], m.w3[:, 4, :], start=True, stop=True)
                    t.then_inc(y_sum, 1)

                eng.transpose(ps[:, 6, 0:P], m.lane_end[:, 0:D], m.ident[:, :]).then_inc(l_t, 1)
                eng.wait_ge(l_made, 1)
                eng.transpose(ps[:, 7, 0:P], lane_max[:, 0:P], m.ident[:, :]).then_inc(l_back, 1)
                for k in range(NCH):
                    if k >= 2:
                        eng.wait_ge(d_made, k - 1)
                    for n, b in enumerate(range(*blocks(k))):
                        t = eng.matmul(ps[:, 2 + k % 2, n * P:(n + 1) * P], m.xT[:, b * P:(b + 1) * P], m.w3[:, 0, :], start=True, stop=True)
                    t.then_inc(d_sum, 1)
                in_turns((turn, hidden, outputs))

            @block.scalar
            def _(eng):
                b1 = COLUMNS.index("L3_gnn_b1")

                def turned(k):
                    at, n = CHUNKS[k]
                    eng.wait_ge(a_t, k + 1)
                    eng.activation(aT[:, at:at + n], ps[:, k % 2, 0:n], ACT.Copy).then_inc(a_k, 1)

                def relu(k):
                    at, n = CHUNKS[k]
                    eng.wait_ge(h_sum, k + 1)
                    eng.activation(hT[:, at:at + n], ps[:, 4 + k % 2, 0:n], ACT.Relu, bias=m.cols[:, b1:b1 + 1]).then_inc(h_made, 1)

                def root(k):
                    first, last = blocks(k)
                    eng.wait_ge(varn, k + 1)
                    eng.activation(sd_n[:, first:last], mv_n[:, first:last, 1], ACT.Sqrt, bias=m.eps[:, 0:1]).then_inc(rootn, 1)

                in_turns((turned, relu, None, root))

            @block.vector
            def _(eng):
                v = Steps(eng, vec)
                v.put(eng.memset(lane_max[:, 0:1], -BIG))
                eng.wait_ge(l_t, 1)
                v.then(eng.tensor_tensor_scan(lane_max[:, 1:P + 1], m.whole_neg[:, :], ps[:, 6, 0:P], -BIG, ALU.add, ALU.max))
                eng.engine_nop().then_inc(l_made, 1)
                eng.wait_ge(row_in, 16)
                eng.wait_ge(l_back, 1)
                eng.tensor_tensor(row, row, ps[:, 7, 0:P], ALU.max).then_inc(merged, 1)
                for k in range(NCH):
                    b0, b1 = blocks(k)
                    eng.wait_ge(d_sum, k + 1)
                    eng.tensor_tensor(own[:, b0:b1, :], ps[:, 2 + k % 2, 0:CHUNKS[k][1]].rearrange("p (b f) -> p b f", f=D),
                                      spread(r("L3_gnn_bm"), 1, [P, b1 - b0, D]), ALU.add).then_inc(d_made, 1)
                eng.wait_ge(d_made, NCH)
                v.then(eng.tensor_tensor(m.xN[:, :, :], m.xN[:, :, :], spread(r("L3_gnn_b2"), 1, [P, NB, D]), ALU.add))

                def aggregate(k):
                    b0, b1 = blocks(k)
                    a = agg[:, b0:b1, :]
                    eng.wait_ge(agg_in[k], 16 * (b1 - b0))
                    v.then(eng.tensor_tensor(a, a, own[:, b0:b1, :], ALU.add))
                    eng.tensor_tensor(a, a, spread(m.has[:, b0:b1], 2, [P, b1 - b0, D]), ALU.mult).then_inc(a_made, 1)

                def outputs(k):
                    b0, b1 = blocks(k)
                    eng.wait_ge(y_sum, k + 1)
                    eng.tensor_tensor(y[:, b0:b1, :], ps[:, 6 + k % 2, 0:CHUNKS[k][1]].rearrange("p (b f) -> p b f", f=D), m.xN[:, b0:b1, :], ALU.add).then_inc(y_made, 1)
                    eng.wait_ge(y_made, k + 1)
                    for b in range(b0, b1):
                        v.put(eng.bn_stats(st_n[:, b, :], y[:, b, :]))
                    v.wait()
                    for b in range(b0, b1):
                        v.put(eng.bn_aggr(mv_n[:, b, :], st_n[:, b, :]))
                    v.wait()
                    eng.engine_nop().then_inc(varn, 1)

                def norm(k):
                    b0, b1 = blocks(k)
                    eng.wait_ge(rootn, k + 1)
                    v.then(eng.reciprocal(sd_n[:, b0:b1], sd_n[:, b0:b1]))
                    for b in range(b0, b1):
                        v.put(eng.tensor_scalar(m.xN[:, b, :], y[:, b, :], mv_n[:, b, 0:1], sd_n[:, b:b + 1], ALU.subtract, ALU.mult))
                    v.wait()
                    eng.engine_nop().then_inc(x_made, 1)

                in_turns((aggregate, None, None, outputs, norm))


def gnn_resnorm_stack(nc, I, out):
    with ExitStack() as ctx:
        m = allocate(nc, ctx)
        setup_phase(nc, m, I)
        layer0_edges(nc, m, I)
        layer0_nodes(nc, m, I)
        layer1_edges(nc, m, I)
        carry_sums(nc, m, m.rows1, REL, H1)
        layer1_nodes(nc, m, I)
        layer2_edges(nc, m, I)
        carry_sums(nc, m, m.rows2, 1, H2)
        layer2_nodes(nc, m, I)
        layer3_edges(nc, m, I)
        layer3_nodes(nc, m, I, out)


_INS = ['x', 'src', 'dst', 'edge_type_4', 'edge_weight'] + [
    'L0_gnn_' + n for n in ('W1w', 'W1b', 'U1w', 'U1b', 'W2w', 'W2b', 'U2w', 'U2b', 'W3w', 'W3b', 'U3w', 'U3b', 'bn_g',
                            'bn_b', 'm_w0', 'm_b0', 'm_bng', 'm_bnb', 'm_w1', 'm_b1')] + [
    'L1_gnn_' + n for n in ('W', 'attn_src', 'attn_dst', 'bias', 'ln_gamma', 'ln_beta')] + [
    'L2_gnn_' + n for n in ('q_w', 'q_b', 'k_w', 'v_w', 'out_w', 'out_b', 'g1', 'b1', 'lin1_w', 'lin1_b', 'lin2_w',
                            'lin2_b', 'g2', 'b2')] + [
    'L3_gnn_' + n for n in ('Wm', 'bm', 'W1', 'b1', 'W2', 'b2')]
_OUTS = [((3125, 128), 'float32')]


def kernel(**inputs):
    import numpy as _np
    import concourse.bacc as _bacc
    from concourse import mybir as _mybir
    from concourse.bass_utils import run_bass_kernel_spmd as _run

    nc = _bacc.Bacc("TRN2", target_bir_lowering=False, num_devices=1)
    arrays, I, outs = {}, {}, []
    for name in _INS:
        a = _np.ascontiguousarray(inputs[name])
        arrays[f"in_{name}_dram"] = a
        I[name] = nc.dram_tensor(f"in_{name}_dram", a.shape, _mybir.dt.from_np(a.dtype), kind="ExternalInput").ap()
    for i, (shape, dtype) in enumerate(_OUTS):
        dt = _mybir.dt.from_np(_np.dtype(dtype))
        outs.append(nc.dram_tensor(f"out_{i}_dram", shape, dt, kind="ExternalOutput").ap())
    gnn_resnorm_stack(nc, I, outs[0])
    r = _run(nc, [arrays], core_ids=[0])
    got = tuple(r.results[0][f"out_{i}_dram"] for i in range(len(_OUTS)))
    return got[0]
```
